# Optimizing a Trainium2 kernel written in Bass

```python
import numpy as np
import jax
import jax.numpy as jnp

def _softmax(x, axis=-1):
    return jax.nn.softmax(x, axis=axis)

def _gelu(x):
    return jax.nn.gelu(x, approximate=True)

def _silu(x):
    return jax.nn.silu(x)

def _sigmoid(x):
    return jax.nn.sigmoid(x)

def _layernorm(x, axis=-1, eps=1e-05):
    m = jnp.mean(x, axis=axis, keepdims=True)
    v = jnp.var(x, axis=axis, keepdims=True)
    return (x - m) / jnp.sqrt(v + eps)

def _scatter_add(tgt, idx, src, axis=0):
    return tgt.at[idx].add(src)

def _segment_sum(src, seg, n):
    return jax.ops.segment_sum(src, seg, n)
kernel_name = 'mk_gnn_resnorm_d2_gnn_r64_07ffb2'

def setup_inputs(seed: int=0):
    np.random.seed(seed)
    _w = jnp.asarray

    def _rec_inputs():
        import jax
        import jax.numpy as jnp
        _gk = jax.random.key(seed)
        x = -0.0005121 + 1.001 * jax.random.normal(jax.random.fold_in(_gk, 1), (100000, 64), jnp.float32)
        src = jax.random.randint(jax.random.fold_in(_gk, 2), (50000,), 0, 100000, jnp.int32)
        dst = jnp.minimum((100000 * jax.random.uniform(jax.random.fold_in(_gk, 3), (50000,)) ** 2.0).astype(jnp.int32), 99999)
        _o = jnp.argsort(dst, stable=True)
        src = src[_o]
        dst = dst[_o]
        edge_attr_64 = 0.000103221 + 1.00003 * jax.random.normal(jax.random.fold_in(_gk, 13), (50000, 64), jnp.float32)
        edge_weight1 = 0.00107675 + 0.999702 * jax.random.normal(jax.random.fold_in(_gk, 15), (50000, 1), jnp.float32)
        node_vec1 = jax.random.uniform(jax.random.fold_in(_gk, 16), (100000, 1), jnp.float32, 0.0, 1)
        return (x, src, dst, edge_attr_64, edge_weight1, node_vec1)
    x, src, dst, edge_attr_64, edge_weight1, node_vec1 = _rec_inputs()

    def _L0_gnn_setup():
        import jax, jax.numpy as jnp
        import numpy as np
        N_NODES = 50000
        N_EDGES = 12500
        C_IN = 64
        N_HEADS = 4
        HEAD_DIM = 16
        FC = 64
        key = jax.random.key(seed)
        ks = jax.random.split(key, 20)
        d = {}
        d['node_input'] = jax.random.normal(ks[0], (N_NODES, C_IN), jnp.float32)
        d['node_attr'] = jnp.ones((N_NODES, 1), jnp.float32)
        d['edge_src'] = jax.random.randint(ks[1], (N_EDGES,), 0, N_NODES)
        d['edge_dst'] = jax.random.randint(ks[2], (N_EDGES,), 0, N_NODES)
        d['edge_attr'] = jax.random.normal(ks[3], (N_EDGES, 1), jnp.float32)
        d['edge_scalars'] = jax.random.normal(ks[4], (N_EDGES, FC), jnp.float32)
        d['batch'] = jnp.zeros((N_NODES,), jnp.int32)
        s = 1.0 / np.sqrt(C_IN)
        AD = N_HEADS * HEAD_DIM
        d['Wq'] = jax.random.normal(ks[5], (C_IN, AD), jnp.float32) * s
        d['bq'] = jnp.zeros((AD,), jnp.float32)
        d['W_src'] = jax.random.normal(ks[6], (C_IN, C_IN), jnp.float32) * s
        d['b_src'] = jnp.zeros((C_IN,), jnp.float32)
        d['W_dst'] = jax.random.normal(ks[7], (C_IN, C_IN), jnp.float32) * s
        d['W_fc1'] = jax.random.normal(ks[8], (FC, FC), jnp.float32) * (1.0 / np.sqrt(FC))
        d['b_fc1'] = jnp.zeros((FC,), jnp.float32)
        d['W_fc2'] = jax.random.normal(ks[9], (FC, FC), jnp.float32) * (1.0 / np.sqrt(FC))
        d['b_fc2'] = jnp.zeros((FC,), jnp.float32)
        d['W_fc3'] = jax.random.normal(ks[10], (FC, C_IN), jnp.float32) * (1.0 / np.sqrt(FC))
        d['b_fc3'] = jnp.zeros((C_IN,), jnp.float32)
        d['W_kv'] = jax.random.normal(ks[11], (C_IN, 2 * AD), jnp.float32) * s
        d['b_kv'] = jnp.zeros((2 * AD,), jnp.float32)
        d['W_proj'] = jax.random.normal(ks[12], (AD, C_IN), jnp.float32) * (1.0 / np.sqrt(AD))
        d['b_proj'] = jnp.zeros((C_IN,), jnp.float32)
        return d
    _L0_gnn_all = _L0_gnn_setup()
    _L0_gnn_in = {k: v for k, v in _L0_gnn_all.items() if k in ('Wq', 'bq', 'W_src', 'b_src', 'W_dst', 'W_fc1', 'b_fc1', 'W_fc2', 'b_fc2', 'W_fc3', 'b_fc3', 'W_kv', 'b_kv', 'W_proj', 'b_proj')}
    del _L0_gnn_all

    def _L1_gnn_setup():
        import jax, jax.numpy as jnp
        import numpy as np
        NUM_NODES = 100000
        EMBED_DIM = 64
        NUM_LAYERS = 3
        NUM_EDGES = 1250000
        key = jax.random.key(seed)
        k1, k2 = jax.random.split(key)
        edge_index = jax.random.randint(k1, (2, NUM_EDGES), 0, NUM_NODES, dtype=jnp.int64)
        bound = float(np.sqrt(6.0 / (NUM_NODES + EMBED_DIM)))
        emb = jax.random.uniform(k2, (NUM_NODES, EMBED_DIM), dtype=jnp.float32, minval=-bound, maxval=bound)
        return {'edge_index': edge_index, 'emb': emb}
    _L1_gnn_all = _L1_gnn_setup()
    _L1_gnn_in = {k: v for k, v in _L1_gnn_all.items() if k in ()}
    del _L1_gnn_all
    return {'x': x, 'src': src, 'dst': dst, 'edge_attr_64': edge_attr_64, 'edge_weight1': edge_weight1, 'node_vec1': node_vec1, 'L0_gnn_Wq': _L0_gnn_in['Wq'], 'L0_gnn_bq': _L0_gnn_in['bq'], 'L0_gnn_W_src': _L0_gnn_in['W_src'], 'L0_gnn_b_src': _L0_gnn_in['b_src'], 'L0_gnn_W_dst': _L0_gnn_in['W_dst'], 'L0_gnn_W_fc1': _L0_gnn_in['W_fc1'], 'L0_gnn_b_fc1': _L0_gnn_in['b_fc1'], 'L0_gnn_W_fc2': _L0_gnn_in['W_fc2'], 'L0_gnn_b_fc2': _L0_gnn_in['b_fc2'], 'L0_gnn_W_fc3': _L0_gnn_in['W_fc3'], 'L0_gnn_b_fc3': _L0_gnn_in['b_fc3'], 'L0_gnn_W_kv': _L0_gnn_in['W_kv'], 'L0_gnn_b_kv': _L0_gnn_in['b_kv'], 'L0_gnn_W_proj': _L0_gnn_in['W_proj'], 'L0_gnn_b_proj': _L0_gnn_in['b_proj']}

def reference(x, src, dst, edge_attr_64, edge_weight1, node_vec1, L0_gnn_Wq, L0_gnn_bq, L0_gnn_W_src, L0_gnn_b_src, L0_gnn_W_dst, L0_gnn_W_fc1, L0_gnn_b_fc1, L0_gnn_W_fc2, L0_gnn_b_fc2, L0_gnn_W_fc3, L0_gnn_b_fc3, L0_gnn_W_kv, L0_gnn_b_kv, L0_gnn_W_proj, L0_gnn_b_proj):
    import jax
    import jax.numpy as jnp

    def _L0_gnn_ref(node_input, node_attr, edge_src, edge_dst, edge_attr, edge_scalars, batch, Wq, bq, W_src, b_src, W_dst, W_fc1, b_fc1, W_fc2, b_fc2, W_fc3, b_fc3, W_kv, b_kv, W_proj, b_proj):
        import jax, jax.numpy as jnp
        import numpy as np
        N_NODES = 50000
        N_EDGES = 12500
        C_IN = 64
        N_HEADS = 4
        HEAD_DIM = 16
        FC = 64
        N = node_input.shape[0]
        q = (node_input @ Wq + bq).reshape(N, N_HEADS, HEAD_DIM)
        q = q * (1.0 / jnp.sqrt(jnp.float32(HEAD_DIM)))
        msg_src = node_input @ W_src + b_src
        msg_dst = node_input @ W_dst
        kv = msg_src[edge_src] + msg_dst[edge_dst]
        h = jax.nn.silu(edge_scalars @ W_fc1 + b_fc1)
        h = jax.nn.silu(h @ W_fc2 + b_fc2)
        w = h @ W_fc3 + b_fc3
        tp = kv * edge_attr * w
        kv2 = (tp @ W_kv + b_kv).reshape(-1, 2 * N_HEADS, HEAD_DIM)
        k = kv2[:, :N_HEADS]
        v = kv2[:, N_HEADS:]
        alpha = jnp.einsum('ehd,ehd->eh', q[edge_dst], k)
        seg_max = jax.ops.segment_max(alpha, edge_dst, num_segments=N)
        seg_max = jnp.where(jnp.isfinite(seg_max), seg_max, 0.0)
        ex = jnp.exp(alpha - seg_max[edge_dst])
        denom = jax.ops.segment_sum(ex, edge_dst, num_segments=N)
        alpha = ex / (denom[edge_dst] + 1e-16)
        attn = jax.ops.segment_sum(v * alpha[..., None], edge_dst, num_segments=N)
        attn = attn.reshape(N, N_HEADS * HEAD_DIM)
        return attn @ W_proj + b_proj

    def _L1_gnn_ref(edge_index, emb):
        import jax, jax.numpy as jnp
        import numpy as np
        NUM_NODES = 100000
        EMBED_DIM = 64
        NUM_LAYERS = 3
        NUM_EDGES = 1250000
        row, col = (edge_index[0], edge_index[1])
        num_nodes = emb.shape[0]
        deg = jax.ops.segment_sum(jnp.ones_like(row, dtype=emb.dtype), row, num_segments=num_nodes)
        deg_inv_sqrt = jnp.where(deg > 0, jax.lax.rsqrt(jnp.maximum(deg, 1.0)) * jnp.where(deg > 0, 1.0, 0.0), 0.0)
        deg_inv_sqrt = jnp.where(deg > 0, deg ** (-0.5), 0.0)
        x = emb
        acc = emb
        for _ in range(NUM_LAYERS):
            m = deg_inv_sqrt[row][:, None] * x[col]
            x = jax.ops.segment_sum(m, row, num_segments=num_nodes)
            x = x * deg_inv_sqrt[:, None]
            acc = acc + x
        return acc / (NUM_LAYERS + 1)
    edge_index = jnp.stack([src, dst])
    batch0 = jnp.zeros((100000,), jnp.int32)
    x = _layernorm(x + _L0_gnn_ref(x, node_vec1, src, dst, edge_weight1, edge_attr_64, batch0, L0_gnn_Wq, L0_gnn_bq, L0_gnn_W_src, L0_gnn_b_src, L0_gnn_W_dst, L0_gnn_W_fc1, L0_gnn_b_fc1, L0_gnn_W_fc2, L0_gnn_b_fc2, L0_gnn_W_fc3, L0_gnn_b_fc3, L0_gnn_W_kv, L0_gnn_b_kv, L0_gnn_W_proj, L0_gnn_b_proj), axis=-1)
    x = _layernorm(x + _L1_gnn_ref(edge_index, x), axis=-1)
    return x

_drawn_inputs = setup_inputs


def setup_inputs(seed=0):
    import zlib

    import numpy as np

    out = dict(_drawn_inputs(seed))
    spreads = {'L0_gnn_bq': (0.0, 0.8),
     'L0_gnn_b_src': (0.0, 0.586),
     'L0_gnn_b_fc1': (0.0, 0.384),
     'L0_gnn_b_fc2': (0.0, 0.1),
     'L0_gnn_b_fc3': (0.0, 0.1),
     'L0_gnn_b_kv': (0.0, 0.1),
     'L0_gnn_b_proj': (0.0, 0.1)}
    factors = {}
    for name, (base, spread) in spreads.items():
        noise = np.random.default_rng([zlib.crc32(name.encode()), seed]).standard_normal(out[name].shape)
        drawn = base * np.exp(spread * noise) if base else spread * noise
        out[name] = jnp.asarray(drawn.astype(out[name].dtype))
    for name, factor in factors.items():
        out[name] = (out[name] * factor).astype(out[name].dtype)
    return out
```

```python
import concourse.bass as bass
from concourse import mybir
from contextlib import ExitStack

F32, F16, I32 = mybir.dt.float32, mybir.dt.float16, mybir.dt.int32
ALU = mybir.AluOpType
ACT = mybir.ActivationFunctionType
AX = mybir.AxisListType.X

P = 128
C = 64
HEADS, HD = 4, 16
GROUP = 4
GE = GROUP * P
LO = 256
BLK = 4
KEYS_PER_PART = BLK * LO
PAY = 136
V_W = 69
XD = 72
XW = 65
EPS = 1e-5
BIG = 1e37


class Pool2:

    def __init__(self, nc, tag):
        self.nc, self.tag, self.stack, self.marks = nc, tag, ExitStack(), {}
        self.counters = []

    def sb(self, name, shape, dt=F32):
        return self.stack.enter_context(self.nc.sbuf_tensor(f"{self.tag}_{name}", shape, dt))

    def ps(self, name, shape, dt=F32):
        return self.stack.enter_context(self.nc.psum_tensor(f"{self.tag}_{name}", shape, dt))

    def sem(self, name):
        self.counters.append(self.nc.alloc_semaphore(f"{self.tag}_{name}"))
        return self.counters[-1]

    def sems(self, name, n=2):
        return [self.sem(f"{name}{k}") for k in range(n)]

    def passed(self, engine):
        if engine not in self.marks:
            self.marks[engine] = self.sem(f"passed_{engine}")
        return self.marks[engine]

    def close(self):
        self.stack.close()
        if self.counters:
            self.nc.clear_and_free_semaphores(self.counters)
            self.nc.all_engine_barrier()


class Steps:

    def __init__(self, eng, sem, base=0):
        self.eng, self.sem, self.base, self.n = eng, sem, base, 0

    def did(self, ins):
        ins.then_inc(self.sem, 1)
        self.n += 1

    def settle(self):
        self.eng.wait_ge(self.sem, self.base + self.n)

    def link(self, ins):
        self.did(ins)
        self.settle()


def setup(nc, k, d, io):
    T, HP = d["T"], d["HP"]
    k.ident = k.sb("ident", [P, P])
    k.iota_lo = k.sb("iota_lo", [P, LO], F16)
    k.iota_hi = k.sb("iota_hi", [P, BLK, HP], F16)
    k.hi_of_part = k.sb("hi_of_part", [P, BLK])
    k.below = k.sb("below", [P, P])
    k.earlier = k.sb("earlier", [P, GE], F16)
    k.ones = k.sb("ones", [P, KEYS_PER_PART])
    k.place = k.sb("place", [P, T])
    k.w_kvx = k.sb("w_kvx", [P, C])
    k.w_out = k.sb("w_out", [P, 3 * C])
    k.w_fc = k.sb("w_fc", [C, 3, C])
    k.w_proj = k.sb("w_proj", [C, C])
    k.b_col = k.sb("b_col", [C, 4])
    k.b_kv = k.sb("b_kv", [P, 2 * C])
    k.b_q = k.sb("b_q", [P, GROUP, C])
    k.b_proj = k.sb("b_proj", [P, GROUP, C])
    k.hi, k.lo, k.key = {}, {}, {}
    for key in ("dst", "src"):
        k.hi[key] = k.sb(f"hi_{key}", [P, T])
        k.lo[key] = k.sb(f"lo_{key}", [P, T])
        k.key[key] = k.sb(f"key_{key}", [P, T])
    k.ew = k.sb("ew", [P, T])
    k.d_hi, k.d_key = {}, {}
    for key in ("dst", "src"):
        k.d_hi[key] = nc.dram_tensor(f"hi_rows_{key}", (d["S"], GE), F16).ap()
        k.d_key[key] = nc.dram_tensor(f"key_rows_{key}", (d["S"], GE), F32).ap()

    t = Pool2(nc, "setup")
    S = d["S"]
    ki = t.sb("ki", [P, 2, T], I32)
    ti = t.sb("ti", [S, 2, GE], I32)
    dig = t.sb("dig", [P, 2, T], I32)
    tdig = t.sb("tdig", [S, GE], I32)
    hi16 = t.sb("hi16", [S, 2, GE], F16)
    kf = t.sb("kf", [S, 2, GE])
    tri = t.sb("tri", [P, P])
    loaded, wl, made, v_step, rows, rowsem = (t.sem(n) for n in ("loaded", "weights", "made", "v_step", "rows", "row_w"))
    with nc.Block() as block:
        @block.sync
        def _(sp):
            for n, key in enumerate(("dst", "src")):
                sp.dma_start(ki[:, n, :], io[f"{key}_pt"]).then_inc(loaded, 16)
                sp.dma_start(ti[:, n, :], io[f"{key}_tp"]).then_inc(loaded, 16)
            sp.dma_start(k.ew[:, :], io["ew"]).then_inc(wl, 16)
            sp.dma_start(k.w_kvx[0:C, :], io["W_src"]).then_inc(wl, 16)
            sp.dma_start(k.w_kvx[C:P, :], io["W_dst"]).then_inc(wl, 16)
            sp.wait_ge(made, 1)
            sp.dma_start(k.w_out[0:C, 0:2 * C], io["W_kv"]).then_inc(wl, 16)
            sp.dma_start(k.w_out[C:P, 2 * C:3 * C], io["Wq"]).then_inc(wl, 16)
            for n in range(3):
                sp.dma_start(k.w_fc[:, n, :], io[f"W_fc{n + 1}"]).then_inc(wl, 16)
            sp.dma_start(k.w_proj[:, :], io["W_proj"]).then_inc(wl, 16)
            with nc.allow_non_contiguous_dma(reason="64 biases, one per partition"):
                for n, b in enumerate(("b_fc1", "b_fc2", "b_fc3", "b_src")):
                    sp.dma_start(k.b_col[:, n:n + 1], io[b].rearrange("(c o) -> c o", o=1)).then_inc(wl, 16)
            sp.dma_start(k.b_kv[:, :], io["b_kv"].partition_broadcast(P)).then_inc(wl, 16)
            for g in range(GROUP):
                sp.dma_start(k.b_q[:, g, :], io["bq"].partition_broadcast(P)).then_inc(wl, 16)
                sp.dma_start(k.b_proj[:, g, :], io["b_proj"].partition_broadcast(P)).then_inc(wl, 16)
            sp.wait_ge(wl, 16 * (9 + 4 + 1 + 2 * GROUP))
            sp.wait_ge(rows, 1)
            for n, key in enumerate(("dst", "src")):
                sp.dma_start(k.d_hi[key], hi16[:, n, :]).then_inc(rowsem, 16)
                sp.dma_start(k.d_key[key], kf[:, n, :]).then_inc(rowsem, 16)
            sp.wait_ge(rowsem, 64)

        @block.gpsimd
        def _(g):
            nc.gpsimd.memset(k.w_out[:, :], 0.0).then_inc(made, 1)
            nc.gpsimd.memset(k.ident[:, :], 0.0)
            nc.gpsimd.memset(k.ones[:, :], 1.0)
            nc.gpsimd.memset(tri[:, :], 1.0).then_inc(made, 1)
            nc.gpsimd.iota(k.iota_lo[:, :], pattern=[[1, LO]], base=0, channel_multiplier=0,
                           allow_small_or_imprecise_dtypes=True)
            nc.gpsimd.iota(k.iota_hi[:, :, :], pattern=[[1, BLK], [BLK, HP]], base=0, channel_multiplier=0,
                           allow_small_or_imprecise_dtypes=True)
            nc.gpsimd.iota(k.hi_of_part[:, :], pattern=[[1, BLK]], base=0, channel_multiplier=BLK,
                           allow_small_or_imprecise_dtypes=True)
            nc.gpsimd.iota(k.place[:, :], pattern=[[1, T]], base=0, channel_multiplier=T,
                           allow_small_or_imprecise_dtypes=True)
            nc.gpsimd.memset(k.earlier[:, :], 1.0).then_inc(made, 1)
            g.wait_ge(made, 3)
            nc.gpsimd.affine_select(out=k.ident[:, :], in_=k.ident[:, :], compare_op=ALU.not_equal, fill=1.0,
                                    base=0, pattern=[[-1, P]], channel_multiplier=1)
            nc.gpsimd.affine_select(out=k.below[:, :], in_=tri[:, :], compare_op=ALU.is_gt, fill=0.0,
                                    base=0, pattern=[[1, P]], channel_multiplier=-1)
            last = k.earlier[:, GE - P:GE]
            nc.gpsimd.affine_select(out=last, in_=last, compare_op=ALU.is_gt, fill=0.0,
                                    base=0, pattern=[[-1, P]], channel_multiplier=1).then_inc(made, 1)

        @block.vector
        def _(v):
            st = Steps(v, v_step)
            v.wait_ge(loaded, 64)
            for n, key in enumerate(("dst", "src")):
                nc.vector.tensor_copy(k.key[key][:, :], ki[:, n, :])
                nc.vector.tensor_scalar(dig[:, 0, :], ki[:, n, :], 8, None, ALU.logical_shift_right)
                nc.vector.tensor_copy(kf[:, n, :], ti[:, n, :])
                nc.vector.tensor_scalar(dig[:, 1, :], ki[:, n, :], LO - 1, None, ALU.bitwise_and)
                st.link(nc.vector.tensor_scalar(tdig[:, :], ti[:, n, :], 8, None, ALU.logical_shift_right))
                nc.vector.tensor_copy(k.hi[key][:, :], dig[:, 0, :])
                nc.vector.tensor_copy(k.lo[key][:, :], dig[:, 1, :])
                st.link(nc.vector.tensor_copy(hi16[:, n, :], tdig[:, :]))
            v.wait_ge(wl, 16 * (9 + 4 + 1 + 2 * GROUP))
            nc.vector.tensor_scalar(k.w_out[C:P, 2 * C:3 * C], k.w_out[C:P, 2 * C:3 * C], HD ** -0.5, None, ALU.mult)
            nc.vector.tensor_scalar(k.b_q[:, :, :], k.b_q[:, :, :], HD ** -0.5, None, ALU.mult).then_inc(rows, 1)
    t.close()


def one_hots(nc, k, key, t_at, lo_out, hi_out):
    nc.vector.tensor_scalar(lo_out, k.iota_lo[:, :], k.lo[key][:, bass.ds(t_at, 1)], None, ALU.is_equal)
    return nc.vector.tensor_scalar(hi_out, k.iota_hi[:, :, :], k.hi[key][:, bass.ds(t_at, 1)], None, ALU.is_equal)


def histograms(nc, k, d):
    HP, T = d["HP"], d["T"]
    k.start_hi = {key: k.sb(f"start_hi_{key}", [HP, KEYS_PER_PART], F16) for key in ("dst", "src")}
    k.start_lo = {key: k.sb(f"start_lo_{key}", [HP, KEYS_PER_PART], F16) for key in ("dst", "src")}
    k.d_last = nc.dram_tensor("last_place", (HP, KEYS_PER_PART), F32).ap()
    t = Pool2(nc, "hist")
    keys = ("dst", "src")
    lo1 = [t.sb(f"lo1_{b}", [P, 2, LO], F16) for b in range(4)]
    hi1 = [t.sb(f"hi1_{b}", [P, 2, BLK, HP], F16) for b in range(4)]
    table = [t.ps(f"table_{key}", [HP, KEYS_PER_PART]) for key in keys]
    base = t.ps("base", [HP, 8])
    count = t.sb("count", [HP, 2, KEYS_PER_PART])
    run = t.sb("run", [HP, 2, KEYS_PER_PART])
    start = t.sb("start", [HP, 2, KEYS_PER_PART])
    off = t.sb("off", [HP, 8])
    last = t.sb("last", [HP, KEYS_PER_PART])
    some = t.sb("some", [HP, KEYS_PER_PART])
    ready, used = t.sems("ready", 4), t.sems("used", 4)
    zeroed, counted, totals, based, v_step, out_s, last_s = (
        t.sem(n) for n in ("zeroed", "counted", "totals", "based", "v_step", "out", "last_ready"))
    with nc.Block() as block:
        @block.vector
        def _(v):
            for n in range(2):
                nc.vector.memset(table[n][:, :], 0.0)
            nc.vector.memset(off[:, :], 0.0).then_inc(zeroed, 1)
            with v.Fori(0, T // 4) as i:
                for b in range(4):
                    v.wait_ge(used[b], i)
                    for n, key in enumerate(keys):
                        ins = one_hots(nc, k, key, i * 4 + b, lo1[b][:, n, :], hi1[b][:, n, :, :])
                    ins.then_inc(ready[b], 1)
            st = Steps(v, v_step)
            v.wait_ge(counted, 1)
            for n in range(2):
                st.did(nc.vector.tensor_copy(count[:, n, :], table[n][:, :]))
            st.settle()
            for n in range(2):
                st.did(nc.vector.tensor_tensor_scan(run[:, n, :], k.ones[0:HP, :], count[:, n, :], 0.0,
                                                    ALU.mult, ALU.add))
            st.settle()
            for n in range(2):
                nc.vector.tensor_copy(off[:, n:n + 1], run[:, n, KEYS_PER_PART - 1:KEYS_PER_PART])\
                    .then_inc(totals, 1)
            v.wait_ge(based, 1)
            st.link(nc.vector.tensor_copy(off[:, 2:4], base[:, 0:2]))
            for n, key in enumerate(keys):
                st.link(nc.vector.tensor_tensor(start[:, n, :], run[:, n, :], count[:, n, :], ALU.subtract))
                st.link(nc.vector.tensor_scalar(start[:, n, :], start[:, n, :], off[:, 2 + n:3 + n], None, ALU.add))
                st.link(nc.vector.tensor_copy(k.start_hi[key][:, :], start[:, n, :]))
                st.link(nc.vector.tensor_tensor(k.start_lo[key][:, :], start[:, n, :], k.start_hi[key][:, :],
                                                ALU.subtract))
            st.link(nc.vector.tensor_tensor(last[:, :], start[:, 1, :], count[:, 1, :], ALU.add))
            st.link(nc.vector.tensor_scalar(some[:, :], count[:, 1, :], 1.0, None, ALU.min))
            st.link(nc.vector.scalar_tensor_tensor(last[:, :], last[:, :], -1.0 - d["E_PAD"], some[:, :],
                                                   ALU.add, ALU.mult))
            st.did(nc.vector.tensor_scalar(last[:, :], last[:, :], float(d["E_PAD"]), None, ALU.add))
            st.settle()
            nc.vector.memset(off[:, 4:5], 0.0).then_inc(last_s, 1)

        @block.tensor
        def _(pe):
            pe.wait_ge(zeroed, 1)
            with pe.Fori(0, T // 4) as i:
                for b in range(4):
                    pe.wait_ge(ready[b], i + 1)
                    for n in range(2):
                        for q in range(BLK):
                            ins = nc.tensor.matmul(table[n][:, q * LO:(q + 1) * LO], hi1[b][:, n, q, :],
                                                   lo1[b][:, n, :], start=False, stop=False, skip_group_check=True)
                    ins.then_inc(used[b], 1)
            nc.tensor.matmul(base[:, 4:8], k.below[0:HP, 0:HP], k.ones[0:HP, 0:4], start=True, stop=True)\
                .then_inc(counted, 1)
            pe.wait_ge(totals, 2)
            nc.tensor.matmul(base[:, 0:2], k.below[0:HP, 0:HP], off[:, 0:2], start=True, stop=True)\
                .then_inc(based, 1)

        @block.sync
        def _(sp):
            sp.wait_ge(last_s, 1)
            sp.dma_start(k.d_last, last[:, :]).then_inc(out_s, 16)
            sp.wait_ge(out_s, 16)
    t.close()


def messages(nc, k, d, io):
    T, S = d["T"], d["S"]
    k.d_pay = nc.dram_tensor("payload", (P, T, PAY), F32).ap()
    t = Pool2(nc, "msg")
    two = range(2)
    idx = [t.sb(f"idx{b}", [P, 2, GROUP], I32) for b in two]
    xg = [t.sb(f"xg{b}", [P, GROUP, 2 * C]) for b in two]
    ea = [t.sb(f"ea{b}", [P, GROUP, C]) for b in two]
    xt = [t.sb(f"xt{b}", [P, GE]) for b in two]
    et = [t.sb(f"et{b}", [C, GE]) for b in two]
    h1 = [t.sb(f"h1{b}", [C, GE]) for b in two]
    h2 = [t.sb(f"h2{b}", [C, GE]) for b in two]
    w3 = [t.sb(f"w3{b}", [C, GE]) for b in two]
    pay = [t.sb(f"pay{b}", [P, GROUP, C + PAY]) for b in two]
    qb = [t.sb(f"qb{b}", [P, GROUP, C]) for b in two]
    dst_f = k.key["dst"]
    ps_x = [t.ps(f"ps_x{b}", [P, GE]) for b in two]
    ps_e = [t.ps(f"ps_e{b}", [P, GE]) for b in two]
    ps_o = [t.ps(f"ps_o{b}", [P, 2, GE]) for b in two]
    s = {n: t.sems(n) for n in ("idx_in", "gathered", "ea_in", "x_used", "xT", "xT_sb", "eT", "eT_sb", "h1_ps",
                                "h1_sb", "h2_ps", "h2_sb", "w_ps", "w_sb", "kv_ps", "tp", "out_ps", "out_used",
                                "pay_ready", "stored", "v_step")}
    init = t.sem("init")
    N = S // 2

    def out_tile(b, g, lo, hi):
        return ps_o[b][:, g // 2, (g % 2) * 3 * C + lo:(g % 2) * 3 * C + hi]

    with nc.Block() as block:
        @block.sync
        def _(sp):
            def load(b, n):
                at = n * 2 * GROUP + b * GROUP
                sp.wait_ge(s["gathered"][b], n * 2 * GROUP * 16)
                sp.sem_inc(t.passed("sp"), 1)
                sp.dma_start(idx[b][:, 0, :], io["src_pt"][:, bass.ds(at, GROUP)]).then_inc(s["idx_in"][b], 16)
                sp.dma_start(idx[b][:, 1, :], io["dst_pt"][:, bass.ds(at, GROUP)]).then_inc(s["idx_in"][b], 16)
                sp.wait_ge(s["eT"][b], n)
                sp.sem_inc(t.passed("sp"), 1)
                sp.dma_start(ea[b][:, :, :], io["ea"][:, bass.ds(at, GROUP), :]).then_inc(s["ea_in"][b], 16)

            def store(b, n):
                at = n * 2 * GROUP + b * GROUP
                sp.wait_ge(s["pay_ready"][b], n + 1)
                sp.sem_inc(t.passed("sp"), 1)
                sp.dma_start(k.d_pay[:, bass.ds(at, GROUP), :], pay[b][:, :, C:]).then_inc(s["stored"][b], 16)

            for b in two:
                load(b, 0)
            with sp.Fori(0, N - 1) as i:
                for b in two:
                    load(b, i + 1)
                    store(b, i)
            for b in two:
                store(b, N - 1)
            for b in two:
                sp.wait_ge(s["stored"][b], 16 * N)

        @block.gpsimd
        def _(g):
            with g.Fori(0, N) as i:
                for b in two:
                    g.wait_ge(s["idx_in"][b], i * 32 + 32)
                    g.wait_ge(s["x_used"][b], i)
                    g.wait_ge(s["xT"][b], i)
                    g.sem_inc(t.passed("pool"), 1)
                    for side in two:
                        for q in range(GROUP):
                            g.indirect_dma_start(
                                out=xg[b][:, q, side * C:(side + 1) * C], out_offset=None, in_=io["x"],
                                in_offset=bass.IndirectOffsetOnAxis(ap=idx[b][:, side, q:q + 1], axis=0),
                            ).then_inc(s["gathered"][b], 16)

        @block.tensor
        def _(pe):
            with pe.Fori(0, N) as i:
                for b in two:
                    pe.wait_ge(s["ea_in"][b], i * 16 + 16)
                    pe.wait_ge(s["w_sb"][b], i)
                    pe.sem_inc(t.passed("pe"), 1)
                    for q in range(GROUP):
                        ins = nc.tensor.transpose(ps_e[b][0:C, q * P:(q + 1) * P], ea[b][:, q, :], k.ident[:, :])
                    ins.then_inc(s["eT"][b], 1)
                for b in two:
                    pe.wait_ge(s["eT_sb"][b], i + 1)
                    pe.sem_inc(t.passed("pe"), 1)
                    nc.tensor.matmul(ps_e[b][0:C, :], k.w_fc[:, 0, :], et[b][:, :], start=True, stop=True)\
                        .then_inc(s["h1_ps"][b], 1)
                for b in two:
                    pe.wait_ge(s["gathered"][b], i * 128 + 128)
                    pe.wait_ge(s["tp"][b], i)
                    for q in range(GROUP):
                        ins = nc.tensor.transpose(ps_x[b][:, q * P:(q + 1) * P], xg[b][:, q, :], k.ident[:, :])
                    ins.then_inc(s["xT"][b], 1)
                    pe.wait_ge(s["h1_sb"][b], i + 1)
                    pe.sem_inc(t.passed("pe"), 1)
                    nc.tensor.matmul(ps_e[b][0:C, :], k.w_fc[:, 1, :], h1[b][:, :], start=True, stop=True)\
                        .then_inc(s["h2_ps"][b], 1)
                for b in two:
                    pe.wait_ge(s["xT_sb"][b], i + 1)
                    nc.tensor.matmul(ps_x[b][0:C, :], k.w_kvx[:, :], xt[b][:, :], start=True, stop=True)\
                        .then_inc(s["kv_ps"][b], 1)
                    pe.wait_ge(s["h2_sb"][b], i + 1)
                    pe.sem_inc(t.passed("pe"), 1)
                    nc.tensor.matmul(ps_e[b][0:C, :], k.w_fc[:, 2, :], h2[b][:, :], start=True, stop=True)\
                        .then_inc(s["w_ps"][b], 1)
                for b in two:
                    pe.wait_ge(s["tp"][b], i + 1)
                    pe.wait_ge(s["out_used"][b], i)
                    for q in range(GROUP):
                        ins = nc.tensor.matmul(out_tile(b, q, 0, 3 * C), xt[b][:, q * P:(q + 1) * P],
                                               k.w_out[:, :], start=True, stop=True)
                    ins.then_inc(s["out_ps"][b], 1)

        @block.scalar
        def _(act):
            with act.Fori(0, N) as i:
                for b in two:
                    act.wait_ge(s["eT"][b], i + 1)
                    nc.scalar.activation(et[b][:, :], ps_e[b][0:C, :], ACT.Copy).then_inc(s["eT_sb"][b], 1)
                for b in two:
                    act.wait_ge(s["h1_ps"][b], i + 1)
                    nc.scalar.activation(h1[b][:, :], ps_e[b][0:C, :], ACT.Silu, bias=k.b_col[:, 0:1])\
                        .then_inc(s["h1_sb"][b], 1)
                for b in two:
                    act.wait_ge(s["xT"][b], i + 1)
                    act.wait_ge(s["out_ps"][b], i)
                    nc.scalar.activation(xt[b][:, :], ps_x[b][:, :], ACT.Copy).then_inc(s["xT_sb"][b], 1)
                    act.wait_ge(s["h2_ps"][b], i + 1)
                    nc.scalar.activation(h2[b][:, :], ps_e[b][0:C, :], ACT.Silu, bias=k.b_col[:, 1:2])\
                        .then_inc(s["h2_sb"][b], 1)
                for b in two:
                    act.wait_ge(s["w_ps"][b], i + 1)
                    act.wait_ge(s["tp"][b], i)
                    nc.scalar.activation(w3[b][:, :], ps_e[b][0:C, :], ACT.Identity, bias=k.b_col[:, 2:3])\
                        .then_inc(s["w_sb"][b], 1)

        @block.vector
        def _(v):
            for b in two:
                nc.vector.memset(pay[b][:, :, :], 0.0).then_inc(init, 1)
            v.wait_ge(init, 2)
            with v.Fori(0, N) as i:
                for b in two:
                    at = i * 2 * GROUP + b * GROUP
                    v.wait_ge(s["gathered"][b], i * 128 + 128)
                    v.wait_ge(s["stored"][b], i * 16)
                    nc.vector.tensor_copy(pay[b][:, :, C + XD:], xg[b][:, :, C:]).then_inc(s["x_used"][b], 1)
                    nc.vector.tensor_scalar(pay[b][:, :, C + 68], dst_f[:, bass.ds(at, GROUP)], 1.0, None, ALU.mult)
                for b in two:
                    v.wait_ge(s["kv_ps"][b], i + 1)
                    v.wait_ge(s["w_sb"][b], i + 1)
                    nc.vector.scalar_tensor_tensor(xt[b][0:C, :], ps_x[b][0:C, :], k.b_col[:, 3:4], w3[b][:, :],
                                                   ALU.add, ALU.mult).then_inc(s["tp"][b], 1)
                for b in two:
                    st = Steps(v, s["v_step"][b], i * 4)
                    v.wait_ge(s["out_ps"][b], i + 1)
                    for q in range(GROUP):
                        at = i * 2 * GROUP + (b * GROUP + q)
                        ins = nc.vector.scalar_tensor_tensor(pay[b][:, q, 0:2 * C], out_tile(b, q, 0, 2 * C),
                                                             k.ew[:, bass.ds(at, 1)], k.b_kv[:, :],
                                                             ALU.mult, ALU.add)
                    st.did(ins)
                    q_ps = ps_o[b][:, :, 0:6 * C].rearrange("p a (t c) -> p a t c", t=2)[:, :, :, 2 * C:3 * C]
                    ins = nc.vector.tensor_tensor(qb[b][:, :, :].rearrange("p (a t) c -> p a t c", t=2), q_ps,
                                                  k.b_q[:, :, :].rearrange("p (a t) c -> p a t c", t=2), ALU.add)
                    st.did(ins)
                    st.settle()
                    st.link(nc.vector.tensor_tensor(qb[b][:, :, :], qb[b][:, :, :], pay[b][:, :, 0:C], ALU.mult))
                    st.did(nc.vector.tensor_reduce(pay[b][:, :, 2 * C:2 * C + HEADS],
                                                   qb[b][:, :, :].rearrange("p g (h c) -> p g h c", h=HEADS),
                                                   AX, ALU.add))
                    st.settle()
                    v.sem_inc(s["pay_ready"][b], 1)
                    v.sem_inc(s["out_used"][b], 1)
    t.close()


def positions(nc, k, d, key, payload, width, dt, out):
    T, S, HP = d["T"], d["S"], d["HP"]
    t = Pool2(nc, f"pos_{key}")
    two = range(2)
    N = S // 2
    hi_b = [t.sb(f"hi_b{b}", [HP, GE], F16) for b in two]
    key_b = [t.sb(f"key_b{b}", [P, GE]) for b in two]
    pay = [t.sb(f"pay{b}", [P, GROUP, width], dt) for b in two]
    hi_t = [t.sb(f"hi_t{b}", [HP, BLK, GE], F16) for b in two]
    lo1 = [t.sb(f"lo1{b}", [P, GROUP, LO], F16) for b in two]
    hi1 = [t.sb(f"hi1{b}", [P, GROUP, BLK, HP], F16) for b in two]
    run_hi = [t.sb(f"run_hi{b}", [HP, KEYS_PER_PART], F16) for b in two]
    run_lo = [t.sb(f"run_lo{b}", [HP, KEYS_PER_PART], F16) for b in two]
    junk = [t.sb(f"junk{b}", [P, GROUP, LO], F16) for b in two]
    same = [t.sb(f"same{b}", [P, GROUP, GE], F16) for b in two]
    rank = [t.sb(f"rank{b}", [P, GROUP]) for b in two]
    base = [t.sb(f"base{b}", [P, GROUP]) for b in two]
    pos = [t.sb(f"pos{b}", [P, GROUP], I32) for b in two]
    ident16 = t.sb("ident16", [P, P], F16)
    table = t.ps("table", [HP, KEYS_PER_PART])
    look = [t.ps(f"look{b}", [P, GROUP, LO]) for b in two]
    s = {n: t.sems(n) for n in ("rows_in", "pay_in", "prepared", "hi_made", "split", "updated", "looked", "reduced",
                                "pos_ready", "scattered", "v_step")}
    zeroed, started = t.sem("zeroed"), t.sem("started")

    with nc.Block() as block:
        @block.sync
        def _(sp):
            with sp.Fori(0, N) as i:
                for b in two:
                    at = i * 2 + b
                    sp.wait_ge(s["prepared"][b], i)
                    sp.sem_inc(t.passed("sp"), 1)
                    sp.dma_start(hi_b[b][:, :], k.d_hi[key][bass.ds(at, 1), :].to_broadcast([HP, GE]))\
                        .then_inc(s["rows_in"][b], 16)
                    sp.dma_start(key_b[b][:, :], k.d_key[key][bass.ds(at, 1), :].to_broadcast([P, GE]))\
                        .then_inc(s["rows_in"][b], 16)
                    sp.wait_ge(s["scattered"][b], i * GROUP * 16)
                    sp.sem_inc(t.passed("sp"), 1)
                    sp.dma_start(pay[b][:, :, :], payload[:, bass.ds(i * 2 * GROUP + b * GROUP, GROUP), :])\
                        .then_inc(s["pay_in"][b], 16)

        @block.scalar
        def _(act):
            def head(b, n):
                if b == 0:
                    act.wait_ge(s["updated"][1], n)
                    act.wait_ge(started, 1)
                else:
                    act.wait_ge(s["updated"][0], n + 1)
                act.wait_ge(s["looked"][b], n)
                nc.scalar.activation(run_hi[b][:, :], table[:, :], ACT.Copy).then_inc(s["hi_made"][b], 1)

            with act.Fori(0, N) as i:
                for b in two:
                    head(b, i)

        @block.tensor
        def _(pe):
            pe.wait_ge(zeroed, 1)
            for half in (k.start_hi[key], k.start_lo[key]):
                for q in range(0, KEYS_PER_PART, 512):
                    ins = nc.tensor.matmul(table[:, q:q + 512], ident16[0:HP, 0:HP], half[:, q:q + 512],
                                           start=False, stop=False, skip_group_check=True)
            ins.then_inc(started, 1)
            with pe.Fori(0, N) as i:
                for b in two:
                    pe.wait_ge(s["prepared"][b], i + 1)
                    pe.wait_ge(s["split"][b], i + 1)
                    for g in range(GROUP):
                        for q in range(BLK):
                            ins = nc.tensor.matmul(table[:, q * LO:(q + 1) * LO], hi1[b][:, g, q, :],
                                                   lo1[b][:, g, :], start=False, stop=False, skip_group_check=True)
                    ins.then_inc(s["updated"][b], 1)
                    pe.wait_ge(s["reduced"][b], i)
                    for g in range(GROUP):
                        n = 0
                        for part in (run_hi[b], run_lo[b]):
                            for q in range(BLK):
                                ins = nc.tensor.matmul(look[b][:, g, :], hi_t[b][:, q, g * P:(g + 1) * P],
                                                       part[:, q * LO:(q + 1) * LO],
                                                       start=(n == 0), stop=(n == 2 * BLK - 1))
                                n += 1
                    ins.then_inc(s["looked"][b], 1)

        @block.vector
        def _(v):
            nc.vector.memset(table[:, :], 0.0)
            nc.vector.tensor_copy(ident16[:, :], k.ident[:, :]).then_inc(zeroed, 1)

            def prepare(b, n):
                v.wait_ge(s["rows_in"][b], n * 32 + 32)
                v.wait_ge(s["looked"][b], n)
                v.wait_ge(s["pos_ready"][b], n)
                for q in range(BLK):
                    nc.vector.tensor_scalar(hi_t[b][:, q, :], hi_b[b][:, :], k.hi_of_part[0:HP, q:q + 1], None,
                                            ALU.is_equal)
                for g in range(GROUP):
                    at = n * 2 * GROUP + (b * GROUP + g)
                    one_hots(nc, k, key, at, lo1[b][:, g, :], hi1[b][:, g, :, :])
                for g in range(GROUP):
                    at = n * 2 * GROUP + (b * GROUP + g)
                    w = (g + 1) * P
                    ins = nc.vector.scalar_tensor_tensor(same[b][:, g, 0:w], key_b[b][:, 0:w], k.key[key][:, bass.ds(at, 1)],
                                                         k.earlier[:, GE - w:], ALU.is_equal, ALU.mult,
                                                         accum_out=rank[b][:, g:g + 1])
                ins.then_inc(s["prepared"][b], 1)
                v.wait_ge(s["hi_made"][b], n + 1)
                nc.vector.tensor_tensor(run_lo[b][:, :], table[:, :], run_hi[b][:, :], ALU.subtract)\
                    .then_inc(s["split"][b], 1)

            def reduce(b, n):
                v.wait_ge(s["looked"][b], n + 1)
                for g in range(GROUP):
                    ins = nc.vector.tensor_tensor_reduce(out=junk[b][:, g, :], in0=lo1[b][:, g, :], in1=look[b][:, g, :],
                                                         scale=1.0, scalar=0.0, op0=ALU.mult, op1=ALU.add,
                                                         accum_out=base[b][:, g:g + 1])
                ins.then_inc(s["reduced"][b], 1)
                v.wait_ge(s["reduced"][b], n + 1)
                v.wait_ge(s["scattered"][b], n * GROUP * 16)
                nc.vector.tensor_tensor(pos[b][:, :], base[b][:, :], rank[b][:, :], ALU.add)\
                    .then_inc(s["pos_ready"][b], 1)

            prepare(0, 0)
            with v.Fori(0, N - 1) as i:
                prepare(1, i)
                reduce(0, i)
                prepare(0, i + 1)
                reduce(1, i)
            prepare(1, N - 1)
            reduce(0, N - 1)
            reduce(1, N - 1)

        @block.gpsimd
        def _(g):
            with g.Fori(0, N) as i:
                for b in two:
                    g.wait_ge(s["pos_ready"][b], i + 1)
                    g.wait_ge(s["pay_in"][b], i * 16 + 16)
                    g.sem_inc(t.passed("pool"), 1)
                    for q in range(GROUP):
                        g.indirect_dma_start(out=out, out_offset=bass.IndirectOffsetOnAxis(ap=pos[b][:, q:q + 1], axis=0),
                                             in_=pay[b][:, q, :], in_offset=None).then_inc(s["scattered"][b], 16)
            for b in two:
                g.wait_ge(s["scattered"][b], N * GROUP * 16)
    t.close()


def nodes_dense(nc, k, d, io, final):
    R, J = d["R"], d["J"]
    N = R // J // 2
    t = Pool2(nc, "final" if final else "first")
    two = range(2)
    xin = [t.sb(f"x{b}", [P, J, XW]) for b in two]
    acc = [t.sb(f"acc{b}", [P, J, C]) for b in two]
    cen = [t.sb(f"cen{b}", [P, J, C]) for b in two]
    sq = [t.sb(f"sq{b}", [P, J, C]) for b in two]
    stat = [t.sb(f"stat{b}", [P, 4, J]) for b in two]
    res = [t.sb(f"res{b}", [P, J, C if final else XW]) for b in two]
    eps = t.sb("eps", [P, 1])
    s = {n: t.sems(n) for n in ("in", "cen", "sq", "var", "dev", "scale", "res", "stored", "v_step")}
    init, zero_s, zeroed, x_ok = t.sem("init"), t.sem("zero"), t.sem("zeroed"), t.sem("x_ok")
    xt_rows = k.d_xt.rearrange("(a b) o -> a (b o)", b=XW)
    xt_nodes = xt_rows[0:d["N_PAD"], :].rearrange("(p r) c -> p r c", r=R)
    if not final:
        bias = t.sb("bias", [P, J, C])
        zeros = t.sb("zeros", [P, 28 * C])
        x_nodes = io["x"].rearrange("(p r) c -> p r c", r=R)
        last_nodes = k.d_last.rearrange("a b -> (a b)").rearrange("(p r) -> p r", r=R)
        last_sb = t.sb("last", [P, R])
    acc_nodes = k.d_acc[0:d["N_PAD"], :].rearrange("(p r) c -> p r c", r=R)
    with nc.Block() as block:
        @block.sync
        def _(sp):
            def load(b, n):
                at = n * 2 * J + b * J
                sp.wait_ge(s["cen"][b], n)
                if final:
                    sp.dma_start(xin[b][:, :, :], xt_nodes[:, bass.ds(at, J), :]).then_inc(s["in"][b], 16)
                    sp.dma_start(acc[b][:, :, :], acc_nodes[:, bass.ds(at, J), :]).then_inc(s["in"][b], 16)
                else:
                    sp.dma_start(xin[b][:, :, 0:C], x_nodes[:, bass.ds(at, J), :]).then_inc(s["in"][b], 32)

            def store(b, n):
                at = n * 2 * J + b * J
                sp.wait_ge(s["res"][b], n + 1)
                sp.sem_inc(t.passed("sp"), 1)
                to = io["out"].rearrange("(p r) c -> p r c", r=R) if final else xt_nodes
                sp.dma_start(to[:, bass.ds(at, J), :], res[b][:, :, :]).then_inc(s["stored"][b], 16)

            if not final:
                sp.dma_start(last_sb[:, :], last_nodes).then_inc(x_ok, 16)
            for b in two:
                load(b, 0)
            with sp.Fori(0, N - 1) as i:
                for b in two:
                    load(b, i + 1)
                    store(b, i)
            for b in two:
                store(b, N - 1)
            for b in two:
                sp.wait_ge(s["stored"][b], 16 * N)

        @block.scalar
        def _(act):
            with act.Fori(0, N) as i:
                for b in two:
                    act.wait_ge(s["cen"][b], i + 1)
                    nc.scalar.activation(sq[b][:, :, :], cen[b][:, :, :], ACT.Square).then_inc(s["sq"][b], 1)
                for b in two:
                    act.wait_ge(s["var"][b], i + 1)
                    nc.scalar.activation(stat[b][:, 2, :], stat[b][:, 1, :], ACT.Sqrt, bias=eps[:, 0:1],
                                         scale=1.0 / C).then_inc(s["dev"][b], 1)
            if not final:
                act.wait_ge(init, 1)
                zv = k.d_acc[0:d["N_PAD"], :].rearrange("(p m r) c -> m p (r c)", p=P, r=28)
                for m in range(R // 28):
                    act.dma_start(zv[m], zeros[:, :]).then_inc(zero_s, 16)
                for z in k.d_z[0:2]:
                    act.dma_start(z[d["E_PAD"]:d["E_PAD"] + P, :], zeros[:, 0:C]).then_inc(zero_s, 16)
                act.wait_ge(zero_s, 16 * (R // 28 + 2))

        @block.vector
        def _(v):
            if not final:
                nc.vector.memset(zeros[:, :], 0.0)
                for j in range(J):
                    nc.vector.tensor_copy(bias[:, j, :], k.b_proj[:, 0, :])
            nc.vector.memset(eps[:, :], EPS).then_inc(init, 1)
            v.wait_ge(init, 1)
            if not final:
                v.wait_ge(x_ok, 16)

            def centre(b, n):
                st = Steps(v, s["v_step"][b], n * (4 if final else 3))
                v.wait_ge(s["in"][b], n * 32 + 32)
                x = xin[b][:, :, 0:C]
                if final:
                    st.link(nc.vector.tensor_scalar(acc[b][:, :, :], acc[b][:, :, :], 0.25, None, ALU.mult))
                    st.link(nc.vector.scalar_tensor_tensor(x, x, 1.25, acc[b][:, :, :], ALU.mult, ALU.add))
                else:
                    st.link(nc.vector.tensor_tensor(x, x, bias[:, :, :], ALU.add))
                st.link(nc.vector.tensor_reduce(stat[b][:, 0, :], x, AX, ALU.add))
                st.link(nc.vector.tensor_scalar(stat[b][:, 0, :], stat[b][:, 0, :], 1.0 / C, None, ALU.mult))
                nc.vector.tensor_tensor(cen[b][:, :, :], x, stat[b][:, 0, :].unsqueeze(2).to_broadcast([P, J, C]),
                                        ALU.subtract).then_inc(s["cen"][b], 1)

            def finish(b, n):
                v.wait_ge(s["stored"][b], n * 16)
                if not final:
                    nc.vector.tensor_scalar(res[b][:, :, C], last_sb[:, bass.ds(n * 2 * J + b * J, J)], 1.0, None,
                                            ALU.mult)
                nc.vector.tensor_tensor(res[b][:, :, 0:C], cen[b][:, :, :],
                                        stat[b][:, 3, :].unsqueeze(2).to_broadcast([P, J, C]), ALU.mult)\
                    .then_inc(s["res"][b], 1)

            with v.Fori(0, N) as i:
                for b in two:
                    centre(b, i)
                for b in two:
                    v.wait_ge(s["sq"][b], i + 1)
                    nc.vector.tensor_reduce(stat[b][:, 1, :], sq[b][:, :, :], AX, ALU.add).then_inc(s["var"][b], 1)
                for b in two:
                    v.wait_ge(s["dev"][b], i + 1)
                    nc.vector.reciprocal(stat[b][:, 3, :], stat[b][:, 2, :]).then_inc(s["scale"][b], 1)
                for b in two:
                    v.wait_ge(s["scale"][b], i + 1)
                    finish(b, i)
    t.close()


def segments(nc, k, d, g, tag):
    T = d["T"]
    t = Pool2(nc, f"seg_{tag}")
    before, after = t.sb("before", [P, 1]), t.sb("after", [P, 1])
    n_lead = t.sb("n_lead", [P, 1])
    rowf = t.sb("rowf", [P, 1])
    away = t.sb("away", [P, T])
    v_step, shifted, ready = t.sem("v_step"), t.sem("shifted"), t.sem("ready")
    with nc.Block() as block:
        @block.sync
        def _(sp):
            sp.wait_ge(ready, 1)
            with nc.allow_non_contiguous_dma(reason="one key per partition"):
                sp.dma_start(before[1:P, :], g.key[0:P - 1, T - 1:T]).then_inc(shifted, 16)
                sp.dma_start(after[0:P - 1, :], g.key[1:P, 0:1]).then_inc(shifted, 16)

        @block.vector
        def _(v):
            st = Steps(v, v_step)
            nc.vector.memset(before[:, :], -1.0)
            nc.vector.memset(g.cont[:, 0:1], 0.0)
            nc.vector.memset(after[:, :], -1.0).then_inc(ready, 1)
            st.did(nc.vector.tensor_tensor(g.cont[:, 1:T], g.key[:, 1:T], g.key[:, 0:T - 1], ALU.is_equal))
            st.did(nc.vector.tensor_tensor(g.last[:, 0:T - 1], g.key[:, 0:T - 1], g.key[:, 1:T], ALU.not_equal))
            st.link(nc.vector.tensor_scalar(g.lead[:, :], g.key[:, :], g.key[:, 0:1], None, ALU.is_equal))
            st.link(nc.vector.tensor_reduce(n_lead[:, :], g.lead[:, :], AX, ALU.add))
            st.did(nc.vector.tensor_scalar(g.whole[:, :], n_lead[:, :], float(T), None, ALU.is_equal))
            nc.vector.memset(g.end_lead[:, T - 1:T], 1.0)
            st.did(nc.vector.tensor_copy(g.end_lead[:, 0:T - 1], g.last[:, 0:T - 1]))
            st.link(nc.vector.scalar_tensor_tensor(rowf[:, :], n_lead[:, :], -1.0, k.place[:, 0:1], ALU.add, ALU.add))
            nc.vector.tensor_copy(g.row[:, :], rowf[:, :])
            st.did(nc.vector.tensor_tensor(g.end_lead[:, :], g.end_lead[:, :], g.lead[:, :], ALU.mult))
            v.wait_ge(shifted, 32)
            st.did(nc.vector.tensor_tensor(g.joins[:, :], g.key[:, 0:1], before[:, :], ALU.is_equal))
            st.link(nc.vector.tensor_tensor(g.last[:, T - 1:T], g.key[:, T - 1:T], after[:, :], ALU.not_equal))
            st.link(nc.vector.tensor_scalar(away[:, :], k.place[:, :], float(d["N_PAD"]), None, ALU.add))
            st.link(nc.vector.tensor_tensor(g.at[:, :], g.key[:, :], away[:, :], ALU.subtract))
            st.link(nc.vector.tensor_tensor(g.at[:, :], g.at[:, :], g.last[:, :], ALU.mult))
            st.link(nc.vector.tensor_tensor(g.at[:, :], g.at[:, :], away[:, :], ALU.add))
    t.close()


class Segments:
    def __init__(self, m, T):
        self.key, self.cont, self.last, self.lead, self.end_lead, self.at = (
            m.sb(n, [P, T]) for n in ("key", "cont", "last", "lead", "end_lead", "at"))
        self.joins, self.whole, self.row = m.sb("joins", [P, 1]), m.sb("whole", [P, 1]), m.sb("row", [P, 1], I32)


def hand_over(nc, k, tag, width, state, carry, op, weight):
    t = Pool2(nc, f"hand_{tag}")
    ps_s, ps_w, ps_b = t.ps("state", [P, P]), t.ps("weight", [P, P]), t.ps("back", [P, P])
    wt = t.sb("wt", [P, P])
    out = t.sb("out", [P, P + 1])
    turned, wt_in, scanned, back = t.sem("turned"), t.sem("wt_in"), t.sem("scanned"), t.sem("back")
    with nc.Block() as block:
        @block.tensor
        def _(pe):
            nc.tensor.transpose(ps_s[0:width, :], state, k.ident[:, :])
            nc.tensor.transpose(ps_w[0:width, :], weight, k.ident[:, :]).then_inc(turned, 1)
            pe.wait_ge(scanned, 1)
            nc.tensor.transpose(ps_b[:, 0:width], out[0:width, 0:P], k.ident[0:width, 0:width]).then_inc(back, 1)

        @block.vector
        def _(v):
            nc.vector.memset(out[0:width, 0:1], 0.0)
            v.wait_ge(turned, 1)
            nc.vector.tensor_copy(wt[0:width, :], ps_w[0:width, :]).then_inc(wt_in, 1)
            v.wait_ge(wt_in, 1)
            nc.vector.tensor_tensor_scan(out[0:width, 1:P + 1], wt[0:width, :], ps_s[0:width, :], 0.0,
                                         ALU.mult if op == ALU.add else ALU.add, op).then_inc(scanned, 1)
            v.wait_ge(back, 1)
            nc.vector.tensor_copy(carry, ps_b[:, 0:width])
    t.close()


def attention(nc, k, d, io):
    T, S = d["T"], d["S"]
    m = Pool2(nc, "att")
    g = Segments(m, T)
    V = m.sb("values", [P, T, V_W])
    top = m.sb("top", [P, HEADS, T])
    wgt = m.sb("wgt", [P, HEADS, T])
    pen = m.sb("pen", [P, T])
    tail, carry = m.sb("tail", [P, 80]), m.sb("carry", [P, 80])
    w4, top_lead, decay = m.sb("w4", [P, HEADS]), m.sb("top_lead", [P, HEADS]), m.sb("decay", [P, HEADS])
    factor = m.sb("factor", [P, C + HEADS])
    factor_w = m.sb("factor_w", [P, C + HEADS])
    rden = m.sb("rden", [P, T, HEADS])
    at65 = m.sb("at65", [P, T])
    pay_rows = k.d_pay_sorted.rearrange("(p t) c -> p t c", t=T)

    a = Pool2(nc, "att_load")
    loaded, keyed = a.sem("loaded"), a.sem("keyed")
    with nc.Block() as block:
        @block.sync
        def _(sp):
            q = T // 4
            for c in range(4):
                sp.dma_start(V[:, c * q:(c + 1) * q, :], pay_rows[:, c * q:(c + 1) * q, 0:V_W]).then_inc(loaded, 16)

        @block.vector
        def _(v):
            v.wait_ge(loaded, 64)
            nc.vector.tensor_copy(g.key[:, :], V[:, :, 68]).then_inc(keyed, 1)
    a.close()
    segments(nc, k, d, g, "dst")

    a = Pool2(nc, "att_max")
    step = a.sem("step")
    with nc.Block() as block:
        @block.vector
        def _(v):
            st = Steps(v, step)
            st.link(nc.vector.tensor_scalar(pen[:, :], g.cont[:, :], -1.0, BIG, ALU.add, ALU.mult))
            for h in range(HEADS):
                st.did(nc.vector.tensor_tensor_scan(top[:, h, :], pen[:, :], V[:, :, C + h], -BIG, ALU.add, ALU.max))
            st.settle()
            st.did(nc.vector.tensor_copy(tail[:, 0:HEADS], top[:, :, T - 1]))
            st.link(nc.vector.tensor_tensor(w4[:, 0:1], g.joins[:, :], g.whole[:, :], ALU.mult))
            for h in range(HEADS):
                st.did(nc.vector.tensor_scalar(tail[:, 8 + h:9 + h], w4[:, 0:1], -1.0, BIG, ALU.add, ALU.mult))
            st.settle()
    a.close()
    hand_over(nc, k, "max", HEADS, tail[:, 0:HEADS], carry[:, 0:HEADS], ALU.max, tail[:, 8:8 + HEADS])

    a = Pool2(nc, "att_sum")
    step, for_exp, exped = a.sem("step"), a.sem("for_exp"), a.sem("exped")
    diff = a.sb("diff", [P, HEADS, T])
    with nc.Block() as block:
        @block.scalar
        def _(act):
            act.wait_ge(for_exp, 1)
            nc.scalar.activation(wgt[:, :, :], wgt[:, :, :], ACT.Exp)
            nc.scalar.activation(diff[:, :, :], diff[:, :, :], ACT.Exp)
            nc.scalar.activation(decay[:, :], decay[:, :], ACT.Exp).then_inc(exped, 1)

        @block.vector
        def _(v):
            st = Steps(v, step)
            st.link(nc.vector.tensor_scalar(pen[:, :], g.lead[:, :], g.joins[:, 0:1], -1.0, ALU.mult, ALU.add))
            st.link(nc.vector.tensor_scalar(pen[:, :], pen[:, :], BIG, None, ALU.mult))
            for h in range(HEADS):
                st.did(nc.vector.scalar_tensor_tensor(top[:, h, :], pen[:, :], carry[:, h:h + 1], top[:, h, :],
                                                      ALU.add, ALU.max))
            st.settle()
            st.did(nc.vector.tensor_scalar(pen[:, :], g.lead[:, :], -1.0, BIG, ALU.add, ALU.mult))
            st.settle()
            for h in range(HEADS):
                st.did(nc.vector.tensor_tensor(diff[:, h, :], top[:, h, :], pen[:, :], ALU.add))
                st.did(nc.vector.tensor_tensor(wgt[:, h, :], V[:, :, C + h], top[:, h, :], ALU.subtract))
            st.settle()
            st.link(nc.vector.tensor_reduce(top_lead[:, :], diff[:, :, :], AX, ALU.max))
            st.link(nc.vector.tensor_tensor(decay[:, :], carry[:, 0:HEADS], top_lead[:, :], ALU.subtract))
            nc.vector.tensor_scalar(decay[:, :], decay[:, :], 0.0, None, ALU.min)
            st.did(nc.vector.memset(diff[:, :, 0:1], 0.0))
            st.link(nc.vector.tensor_tensor(diff[:, :, 1:T], top[:, :, 0:T - 1], top[:, :, 1:T], ALU.subtract))
            nc.vector.tensor_scalar(diff[:, :, :], diff[:, :, :], 0.0, None, ALU.min).then_inc(for_exp, 1)
            v.wait_ge(exped, 1)
            for h in range(HEADS):
                cols = slice(h * HD, (h + 1) * HD)
                st.did(nc.vector.tensor_tensor(top[:, h, :], diff[:, h, :], g.cont[:, :], ALU.mult))
                st.did(nc.vector.tensor_copy(V[:, :, C + h], wgt[:, h, :]))
                st.did(nc.vector.tensor_tensor(V[:, :, cols], V[:, :, cols],
                                               wgt[:, h, :].unsqueeze(2).to_broadcast([P, T, HD]), ALU.mult))
            st.settle()
            with v.Fori(0, HD) as f:
                for h in range(HEADS):
                    col = V[:, :, bass.ds(f + h * HD, 1)].rearrange("p t o -> p (t o)")
                    nc.vector.tensor_tensor_scan(col, top[:, h, :], col, 0.0, ALU.mult, ALU.add)
            for h in range(HEADS):
                st.did(nc.vector.tensor_tensor_scan(V[:, :, C + h], top[:, h, :], V[:, :, C + h], 0.0,
                                                    ALU.mult, ALU.add))
            st.settle()
            st.did(nc.vector.tensor_copy(tail[:, 0:C + HEADS], V[:, T - 1, 0:C + HEADS]))
            st.link(nc.vector.tensor_scalar(decay[:, :], decay[:, :], g.joins[:, 0:1], None, ALU.mult))
            st.did(nc.vector.tensor_copy(factor[:, 0:C].rearrange("p (h c) -> p h c", h=HEADS),
                                         decay[:, :].unsqueeze(2).to_broadcast([P, HEADS, HD])))
            st.did(nc.vector.tensor_copy(factor[:, C:C + HEADS], decay[:, :]))
            st.settle()
            st.link(nc.vector.tensor_scalar(factor_w[:, :], factor[:, :], g.whole[:, 0:1], None, ALU.mult))
    a.close()
    hand_over(nc, k, "sum", C + HEADS, tail[:, 0:C + HEADS], carry[:, 0:C + HEADS], ALU.add, factor_w[:, :])

    a = Pool2(nc, "att_rows")
    two = range(2)
    N = S // 2
    step, fixed = a.sem("step"), a.sem("fixed")
    xd = [a.sb(f"xd{b}", [P, GROUP, C]) for b in two]
    att = [a.sb(f"att{b}", [P, GROUP, C]) for b in two]
    att_t = [a.sb(f"att_t{b}", [C, GE]) for b in two]
    y = [a.sb(f"y{b}", [P, GROUP, C]) for b in two]
    sq = [a.sb(f"sq{b}", [P, GROUP, C]) for b in two]
    stat = [a.sb(f"stat{b}", [P, 4, GROUP]) for b in two]
    res = [a.sb(f"res{b}", [P, GROUP, C]) for b in two]
    idx = [a.sb(f"idx{b}", [P, GROUP], I32) for b in two]
    eps = a.sb("eps", [P, 1])
    ps_t = [a.ps(f"ps_t{b}", [C, GE]) for b in two]
    ps_y = [a.ps(f"ps_y{b}", [P, GROUP, C]) for b in two]
    s = {n: a.sems(n) for n in ("xd_in", "att", "turned", "turned_sb", "proj", "y_made", "cen", "sq", "var", "dev",
                                "res", "scattered", "v_step")}
    with nc.Block() as block:
        @block.sync
        def _(sp):
            with sp.Fori(0, N) as i:
                for b in two:
                    sp.wait_ge(s["y_made"][b], i)
                    sp.sem_inc(a.passed("sp"), 1)
                    sp.dma_start(xd[b][:, :, :], pay_rows[:, bass.ds(i * 2 * GROUP + b * GROUP, GROUP), XD:])\
                        .then_inc(s["xd_in"][b], 16)

        @block.tensor
        def _(pe):
            with pe.Fori(0, N) as i:
                for b in two:
                    pe.wait_ge(s["att"][b], i + 1)
                    pe.wait_ge(s["turned_sb"][b], i)
                    pe.sem_inc(a.passed("pe"), 1)
                    for q in range(GROUP):
                        ins = nc.tensor.transpose(ps_t[b][:, q * P:(q + 1) * P], att[b][:, q, :], k.ident[:, :])
                    ins.then_inc(s["turned"][b], 1)
                for b in two:
                    pe.wait_ge(s["turned_sb"][b], i + 1)
                    pe.wait_ge(s["y_made"][b], i)
                    for q in range(GROUP):
                        ins = nc.tensor.matmul(ps_y[b][:, q, :], att_t[b][:, q * P:(q + 1) * P], k.w_proj[:, :],
                                               start=True, stop=True)
                    ins.then_inc(s["proj"][b], 1)

        @block.scalar
        def _(act):
            with act.Fori(0, N) as i:
                for b in two:
                    act.wait_ge(s["turned"][b], i + 1)
                    act.wait_ge(s["proj"][b], i)
                    nc.scalar.activation(att_t[b][:, :], ps_t[b][:, :], ACT.Copy).then_inc(s["turned_sb"][b], 1)
                for b in two:
                    act.wait_ge(s["cen"][b], i + 1)
                    nc.scalar.activation(sq[b][:, :, :], y[b][:, :, :], ACT.Square).then_inc(s["sq"][b], 1)
                for b in two:
                    act.wait_ge(s["var"][b], i + 1)
                    nc.scalar.activation(stat[b][:, 2, :], stat[b][:, 1, :], ACT.Sqrt, bias=eps[:, 0:1],
                                         scale=1.0 / C).then_inc(s["dev"][b], 1)

        @block.vector
        def _(v):
            st = Steps(v, step)
            nc.vector.memset(eps[:, :], EPS)
            st.link(nc.vector.tensor_tensor(carry[:, 0:C + HEADS], carry[:, 0:C + HEADS], factor[:, :], ALU.mult))
            with v.Fori(0, (C + HEADS) // 4) as f:
                for q in range(4):
                    col = V[:, :, bass.ds(f * 4 + q, 1)].rearrange("p t o -> p (t o)")
                    nc.vector.scalar_tensor_tensor(col, g.end_lead[:, :], carry[:, bass.ds(f * 4 + q, 1)], col,
                                                   ALU.mult, ALU.add)
            st.link(nc.vector.memset(tail[:, 0:1], 0.0))
            st.did(nc.vector.tensor_scalar(at65[:, :], g.at[:, :], float(XW), None, ALU.mult))
            st.link(nc.vector.tensor_scalar(rden[:, :, :], V[:, :, C:C + HEADS], 1e-16, None, ALU.add))
            st.link(nc.vector.reciprocal(rden[:, :, :], rden[:, :, :]))

            def weigh(b, n):
                at = n * 2 * GROUP + b * GROUP
                v.wait_ge(s["turned"][b], n)
                for h in range(HEADS):
                    cols = slice(h * HD, (h + 1) * HD)
                    ins = nc.vector.tensor_tensor(att[b][:, :, cols], V[:, bass.ds(at, GROUP), cols],
                                                  rden[:, bass.ds(at, GROUP), h:h + 1].to_broadcast([P, GROUP, HD]),
                                                  ALU.mult)
                ins.then_inc(s["att"][b], 1)

            for b in two:
                weigh(b, 0)

            def rows(i, more):
                base = [Steps(v, s["v_step"][b], i * 4) for b in two]
                for b in two:
                    v.wait_ge(s["proj"][b], i + 1)
                    v.wait_ge(s["xd_in"][b], i * 16 + 16)
                    v.wait_ge(s["res"][b], i)
                    nc.vector.tensor_tensor(y[b][:, :, :], ps_y[b][:, :, :], xd[b][:, :, :], ALU.add)\
                        .then_inc(s["y_made"][b], 1)
                for b in two:
                    v.wait_ge(s["y_made"][b], i + 1)
                    base[b].did(nc.vector.tensor_tensor(y[b][:, :, :], y[b][:, :, :], k.b_proj[:, :, :], ALU.add))
                for b in two:
                    base[b].settle()
                    base[b].did(nc.vector.tensor_reduce(stat[b][:, 0, :], y[b][:, :, :], AX, ALU.add))
                for b in two:
                    base[b].settle()
                    base[b].did(nc.vector.tensor_scalar(stat[b][:, 0, :], stat[b][:, 0, :], 1.0 / C, None, ALU.mult))
                for b in two:
                    base[b].settle()
                    nc.vector.tensor_tensor(y[b][:, :, :], y[b][:, :, :],
                                            stat[b][:, 0, :].unsqueeze(2).to_broadcast([P, GROUP, C]),
                                            ALU.subtract).then_inc(s["cen"][b], 1)
                if more:
                    for b in two:
                        weigh(b, i + 1)
                for b in two:
                    v.wait_ge(s["sq"][b], i + 1)
                    nc.vector.tensor_reduce(stat[b][:, 1, :], sq[b][:, :, :], AX, ALU.add).then_inc(s["var"][b], 1)
                for b in two:
                    at = i * 2 * GROUP + b * GROUP
                    v.wait_ge(s["dev"][b], i + 1)
                    base[b].did(nc.vector.reciprocal(stat[b][:, 3, :], stat[b][:, 2, :]))
                    v.wait_ge(s["scattered"][b], i * GROUP * 16)
                    nc.vector.tensor_scalar(idx[b][:, :], at65[:, bass.ds(at, GROUP)], 1.0, None, ALU.mult)
                    base[b].settle()
                    nc.vector.tensor_tensor(res[b][:, :, :], y[b][:, :, :],
                                            stat[b][:, 3, :].unsqueeze(2).to_broadcast([P, GROUP, C]),
                                            ALU.mult).then_inc(s["res"][b], 1)

            with v.Fori(0, N - 1) as i:
                rows(i, True)
            rows(N - 1, False)

        @block.gpsimd
        def _(gp):
            with gp.Fori(0, N) as i:
                for b in two:
                    gp.wait_ge(s["res"][b], i + 1)
                    gp.sem_inc(a.passed("pool"), 1)
                    for q in range(GROUP):
                        gp.indirect_dma_start(out=k.d_xt,
                                              out_offset=bass.IndirectOffsetOnAxis(ap=idx[b][:, q:q + 1], axis=0),
                                              in_=res[b][:, q, :], in_offset=None).then_inc(s["scattered"][b], 16)
            for b in two:
                gp.wait_ge(s["scattered"][b], N * GROUP * 16)
    a.close()
    m.close()


def layers(nc, k, d, io):
    T, S = d["T"], d["S"]
    m = Pool2(nc, "lay")
    two = range(2)
    N = S // 2
    CH = 7
    TC = T // CH
    g = Segments(m, T)
    rec = m.sb("rec", [P, T, 2], I32)
    nbr = m.sb("nbr", [P, T])
    G = m.sb("gathered", [P, T, XW])
    inv_deg = m.sb("inv_deg", [P, T])
    inv_row = m.sb("inv_row", [P, 1])
    joins_w = m.sb("joins_w", [P, C])
    joins_c = m.sb("joins_c", [P, C])
    carry = m.sb("carry", [P, C])
    tail = m.sb("tail", [P, C])
    tmp = m.sb("tmp", [P, T])

    a = Pool2(nc, "lay_load")
    loaded, keyed = a.sem("loaded"), a.sem("keyed")
    with nc.Block() as block:
        @block.sync
        def _(sp):
            sp.dma_start(rec[:, :, :], k.d_rec_sorted.rearrange("(p t) c -> p t c", t=T)).then_inc(loaded, 16)

        @block.vector
        def _(v):
            v.wait_ge(loaded, 16)
            nc.vector.tensor_copy(g.key[:, :], rec[:, :, 0])
            nc.vector.tensor_copy(nbr[:, :], rec[:, :, 1]).then_inc(keyed, 1)
    a.close()
    segments(nc, k, d, g, "src")

    a = Pool2(nc, "lay_deg")
    step = a.sem("step")
    with nc.Block() as block:
        @block.vector
        def _(v):
            st = Steps(v, step)
            st.did(nc.vector.tensor_tensor_scan(inv_deg[:, :], g.cont[:, :], k.ones[:, 0:T], 0.0, ALU.mult, ALU.add))
            st.did(nc.vector.tensor_tensor(joins_w[:, 0:1], g.joins[:, :], g.whole[:, :], ALU.mult))
            st.settle()
            st.did(nc.vector.tensor_scalar(joins_w[:, 1:C], k.ones[:, 1:C], joins_w[:, 0:1], None, ALU.mult))
            st.did(nc.vector.tensor_scalar(joins_c[:, :], k.ones[:, 0:C], g.joins[:, 0:1], None, ALU.mult))
            st.did(nc.vector.tensor_scalar(tail[:, :], k.ones[:, 0:C], inv_deg[:, T - 1:T], None, ALU.mult))
            st.settle()
    a.close()
    hand_over(nc, k, "deg", C, tail[:, :], carry[:, :], ALU.add, joins_w[:, :])
    a = Pool2(nc, "lay_inv")
    step = a.sem("step")
    with nc.Block() as block:
        @block.vector
        def _(v):
            st = Steps(v, step)
            st.link(nc.vector.tensor_tensor(carry[:, :], carry[:, :], joins_c[:, :], ALU.mult))
            st.link(nc.vector.scalar_tensor_tensor(inv_deg[:, :], g.lead[:, :], carry[:, 0:1], inv_deg[:, :],
                                                   ALU.mult, ALU.add))
            st.link(nc.vector.reciprocal(inv_deg[:, :], inv_deg[:, :]))
            st.link(nc.vector.tensor_tensor(tmp[:, :], inv_deg[:, :], g.end_lead[:, :], ALU.mult))
            st.link(nc.vector.tensor_reduce(inv_row[:, :], tmp[:, :], AX, ALU.add))
    a.close()

    xt_rows = k.d_xt.rearrange("(a b) o -> a (b o)", b=XW)[0:d["N_PAD"], :]
    for layer in range(3):
        first = layer == 0
        width = XW if first else C
        table = xt_rows if first else k.d_z[layer - 1]
        z = k.d_z[layer]
        z_rows = z[0:d["E_PAD"], :].rearrange("(p t) c -> p t c", t=T)
        a = Pool2(nc, f"lay{layer}")
        idx = [a.sb(f"idx{b}", [P, GROUP], I32) for b in two]
        got = [a.sb(f"got{b}", [P, GROUP, width]) for b in two]
        ends = a.sb("ends", [P, CH + 1, C])
        s = {n: a.sems(n) for n in ("idx", "gathered", "copied")}
        step, scaled, stored = a.sem("step"), a.sem("scaled"), a.sem("stored")
        with nc.Block() as block:
            @block.gpsimd
            def _(gp):
                with gp.Fori(0, N) as i:
                    for b in two:
                        gp.wait_ge(s["idx"][b], i + 1)
                        gp.wait_ge(s["copied"][b], i)
                        gp.sem_inc(a.passed("pool"), 1)
                        for q in range(GROUP):
                            gp.indirect_dma_start(out=got[b][:, q, :], out_offset=None, in_=table,
                                                  in_offset=bass.IndirectOffsetOnAxis(ap=idx[b][:, q:q + 1], axis=0),
                                                  ).then_inc(s["gathered"][b], 16)

            @block.scalar
            def _(act):

                def indices(b, n):
                    at = n * 2 * GROUP + b * GROUP
                    act.wait_ge(s["gathered"][b], n * GROUP * 16)
                    act.sem_inc(a.passed("act"), 1)
                    nc.scalar.activation(idx[b][:, :], nbr[:, bass.ds(at, GROUP)], ACT.Copy).then_inc(s["idx"][b], 1)

                def copy(b, n):
                    at = n * 2 * GROUP + b * GROUP
                    act.wait_ge(s["gathered"][b], n * GROUP * 16 + GROUP * 16)
                    act.sem_inc(a.passed("act"), 1)
                    nc.scalar.activation(G[:, bass.ds(at, GROUP), 0:width], got[b][:, :, :], ACT.Copy)\
                        .then_inc(s["copied"][b], 1)

                for b in two:
                    indices(b, 0)
                with act.Fori(0, N - 1) as i:
                    for b in two:
                        indices(b, i + 1)
                        copy(b, i)
                for b in two:
                    copy(b, N - 1)

            @block.vector
            def _(v):
                st = Steps(v, step)
                st.did(nc.vector.memset(ends[:, 0, :], 0.0))
                for c in range(CH):
                    lo = c * TC
                    groups = (c + 1) * TC // GROUP
                    for b in two:
                        v.wait_ge(s["copied"][b], (groups + 1 - b) // 2)
                    st.settle()
                    with v.Fori(0, C // 4) as f:
                        for q in range(4):
                            col = G[:, lo:lo + TC, bass.ds(f * 4 + q, 1)].rearrange("p t o -> p (t o)")
                            nc.vector.tensor_tensor_scan(col, g.cont[:, lo:lo + TC], col, ends[:, c, bass.ds(f * 4 + q, 1)],
                                                         ALU.mult, ALU.add)
                    st.link(nc.vector.memset(tmp[:, 0:1], 0.0))
                    st.link(nc.vector.tensor_copy(ends[:, c + 1, :], G[:, lo + TC - 1, 0:C]))
                    nc.vector.tensor_tensor(G[:, lo:lo + TC, 0:C], G[:, lo:lo + TC, 0:C],
                                            inv_deg[:, lo:lo + TC].unsqueeze(2).to_broadcast([P, TC, C]), ALU.mult)\
                        .then_inc(scaled, 1)
                nc.vector.tensor_copy(tail[:, :], ends[:, CH, :])
                if first:
                    nc.vector.tensor_copy(nbr[:, :], G[:, :, C])

            @block.sync
            def _(sp):
                for c in range(CH):
                    sp.wait_ge(scaled, c + 1)
                    sp.dma_start(z_rows[:, c * TC:(c + 1) * TC, :], G[:, c * TC:(c + 1) * TC, 0:C])\
                        .then_inc(stored, 16)
                sp.wait_ge(stored, 16 * CH)
        a.close()
        hand_over(nc, k, f"lay{layer}", C, tail[:, :], carry[:, :], ALU.add, joins_w[:, :])
        a = Pool2(nc, f"fix{layer}")
        row = a.sb("row", [P, C])
        got, step, done = a.sem("got"), a.sem("step"), a.sem("done")
        with nc.Block() as block:
            @block.gpsimd
            def _(gp):
                gp.indirect_dma_start(out=row[:, :], out_offset=None, in_=z[0:d["E_PAD"], :],
                                      in_offset=bass.IndirectOffsetOnAxis(ap=g.row[:, 0:1], axis=0)).then_inc(got, 16)
                gp.wait_ge(step, 3)
                gp.sem_inc(a.passed("pool"), 1)
                gp.indirect_dma_start(out=z, out_offset=bass.IndirectOffsetOnAxis(ap=g.row[:, 0:1], axis=0),
                                      in_=row[:, :], in_offset=None).then_inc(done, 16)
                gp.wait_ge(done, 16)

            @block.vector
            def _(v):
                st = Steps(v, step)
                st.link(nc.vector.tensor_tensor(carry[:, :], carry[:, :], joins_c[:, :], ALU.mult))
                st.link(nc.vector.tensor_scalar(carry[:, :], carry[:, :], inv_row[:, 0:1], None, ALU.mult))
                v.wait_ge(got, 16)
                st.did(nc.vector.tensor_tensor(row[:, :], row[:, :], carry[:, :], ALU.add))
        a.close()

    a = Pool2(nc, "sums")
    zin = [[a.sb(f"z{b}{n}", [P, GROUP, C]) for n in range(3)] for b in two]
    idx = [a.sb(f"idx{b}", [P, GROUP], I32) for b in two]
    s = {n: a.sems(n) for n in ("in", "part", "sum", "scattered")}
    with nc.Block() as block:
        @block.sync
        def _(sp):
            with sp.Fori(0, N) as i:
                for b in two:
                    at = i * 2 * GROUP + b * GROUP
                    sp.wait_ge(s["scattered"][b], i * GROUP * 16)
                    sp.sem_inc(a.passed("sp"), 1)
                    for n in range(3):
                        rows = k.d_z[n][0:d["E_PAD"], :].rearrange("(p t) c -> p t c", t=T)
                        sp.dma_start(zin[b][n][:, :, :], rows[:, bass.ds(at, GROUP), :]).then_inc(s["in"][b], 16)

        @block.vector
        def _(v):
            with v.Fori(0, N) as i:
                for b in two:
                    at = i * 2 * GROUP + b * GROUP
                    z0, z1, z2 = (zin[b][n][:, :, :] for n in range(3))
                    v.wait_ge(s["in"][b], i * 48 + 48)
                    nc.vector.tensor_tensor(z0, z0, z1, ALU.add).then_inc(s["part"][b], 1)
                    v.wait_ge(s["part"][b], i + 1)
                    nc.vector.tensor_scalar(idx[b][:, :], g.at[:, bass.ds(at, GROUP)], 1.0, None, ALU.mult)
                    nc.vector.tensor_tensor(z0, z0, z2, ALU.add).then_inc(s["sum"][b], 1)

        @block.gpsimd
        def _(gp):
            with gp.Fori(0, N) as i:
                for b in two:
                    gp.wait_ge(s["sum"][b], i + 1)
                    gp.sem_inc(a.passed("pool"), 1)
                    for q in range(GROUP):
                        gp.indirect_dma_start(out=k.d_acc,
                                              out_offset=bass.IndirectOffsetOnAxis(ap=idx[b][:, q:q + 1], axis=0),
                                              in_=zin[b][0][:, q, :], in_offset=None).then_inc(s["scattered"][b], 16)
            for b in two:
                gp.wait_ge(s["scattered"][b], N * GROUP * 16)
    a.close()
    m.close()


def build(nc, d, io):
    k = Pool2(nc, "k")
    N_PAD, E_PAD, T = d["N_PAD"], d["E_PAD"], d["T"]
    k.d_xt = nc.dram_tensor("node_table", ((N_PAD + E_PAD) * XW, 1), F32).ap()
    k.d_acc = nc.dram_tensor("layer_sums", (N_PAD + E_PAD, C), F32).ap()
    k.d_z = [nc.dram_tensor(f"layer_{n}", (E_PAD + P, C), F32).ap() for n in range(3)]
    k.d_pay_sorted = nc.dram_tensor("payload_sorted", (E_PAD, PAY), F32).ap()
    k.d_rec_sorted = nc.dram_tensor("edges_sorted", (E_PAD, 2), I32).ap()
    setup(nc, k, d, io)
    histograms(nc, k, d)
    nodes_dense(nc, k, d, io, final=False)
    messages(nc, k, d, io)
    positions(nc, k, d, "dst", k.d_pay, PAY, F32, k.d_pay_sorted)
    positions(nc, k, d, "src", io["rec"], 2, I32, k.d_rec_sorted)
    attention(nc, k, d, io)
    layers(nc, k, d, io)
    nodes_dense(nc, k, d, io, final=True)
    k.close()


_WEIGHTS = ("Wq", "bq", "W_src", "b_src", "W_dst", "W_fc1", "b_fc1", "W_fc2", "b_fc2", "W_fc3", "b_fc3",
            "W_kv", "b_kv", "W_proj", "b_proj")


def dims(n_nodes, n_edges):
    unit = KEYS_PER_PART * P // 128
    hp = -(-(n_nodes + 1) // unit)
    while (hp * KEYS_PER_PART) % (P * 28) or (hp * KEYS_PER_PART // P) % 56:
        hp += 1
    t = -(-n_edges // P)
    t = -(-t // 56) * 56
    n_pad = hp * KEYS_PER_PART
    return {"N": n_nodes, "E": n_edges, "HP": hp, "N_PAD": n_pad, "T": t, "E_PAD": t * P, "S": t // GROUP,
            "R": n_pad // P, "J": 28}


def layout(inputs, d):
    import numpy as np
    x = np.asarray(inputs["x"])
    xp = np.zeros((d["N_PAD"], C), x.dtype)
    xp[:d["N"]] = x
    arrays = {"x": xp}
    pads = {}
    for key in ("src", "dst"):
        e = np.full((d["E_PAD"],), d["N"], np.int32)
        e[:d["E"]] = np.asarray(inputs[key])
        pads[key] = e.reshape(P, d["T"])
        arrays[f"{key}_pt"] = pads[key]
        arrays[f"{key}_tp"] = np.ascontiguousarray(pads[key].T).reshape(d["S"], GE)
    arrays["rec"] = np.ascontiguousarray(np.stack([pads["src"], pads["dst"]], axis=-1))
    ea = np.zeros((d["E_PAD"], C), x.dtype)
    ea[:d["E"]] = np.asarray(inputs["edge_attr_64"])
    arrays["ea"] = ea.reshape(P, d["T"], C)
    ew = np.zeros((d["E_PAD"],), x.dtype)
    ew[:d["E"]] = np.asarray(inputs["edge_weight1"])[:, 0]
    arrays["ew"] = ew.reshape(P, d["T"])
    for w in _WEIGHTS:
        arrays[w] = np.ascontiguousarray(np.asarray(inputs[f"L0_gnn_{w}"]))
    return arrays


def kernel(**inputs):
    import concourse.bacc as _bacc
    from concourse import mybir as _mybir
    from concourse.bass_utils import run_bass_kernel_spmd as _run

    d = dims(inputs["x"].shape[0], inputs["src"].shape[0])
    arrays = layout(inputs, d)
    nc = _bacc.Bacc("TRN2", target_bir_lowering=False, num_devices=1)
    io = {n: nc.dram_tensor(f"in_{n}", a.shape, _mybir.dt.from_np(a.dtype), kind="ExternalInput").ap()
          for n, a in arrays.items()}
    io["out"] = nc.dram_tensor("out_rows", (d["N_PAD"], C), F32, kind="ExternalOutput").ap()
    build(nc, d, io)
    r = _run(nc, [{f"in_{n}": a for n, a in arrays.items()}], core_ids=[0])
    return r.results[0]["out_rows"][:d["N"]]
```

```python
import concourse.bass as bass
from concourse import mybir
from contextlib import ExitStack

F32, F16, I32 = mybir.dt.float32, mybir.dt.float16, mybir.dt.int32
ALU = mybir.AluOpType
ACT = mybir.ActivationFunctionType
AX = mybir.AxisListType.X

P = 128
C = 64
HEADS, HD = 4, 16
GROUP = 4
GE = GROUP * P
LO = 256
BLK = 4
KEYS_PER_PART = BLK * LO
PAY = 136
V_W = 69
XD = 72
XW = 65
EPS = 1e-5
BIG = 1e37


class Pool2:

    def __init__(self, nc, tag):
        self.nc, self.tag, self.stack, self.marks = nc, tag, ExitStack(), {}
        self.counters = []

    def sb(self, name, shape, dt=F32):
        return self.stack.enter_context(self.nc.sbuf_tensor(f"{self.tag}_{name}", shape, dt))

    def ps(self, name, shape, dt=F32):
        return self.stack.enter_context(self.nc.psum_tensor(f"{self.tag}_{name}", shape, dt))

    def sem(self, name):
        self.counters.append(self.nc.alloc_semaphore(f"{self.tag}_{name}"))
        return self.counters[-1]

    def sems(self, name, n=2):
        return [self.sem(f"{name}{k}") for k in range(n)]

    def passed(self, engine):
        if engine not in self.marks:
            self.marks[engine] = self.sem(f"passed_{engine}")
        return self.marks[engine]

    def close(self):
        self.stack.close()
        if self.counters:
            self.nc.clear_and_free_semaphores(self.counters)
            self.nc.all_engine_barrier()


class Steps:

    def __init__(self, eng, sem, base=0):
        self.eng, self.sem, self.base, self.n = eng, sem, base, 0

    def did(self, ins):
        ins.then_inc(self.sem, 1)
        self.n += 1

    def settle(self):
        self.eng.wait_ge(self.sem, self.base + self.n)

    def link(self, ins):
        self.did(ins)
        self.settle()


def need(eng, sem, value):
    if not (isinstance(value, int) and value == 0):
        eng.wait_ge(sem, value)


def repeat(eng, n, body):
    body(0)
    if n > 1:
        with eng.Fori(1, n) as i:
            body(i)


def setup(nc, k, d, io):
    T, HP, S = d["T"], d["HP"], d["S"]
    k.ident = k.sb("ident", [P, P])
    k.iota_lo = k.sb("iota_lo", [P, LO], F16)
    k.iota_hi = k.sb("iota_hi", [P, BLK, HP], F16)
    k.hi_of_part = k.sb("hi_of_part", [P, BLK])
    k.below = k.sb("below", [P, P])
    k.earlier = k.sb("earlier", [P, GE], F16)
    k.ones = k.sb("ones", [P, KEYS_PER_PART])
    k.place = k.sb("place", [P, T])
    k.w_kvx = k.sb("w_kvx", [P, 2, P])
    k.w_out = k.sb("w_out", [P, 2, 3 * C])
    k.w_fc = k.sb("w_fc", [P, 3, P])
    k.w_proj = k.sb("w_proj", [C, C])
    k.b_col = k.sb("b_col", [P, 4])
    k.b_kv = k.sb("b_kv", [P, 2 * C])
    k.b_q = k.sb("b_q", [P, GROUP, C])
    k.b_proj = k.sb("b_proj", [P, GROUP, C])
    k.key = {key: k.sb(f"key_{key}", [P, T]) for key in ("dst", "src")}
    k.ew = k.sb("ew", [P, T])
    k.unsorted = k.sb("unsorted", [1, 1], I32)
    k.digits = {}

    t = Pool2(nc, "setup")
    ki = t.sb("ki", [P, 2, T], I32)
    drop = t.sb("drop", [P, T])
    after = t.sb("after", [P, 1])
    drops = t.sb("drops", [P, 4])
    tri = t.sb("tri", [P, P])
    ps = t.ps("ps", [P, 8])
    loaded, wl, made, v_step, shifted, keyed, counted, summed = (
        t.sem(n) for n in ("loaded", "weights", "made", "v_step", "shifted", "keyed", "counted", "summed"))
    n_weights = 1 + 4 + 4 + 6 + 1 + 8 + 1 + 2 * GROUP
    with nc.Block() as block:
        @block.sync
        def _(sp):
            for n, key in enumerate(("dst", "src")):
                sp.dma_start(ki[:, n, :], io[f"{key}_pt"]).then_inc(loaded, 16)
            sp.dma_start(k.ew[:, :], io["ew"]).then_inc(wl, 16)
            sp.wait_ge(made, 1)
            up, low = slice(0, C), slice(C, P)
            for w, to in (("W_src", k.w_kvx[up, 0, 0:C]), ("W_dst", k.w_kvx[low, 0, 0:C]),
                          ("W_dst", k.w_kvx[up, 1, C:P]), ("W_src", k.w_kvx[low, 1, C:P]),
                          ("W_kv", k.w_out[up, 0, 0:2 * C]), ("Wq", k.w_out[low, 0, 2 * C:3 * C]),
                          ("W_kv", k.w_out[low, 1, 0:2 * C]), ("Wq", k.w_out[up, 1, 2 * C:3 * C])):
                sp.dma_start(to, io[w]).then_inc(wl, 16)
            for n in range(3):
                for half in (up, low):
                    sp.dma_start(k.w_fc[half, n, half], io[f"W_fc{n + 1}"]).then_inc(wl, 16)
            sp.dma_start(k.w_proj[:, :], io["W_proj"]).then_inc(wl, 16)
            with nc.allow_non_contiguous_dma(reason="one bias or key per partition"):
                for n, b in enumerate(("b_fc1", "b_fc2", "b_fc3", "b_src")):
                    for half in (up, low):
                        sp.dma_start(k.b_col[half, n:n + 1], io[b].rearrange("(c o) -> c o", o=1)).then_inc(wl, 16)
                sp.wait_ge(keyed, 1)
                sp.dma_start(after[0:P - 1, :], k.key["dst"][1:P, 0:1]).then_inc(shifted, 16)
            sp.dma_start(k.b_kv[:, :], io["b_kv"].partition_broadcast(P)).then_inc(wl, 16)
            for g in range(GROUP):
                sp.dma_start(k.b_q[:, g, :], io["bq"].partition_broadcast(P)).then_inc(wl, 16)
                sp.dma_start(k.b_proj[:, g, :], io["b_proj"].partition_broadcast(P)).then_inc(wl, 16)

        @block.gpsimd
        def _(g):
            nc.gpsimd.memset(k.w_kvx[:, :, :], 0.0)
            nc.gpsimd.memset(k.w_fc[:, :, :], 0.0)
            nc.gpsimd.memset(k.w_out[:, :, :], 0.0).then_inc(made, 1)
            nc.gpsimd.memset(k.ident[:, :], 0.0)
            nc.gpsimd.memset(k.ones[:, :], 1.0)
            nc.gpsimd.memset(tri[:, :], 1.0).then_inc(made, 1)
            nc.gpsimd.iota(k.iota_lo[:, :], pattern=[[1, LO]], base=0, channel_multiplier=0,
                           allow_small_or_imprecise_dtypes=True)
            nc.gpsimd.iota(k.iota_hi[:, :, :], pattern=[[1, BLK], [BLK, HP]], base=0, channel_multiplier=0,
                           allow_small_or_imprecise_dtypes=True)
            nc.gpsimd.iota(k.hi_of_part[:, :], pattern=[[1, BLK]], base=0, channel_multiplier=BLK,
                           allow_small_or_imprecise_dtypes=True)
            nc.gpsimd.iota(k.place[:, :], pattern=[[1, T]], base=0, channel_multiplier=T,
                           allow_small_or_imprecise_dtypes=True)
            nc.gpsimd.memset(k.earlier[:, :], 1.0).then_inc(made, 1)
            g.wait_ge(made, 3)
            nc.gpsimd.affine_select(out=k.ident[:, :], in_=k.ident[:, :], compare_op=ALU.not_equal, fill=1.0,
                                    base=0, pattern=[[-1, P]], channel_multiplier=1)
            nc.gpsimd.affine_select(out=k.below[:, :], in_=tri[:, :], compare_op=ALU.is_gt, fill=0.0,
                                    base=0, pattern=[[1, P]], channel_multiplier=-1)
            last = k.earlier[:, GE - P:GE]
            nc.gpsimd.affine_select(out=last, in_=last, compare_op=ALU.is_gt, fill=0.0,
                                    base=0, pattern=[[-1, P]], channel_multiplier=1).then_inc(made, 1)

        @block.tensor
        def _(pe):
            pe.wait_ge(counted, 1)
            pe.wait_ge(made, 3)
            nc.tensor.matmul(ps[0:1, 0:4], k.ones[:, 0:1], drops[:, :], start=True, stop=True).then_inc(summed, 1)

        @block.vector
        def _(v):
            st = Steps(v, v_step)
            nc.vector.memset(after[:, :], float(d["N_PAD"]))
            nc.vector.memset(drops[:, :], 0.0)
            v.wait_ge(loaded, 32)
            nc.vector.tensor_copy(k.key["src"][:, :], ki[:, 1, :])
            nc.vector.tensor_copy(k.key["dst"][:, :], ki[:, 0, :]).then_inc(keyed, 1)
            v.wait_ge(keyed, 1)
            key = k.key["dst"]
            st.did(nc.vector.tensor_tensor(drop[:, 1:T], key[:, 0:T - 1], key[:, 1:T], ALU.is_gt))
            v.wait_ge(shifted, 16)
            st.link(nc.vector.tensor_tensor(drop[:, 0:1], key[:, T - 1:T], after[:, :], ALU.is_gt))
            nc.vector.tensor_reduce(drops[:, 0:1], drop[:, :], AX, ALU.add).then_inc(counted, 1)
            v.wait_ge(summed, 1)
            st.link(nc.vector.tensor_scalar(k.unsorted[:, :], ps[0:1, 0:1], 1.0, None, ALU.min))
            v.wait_ge(wl, 16 * n_weights)
            for half, n in ((slice(C, P), 0), (slice(0, C), 1)):
                wq = k.w_out[half, n, 2 * C:3 * C]
                nc.vector.tensor_scalar(wq, wq, HD ** -0.5, None, ALU.mult)
            st.link(nc.vector.tensor_scalar(k.b_q[:, :, :], k.b_q[:, :, :], HD ** -0.5, None, ALU.mult))
    t.close()
    digits(nc, k, k, d, io, "src")


class Digits:

    def __init__(self, nc, m, d, key):
        self.hi, self.lo = m.sb(f"hi_{key}", [P, d["T"]]), m.sb(f"lo_{key}", [P, d["T"]])
        self.start_hi = m.sb(f"start_hi_{key}", [d["HP"], KEYS_PER_PART], F16)
        self.start_lo = m.sb(f"start_lo_{key}", [d["HP"], KEYS_PER_PART], F16)
        self.hi_rows = nc.dram_tensor(f"hi_rows_{key}", (d["S"], GE), F16).ap()
        self.key_rows = nc.dram_tensor(f"key_rows_{key}", (d["S"], GE), F32).ap()


def digits(nc, k, m, d, io, key):
    T, S = d["T"], d["S"]
    k.digits[key] = g = Digits(nc, m, d, key)
    t = Pool2(nc, f"dig_{key}")
    ki = t.sb("ki", [P, T], I32)
    ti = t.sb("ti", [S, GE], I32)
    dig = t.sb("dig", [P, 2, T], I32)
    tdig = t.sb("tdig", [S, GE], I32)
    hi16 = t.sb("hi16", [S, GE], F16)
    kf = t.sb("kf", [S, GE])
    loaded, step, stored = t.sem("loaded"), t.sem("step"), t.sem("stored")
    with nc.Block() as block:
        @block.sync
        def _(sp):
            sp.dma_start(ki[:, :], io[f"{key}_pt"]).then_inc(loaded, 16)
            sp.dma_start(ti[:, :], io[f"{key}_tp"]).then_inc(loaded, 16)
            sp.wait_ge(step, 2)
            sp.dma_start(g.hi_rows, hi16[:, :]).then_inc(stored, 16)
            sp.dma_start(g.key_rows, kf[:, :]).then_inc(stored, 16)
            sp.wait_ge(stored, 32)

        @block.vector
        def _(v):
            st = Steps(v, step)
            v.wait_ge(loaded, 32)
            nc.vector.tensor_scalar(dig[:, 0, :], ki[:, :], 8, None, ALU.logical_shift_right)
            nc.vector.tensor_copy(kf[:, :], ti[:, :])
            nc.vector.tensor_scalar(dig[:, 1, :], ki[:, :], LO - 1, None, ALU.bitwise_and)
            st.link(nc.vector.tensor_scalar(tdig[:, :], ti[:, :], 8, None, ALU.logical_shift_right))
            st.link(nc.vector.tensor_copy(hi16[:, :], tdig[:, :]))
            nc.vector.tensor_copy(g.hi[:, :], dig[:, 0, :])
            nc.vector.tensor_copy(g.lo[:, :], dig[:, 1, :])
    t.close()


def one_hots(nc, k, g, at, lo_out, hi_out):
    nc.vector.tensor_scalar(lo_out, k.iota_lo[:, :], g.lo[:, bass.ds(at, 1)], None, ALU.is_equal)
    return nc.vector.tensor_scalar(hi_out, k.iota_hi[:, :, :], g.hi[:, bass.ds(at, 1)], None, ALU.is_equal)


class Counting:

    H = 14

    def __init__(self, nc, k, t, d, key):
        self.nc, self.k, self.g = nc, k, k.digits[key]
        self.lo1 = t.sb("count_lo", [P, self.H, LO], F16)
        self.hi1 = t.sb("count_hi", [P, self.H, BLK, d["HP"]], F16)
        self.table = t.ps("table", [d["HP"], KEYS_PER_PART])
        self.hot, self.used = t.sem("count_hot"), t.sem("count_used")

    def vector(self, v, i):
        for j in range(self.H):
            if not isinstance(i, int) or i > 0:
                v.wait_ge(self.used, i * self.H + (j + 1 - self.H))
            one_hots(self.nc, self.k, self.g, i * self.H + j, self.lo1[:, j, :], self.hi1[:, j, :, :])\
                .then_inc(self.hot, 1)

    def tensor(self, pe, i, lo, hi):
        for j in range(lo, hi):
            pe.wait_ge(self.hot, i * self.H + j + 1)
            for q in range(BLK):
                ins = self.nc.tensor.matmul(self.table[:, q * LO:(q + 1) * LO], self.hi1[:, j, q, :],
                                            self.lo1[:, j, :], start=False, stop=False, skip_group_check=True)
            ins.then_inc(self.used, 1)


def first_places(nc, k, t, d, key, counts, store_last):
    HP = d["HP"]
    g = k.digits[key]
    base = t.ps("base", [HP, 8])
    count = t.sb("count", [HP, KEYS_PER_PART])
    run = t.sb("run", [HP, KEYS_PER_PART])
    start = t.sb("start", [HP, KEYS_PER_PART])
    off = t.sb("off", [HP, 8])
    totals, based, step, last_ready, out_s = (t.sem(n) for n in ("totals", "based", "step", "last_ready", "out"))
    with nc.Block() as block:
        @block.vector
        def _(v):
            st = Steps(v, step)
            nc.vector.memset(off[:, :], 0.0)
            st.link(nc.vector.tensor_copy(count[:, :], counts[:, :]))
            st.link(nc.vector.tensor_tensor_scan(run[:, :], k.ones[0:HP, :], count[:, :], 0.0, ALU.mult, ALU.add))
            nc.vector.tensor_copy(off[:, 0:1], run[:, KEYS_PER_PART - 1:KEYS_PER_PART]).then_inc(totals, 1)
            st.did(nc.vector.tensor_tensor(start[:, :], run[:, :], count[:, :], ALU.subtract))
            v.wait_ge(based, 1)
            st.link(nc.vector.tensor_copy(off[:, 1:2], base[:, 0:1]))
            st.link(nc.vector.tensor_scalar(start[:, :], start[:, :], off[:, 1:2], None, ALU.add))
            st.link(nc.vector.tensor_copy(g.start_hi[:, :], start[:, :]))
            st.link(nc.vector.tensor_tensor(g.start_lo[:, :], start[:, :], g.start_hi[:, :], ALU.subtract))
            if store_last:
                st.link(nc.vector.tensor_tensor(run[:, :], start[:, :], count[:, :], ALU.add))
                st.link(nc.vector.tensor_scalar(count[:, :], count[:, :], 1.0, None, ALU.min))
                st.link(nc.vector.scalar_tensor_tensor(run[:, :], run[:, :], -1.0 - d["E_PAD"], count[:, :],
                                                       ALU.add, ALU.mult))
                nc.vector.tensor_scalar(run[:, :], run[:, :], float(d["E_PAD"]), None, ALU.add)\
                    .then_inc(last_ready, 1)

        @block.tensor
        def _(pe):
            pe.wait_ge(totals, 1)
            nc.tensor.matmul(base[:, 0:1], k.below[0:HP, 0:HP], off[:, 0:1], start=True, stop=True)\
                .then_inc(based, 1)

        @block.sync
        def _(sp):
            if store_last:
                sp.wait_ge(last_ready, 1)
                sp.dma_start(k.d_last, run[:, :]).then_inc(out_s, 16)
                sp.wait_ge(out_s, 16)


class Messages:

    def __init__(self, nc, k, t, d, io):
        two = range(2)
        self.nc, self.k, self.t, self.io, self.N = nc, k, t, io, d["S"] // 2
        self.idx = [t.sb(f"idx{b}", [P, 2, GROUP], I32) for b in two]
        self.xg = [t.sb(f"xg{b}", [P, GROUP, 2 * C]) for b in two]
        self.xt = [t.sb(f"xt{b}", [P, GE]) for b in two]
        self.ea = t.sb("ea", [P, GE])
        self.h1, self.h2, self.w3 = (t.sb(n, [P, GE]) for n in ("h1", "h2", "w3"))
        self.pay = [t.sb(f"pay{b}", [P, GROUP, C + PAY]) for b in two]
        self.qb = [t.sb(f"qb{b}", [P, GROUP, C]) for b in two]
        self.ps_x = [t.ps(f"ps_x{b}", [P, GE]) for b in two]
        self.ps_e = t.ps("ps_e", [P, GE])
        self.ps_o = t.ps("ps_o", [P, 2, GE])
        self.s = {n: t.sems(n) for n in ("idx_in", "gathered", "x_used", "xT", "xT_sb", "tp", "out_ps", "step",
                                         "pay_ready", "stored")}
        self.e = {n: t.sem(n) for n in ("ea_in", "h1_ps", "h1_sb", "h2_ps", "h2_sb", "w_ps", "w_sb", "kv_ps")}
        self.init = t.sem("init")

    def src_half(self, b):
        return slice(0, C) if b == 0 else slice(C, P)

    def dst_half(self, b):
        return slice(C, P) if b == 0 else slice(0, C)

    def sync(self, sp, i):
        for b in range(2):
            at = i * 2 * GROUP + b * GROUP
            need(sp, self.s["gathered"][b], i * 2 * GROUP * 16)
            sp.sem_inc(self.t.passed("sp"), 1)
            for side, key in enumerate(("src", "dst") if b == 0 else ("dst", "src")):
                sp.dma_start(self.idx[b][:, side, :], self.io[f"{key}_pt"][:, bass.ds(at, GROUP)])\
                    .then_inc(self.s["idx_in"][b], 16)
        need(sp, self.e["h1_ps"], i)
        sp.sem_inc(self.t.passed("sp"), 1)
        sp.dma_start(self.ea[:, :], self.io["ea"][bass.ds(i, 1), :, :].rearrange("a p e -> p (a e)"))\
            .then_inc(self.e["ea_in"], 16)

    def gpsimd(self, g, i):
        for b in range(2):
            g.wait_ge(self.s["idx_in"][b], i * 32 + 32)
            need(g, self.s["x_used"][b], i)
            need(g, self.s["xT"][b], i)
            g.sem_inc(self.t.passed("pool"), 1)
            for side in range(2):
                for q in range(GROUP):
                    g.indirect_dma_start(
                        out=self.xg[b][:, q, side * C:(side + 1) * C], out_offset=None, in_=self.io["x"],
                        in_offset=bass.IndirectOffsetOnAxis(ap=self.idx[b][:, side, q:q + 1], axis=0),
                    ).then_inc(self.s["gathered"][b], 16)

    def tensor(self, pe, i, fill):
        nc, k, e, s = self.nc, self.k, self.e, self.s
        pe.wait_ge(e["ea_in"], i * 16 + 16)
        need(pe, e["w_sb"], i)
        nc.tensor.matmul(self.ps_e[:, :], k.w_fc[:, 0, :], self.ea[:, :], start=True, stop=True)\
            .then_inc(e["h1_ps"], 1)
        fill(0)
        pe.wait_ge(e["h1_sb"], i + 1)
        nc.tensor.matmul(self.ps_e[:, :], k.w_fc[:, 1, :], self.h1[:, :], start=True, stop=True)\
            .then_inc(e["h2_ps"], 1)
        fill(1)
        pe.wait_ge(e["h2_sb"], i + 1)
        nc.tensor.matmul(self.ps_e[:, :], k.w_fc[:, 2, :], self.h2[:, :], start=True, stop=True)\
            .then_inc(e["w_ps"], 1)
        fill(2)
        for b in range(2):
            pe.wait_ge(s["gathered"][b], i * 128 + 128)
            if b == 0:
                need(pe, s["tp"][1], i)
            for q in range(GROUP):
                ins = nc.tensor.transpose(self.ps_x[b][:, q * P:(q + 1) * P], self.xg[b][:, q, :], k.ident[:, :])
            ins.then_inc(s["xT"][b], 1)
        for b in range(2):
            pe.wait_ge(s["xT_sb"][b], i + 1)
            ins = nc.tensor.matmul(self.ps_x[0][:, :], k.w_kvx[:, b, :], self.xt[b][:, :], start=(b == 0),
                                   stop=(b == 1))
        ins.then_inc(e["kv_ps"], 1)
        for b in range(2):
            pe.wait_ge(s["tp"][b], i + 1)
            if b == 0:
                need(pe, s["pay_ready"][1], i)
            else:
                pe.wait_ge(s["pay_ready"][0], i + 1)
            for q in range(GROUP):
                ins = nc.tensor.matmul(self.out_tile(q, 0, 3 * C), self.xt[b][:, q * P:(q + 1) * P],
                                       k.w_out[:, b, :], start=True, stop=True)
            ins.then_inc(s["out_ps"][b], 1)

    def out_tile(self, q, lo, hi):
        return self.ps_o[:, q // 2, (q % 2) * 3 * C + lo:(q % 2) * 3 * C + hi]

    def store(self, act, i):
        for b in range(2):
            at = i * 2 * GROUP + b * GROUP
            act.wait_ge(self.s["pay_ready"][b], i + 1)
            act.sem_inc(self.t.passed("act"), 1)
            act.dma_start(self.k.d_pay_rows[:, bass.ds(at, GROUP), :], self.pay[b][:, :, C:])\
                .then_inc(self.s["stored"][b], 16)

    def scalar(self, act, i):
        nc, k, e, s = self.nc, self.k, self.e, self.s
        act.wait_ge(e["h1_ps"], i + 1)
        nc.scalar.activation(self.h1[:, :], self.ps_e[:, :], ACT.Silu, bias=k.b_col[:, 0:1]).then_inc(e["h1_sb"], 1)
        act.wait_ge(e["h2_ps"], i + 1)
        nc.scalar.activation(self.h2[:, :], self.ps_e[:, :], ACT.Silu, bias=k.b_col[:, 1:2]).then_inc(e["h2_sb"], 1)
        if not isinstance(i, int) or i > 0:
            self.store(act, i - 1)
        act.wait_ge(e["w_ps"], i + 1)
        need(act, s["tp"][1], i)
        nc.scalar.activation(self.w3[:, :], self.ps_e[:, :], ACT.Identity, bias=k.b_col[:, 2:3])\
            .then_inc(e["w_sb"], 1)
        for b in range(2):
            act.wait_ge(s["xT"][b], i + 1)
            need(act, s["out_ps"][b], i)
            nc.scalar.activation(self.xt[b][:, :], self.ps_x[b][:, :], ACT.Copy).then_inc(s["xT_sb"][b], 1)

    def vector(self, v, i):
        nc, k, e, s = self.nc, self.k, self.e, self.s
        for b in range(2):
            at = i * 2 * GROUP + b * GROUP
            v.wait_ge(s["gathered"][b], i * 128 + 128)
            need(v, s["stored"][b], i * 16)
            nc.vector.tensor_tensor(self.pay[b][:, :, C + XD:], self.xg[b][:, :, self.dst_half(b)],
                                    k.b_proj[:, :, :], ALU.add).then_inc(s["x_used"][b], 1)
            nc.vector.tensor_scalar(self.pay[b][:, :, C + 68], k.key["dst"][:, bass.ds(at, GROUP)], 1.0, None,
                                    ALU.mult)
        v.wait_ge(e["kv_ps"], i + 1)
        v.wait_ge(e["w_sb"], i + 1)
        for b in range(2):
            half = self.src_half(b)
            nc.vector.scalar_tensor_tensor(self.xt[b][half, :], self.ps_x[0][half, :], k.b_col[half, 3:4],
                                           self.w3[half, :], ALU.add, ALU.mult).then_inc(s["tp"][b], 1)
        for b in range(2):
            st = Steps(v, s["step"][b], i * 3)
            v.wait_ge(s["out_ps"][b], i + 1)
            pay, qb = self.pay[b], self.qb[b]
            for q in range(GROUP):
                at = i * 2 * GROUP + (b * GROUP + q)
                ins = nc.vector.scalar_tensor_tensor(pay[:, q, 0:2 * C], self.out_tile(q, 0, 2 * C),
                                                     k.ew[:, bass.ds(at, 1)], k.b_kv[:, :], ALU.mult, ALU.add)
            st.did(ins)
            q_ps = self.ps_o[:, :, 0:6 * C].rearrange("p a (t c) -> p a t c", t=2)[:, :, :, 2 * C:3 * C]
            st.did(nc.vector.tensor_tensor(qb[:, :, :].rearrange("p (a t) c -> p a t c", t=2), q_ps,
                                           k.b_q[:, :, :].rearrange("p (a t) c -> p a t c", t=2), ALU.add))
            st.settle()
            st.link(nc.vector.tensor_tensor(qb[:, :, :], qb[:, :, :], pay[:, :, 0:C], ALU.mult))
            nc.vector.tensor_reduce(pay[:, :, 2 * C:2 * C + HEADS],
                                    qb[:, :, :].rearrange("p g (h c) -> p g h c", h=HEADS), AX, ALU.add)\
                .then_inc(s["pay_ready"][b], 1)


class FirstNodes:

    def __init__(self, nc, k, t, d, io, J):
        self.nc, self.k, self.t, self.J, self.R = nc, k, t, J, d["R"]
        self.x = t.sb("nodes_x", [P, J, C])
        self.cen = t.sb("nodes_cen", [P, J, C])
        self.sq = t.sb("nodes_sq", [P, J, C])
        self.res = t.sb("nodes_res", [P, J, XW])
        self.stat = t.sb("nodes_stat", [P, 4, J])
        self.eps = t.sb("nodes_eps", [P, 1])
        self.last = t.sb("nodes_last", [P, d["R"]])
        self.rows_in = io["x"].rearrange("(p r) c -> p r c", r=d["R"])
        self.rows_out = k.d_xt.rearrange("(a b) o -> a (b o)", b=XW)[0:d["N_PAD"], :]\
            .rearrange("(p r) c -> p r c", r=d["R"])
        (self.last_in, self.x_in, self.step, self.centred, self.squared, self.dev, self.made,
         self.stored) = (t.sem(f"nodes_{n}") for n in ("last_in", "x_in", "step", "centred", "squared", "dev",
                                                       "made", "stored"))

    def sync(self, sp, n, at, rows):
        need(sp, self.centred, n)
        sp.sem_inc(self.t.passed("sp"), 1)
        sp.dma_start(self.x[:, 0:rows, :], self.rows_in[:, bass.ds(at, rows), :]).then_inc(self.x_in, 16)

    def centre(self, v, n, rows):
        nc, st = self.nc, Steps(v, self.step, n * 4)
        x, mean = self.x[:, 0:rows, :], self.stat[:, 0, 0:rows]
        v.wait_ge(self.x_in, n * 16 + 16)
        st.link(nc.vector.tensor_tensor(x, x, self.k.b_proj[:, 0:1, :].to_broadcast([P, rows, C]), ALU.add))
        st.link(nc.vector.tensor_reduce(mean, x, AX, ALU.add))
        st.link(nc.vector.tensor_scalar(mean, mean, 1.0 / C, None, ALU.mult))
        need(v, self.made, n)
        nc.vector.tensor_tensor(self.cen[:, 0:rows, :], x, mean.unsqueeze(2).to_broadcast([P, rows, C]),
                                ALU.subtract).then_inc(self.centred, 1)

    def scalar(self, act, n, rows):
        nc = self.nc
        act.wait_ge(self.centred, n + 1)
        need(act, self.made, n)
        for j in range(rows):
            ins = nc.scalar.activation(self.sq[:, j, :], self.cen[:, j, :], ACT.Square,
                                       accum_out=self.stat[:, 1, j:j + 1])
        ins.then_inc(self.squared, 1)
        act.wait_ge(self.squared, n + 1)
        nc.scalar.activation(self.stat[:, 2, 0:rows], self.stat[:, 1, 0:rows], ACT.Sqrt, bias=self.eps[:, 0:1],
                             scale=1.0 / C).then_inc(self.dev, 1)

    def finish(self, v, n, at, rows):
        nc, st = self.nc, Steps(v, self.step, n * 4 + 3)
        v.wait_ge(self.dev, n + 1)
        need(v, self.stored, n * 16)
        st.did(nc.vector.reciprocal(self.stat[:, 3, 0:rows], self.stat[:, 2, 0:rows]))
        nc.vector.tensor_scalar(self.res[:, 0:rows, C], self.last[:, bass.ds(at, rows)], 1.0, None, ALU.mult)
        st.settle()
        nc.vector.tensor_tensor(self.res[:, 0:rows, 0:C], self.cen[:, 0:rows, :],
                                self.stat[:, 3, 0:rows].unsqueeze(2).to_broadcast([P, rows, C]), ALU.mult)\
            .then_inc(self.made, 1)

    def store(self, act, n, at, rows):
        act.wait_ge(self.made, n + 1)
        act.sem_inc(self.t.passed("act"), 1)
        act.dma_start(self.rows_out[:, bass.ds(at, rows), :], self.res[:, 0:rows, :]).then_inc(self.stored, 16)


def edges_and_nodes(nc, k, d, io):
    T, R = d["T"], d["R"]
    t = Pool2(nc, "msg")
    m = Messages(nc, k, t, d, io)
    A = T // Counting.H
    B = m.N - A
    J = R // B
    rest = R - J * B
    c = Pool2(nc, "count")
    counting = Counting(nc, k, c, d, "src")
    zeroed = c.sem("zeroed")
    with nc.Block() as block:
        @block.sync
        def _(sp):
            repeat(sp, A, lambda i: m.sync(sp, i))

        @block.gpsimd
        def _(g):
            repeat(g, A, lambda i: m.gpsimd(g, i))

        @block.tensor
        def _(pe):
            pe.wait_ge(zeroed, 1)
            cuts = (0, 5, 10, Counting.H)
            repeat(pe, A, lambda i: m.tensor(pe, i, lambda n: counting.tensor(pe, i, cuts[n], cuts[n + 1])))

        @block.scalar
        def _(act):
            repeat(act, A, lambda i: m.scalar(act, i))

        @block.vector
        def _(v):
            nc.vector.memset(counting.table[:, :], 0.0).then_inc(zeroed, 1)
            for b in range(2):
                nc.vector.memset(m.pay[b][:, :, :], 0.0).then_inc(m.init, 1)
            v.wait_ge(m.init, 2)

            def body(i):
                counting.vector(v, i)
                m.vector(v, i)

            repeat(v, A, body)
    first_places(nc, k, c, d, "src", counting.table, True)
    c.close()

    f = Pool2(nc, "nodes")
    nodes = FirstNodes(nc, k, f, d, io, J)
    zeros = f.sb("zeros", [P, 28 * C])
    init, zero_s = f.sem("init"), f.sem("zero")
    with nc.Block() as block:
        @block.sync
        def _(sp):
            sp.dma_start(nodes.last[:, :], k.d_last.rearrange("a b -> (a b)").rearrange("(p r) -> p r", r=R))\
                .then_inc(nodes.last_in, 16)

            def body(n):
                m.sync(sp, n + A)
                nodes.sync(sp, n, n * J, J)
            repeat(sp, B, body)
            if rest:
                nodes.sync(sp, B, B * J, rest)
            sp.wait_ge(init, 1)
            zv = k.d_acc[0:d["N_PAD"], :].rearrange("(p m r) c -> m p (r c)", p=P, r=28)
            for q in range(R // 28):
                sp.dma_start(zv[q], zeros[:, :]).then_inc(zero_s, 16)
            for z in k.d_z:
                sp.dma_start(z[d["E_PAD"]:d["E_PAD"] + P, :], zeros[:, 0:C]).then_inc(zero_s, 16)
            sp.wait_ge(zero_s, 16 * (R // 28 + 3))

        @block.gpsimd
        def _(g):
            with g.Fori(A, m.N) as i:
                m.gpsimd(g, i)

        @block.tensor
        def _(pe):
            with pe.Fori(A, m.N) as i:
                m.tensor(pe, i, lambda n: None)

        @block.scalar
        def _(act):
            act.wait_ge(init, 1)

            def body(n):
                if not isinstance(n, int) or n > 0:
                    nodes.store(act, n - 1, (n - 1) * J, J)
                m.scalar(act, n + A)
                nodes.scalar(act, n, J)
            repeat(act, B, body)
            nodes.store(act, B - 1, (B - 1) * J, J)
            m.store(act, m.N - 1)
            if rest:
                nodes.scalar(act, B, rest)
                nodes.store(act, B, B * J, rest)
            act.wait_ge(nodes.stored, 16 * (B + (rest > 0)))
            for b in range(2):
                act.wait_ge(m.s["stored"][b], 16 * m.N)

        @block.vector
        def _(v):
            nc.vector.memset(zeros[:, :], 0.0)
            nc.vector.memset(nodes.eps[:, :], EPS).then_inc(init, 1)
            v.wait_ge(nodes.last_in, 16)

            def body(n):
                nodes.centre(v, n, J)
                m.vector(v, n + A)
                nodes.finish(v, n, n * J, J)
            repeat(v, B, body)
            if rest:
                nodes.centre(v, B, rest)
                nodes.finish(v, B, B * J, rest)
    f.close()
    t.close()


class Placing:

    def __init__(self, nc, k, t, d, key, payload, width, dt, out):
        two = range(2)
        HP = d["HP"]
        self.nc, self.k, self.t, self.g, self.key = nc, k, t, k.digits[key], k.key[key]
        self.N, self.HP, self.payload, self.out = d["S"] // 2, HP, payload, out
        self.hi_b = [t.sb(f"hi_b{b}", [HP, GE], F16) for b in two]
        self.key_b = [t.sb(f"key_b{b}", [P, GE]) for b in two]
        self.pay = [t.sb(f"pay{b}", [P, GROUP, width], dt) for b in two]
        self.hi_t = [t.sb(f"hi_t{b}", [HP, BLK, GE], F16) for b in two]
        self.lo1 = [t.sb(f"lo1{b}", [P, GROUP, LO], F16) for b in two]
        self.hi1 = [t.sb(f"hi1{b}", [P, GROUP, BLK, HP], F16) for b in two]
        self.next = t.sb("next", [HP, KEYS_PER_PART], I32)
        self.low = [t.sb(f"low{b}", [HP, KEYS_PER_PART], F16) for b in two]
        self.high = [t.sb(f"high{b}", [HP, KEYS_PER_PART], F16) for b in two]
        self.same = t.sb("same", [P, GROUP, GE], F16)
        self.hit = t.sb("hit", [P, GROUP, LO], F16)
        self.rank = [t.sb(f"rank{b}", [P, GROUP]) for b in two]
        self.base = [t.sb(f"base{b}", [P, GROUP]) for b in two]
        self.pos = [t.sb(f"pos{b}", [P, GROUP], I32) for b in two]
        self.ident16 = t.sb("ident16", [P, P], F16)
        self.table = t.ps("place_table", [HP, KEYS_PER_PART])
        self.look = [t.ps(f"look{b}", [P, GROUP, LO]) for b in two]
        self.s = {n: t.sems(n) for n in ("rows_in", "pay_in", "prepared", "split", "updated", "looked", "reduced",
                                         "pos_ready", "scattered")}
        self.zeroed, self.started, self.whole = t.sem("zeroed"), t.sem("started"), t.sem("next_made")

    def sync(self, sp, i):
        s, g = self.s, self.g
        for b in range(2):
            at = i * 2 + b
            need(sp, s["prepared"][b], i)
            sp.sem_inc(self.t.passed("sp"), 1)
            sp.dma_start(self.hi_b[b][:, :], g.hi_rows[bass.ds(at, 1), :].to_broadcast([self.HP, GE]))\
                .then_inc(s["rows_in"][b], 16)
            sp.dma_start(self.key_b[b][:, :], g.key_rows[bass.ds(at, 1), :].to_broadcast([P, GE]))\
                .then_inc(s["rows_in"][b], 16)
            need(sp, s["scattered"][b], i * GROUP * 16)
            sp.sem_inc(self.t.passed("sp"), 1)
            sp.dma_start(self.pay[b][:, :, :], self.payload[:, bass.ds(i * 2 * GROUP + b * GROUP, GROUP), :])\
                .then_inc(s["pay_in"][b], 16)

    def scalar(self, act, b, n):
        s, nc = self.s, self.nc
        if b == 0:
            need(act, s["updated"][1], n)
            act.wait_ge(self.started, 1)
        else:
            act.wait_ge(s["updated"][0], n + 1)
        need(act, s["looked"][b], n)
        need(act, s["split"][1 - b], n + b)
        nc.scalar.activation(self.next[:, :], self.table[:, :], ACT.Copy).then_inc(self.whole, 1)
        act.wait_ge(self.whole, n * 2 + (b + 1))
        by = self.next[:, :].bitcast(mybir.dt.uint8).rearrange("p (c b) -> p c b", b=4)
        nc.scalar.activation(self.low[b][:, :], by[:, :, 0], ACT.Copy)
        nc.scalar.activation(self.high[b][:, :], by[:, :, 1], ACT.Copy, scale=256.0).then_inc(s["split"][b], 1)

    def begin(self, pe):
        pe.wait_ge(self.zeroed, 1)
        for half in (self.g.start_hi, self.g.start_lo):
            for q in range(0, KEYS_PER_PART, 512):
                ins = self.nc.tensor.matmul(self.table[:, q:q + 512], self.ident16[0:self.HP, 0:self.HP],
                                            half[:, q:q + 512], start=False, stop=False, skip_group_check=True)
        ins.then_inc(self.started, 1)

    def tensor(self, pe, b, n):
        s, nc = self.s, self.nc
        pe.wait_ge(s["prepared"][b], n + 1)
        pe.wait_ge(s["split"][b], n + 1)
        for g in range(GROUP):
            for q in range(BLK):
                ins = nc.tensor.matmul(self.table[:, q * LO:(q + 1) * LO], self.hi1[b][:, g, q, :],
                                       self.lo1[b][:, g, :], start=False, stop=False, skip_group_check=True)
        ins.then_inc(s["updated"][b], 1)
        need(pe, s["reduced"][b], n)
        for g in range(GROUP):
            m = 0
            for part in (self.low[b], self.high[b]):
                for q in range(BLK):
                    ins = nc.tensor.matmul(self.look[b][:, g, :], self.hi_t[b][:, q, g * P:(g + 1) * P],
                                           part[:, q * LO:(q + 1) * LO], start=(m == 0), stop=(m == 2 * BLK - 1))
                    m += 1
        ins.then_inc(s["looked"][b], 1)

    def zero(self):
        self.nc.vector.memset(self.table[:, :], 0.0)
        self.nc.vector.tensor_copy(self.ident16[:, :], self.k.ident[:, :]).then_inc(self.zeroed, 1)

    def prepare(self, v, b, n):
        s, nc = self.s, self.nc
        v.wait_ge(s["rows_in"][b], n * 32 + 32)
        need(v, s["looked"][b], n)
        need(v, s["pos_ready"][b], n)
        for q in range(BLK):
            nc.vector.tensor_scalar(self.hi_t[b][:, q, :], self.hi_b[b][:, :], self.k.hi_of_part[0:self.HP, q:q + 1],
                                    None, ALU.is_equal)
        for g in range(GROUP):
            at = n * 2 * GROUP + (b * GROUP + g)
            one_hots(nc, self.k, self.g, at, self.lo1[b][:, g, :], self.hi1[b][:, g, :, :])
        need(v, s["prepared"][1 - b], n + b)
        for g in range(GROUP):
            at = n * 2 * GROUP + (b * GROUP + g)
            w = (g + 1) * P
            ins = nc.vector.scalar_tensor_tensor(self.same[:, g, 0:w], self.key_b[b][:, 0:w],
                                                 self.key[:, bass.ds(at, 1)], self.k.earlier[:, GE - w:],
                                                 ALU.is_equal, ALU.mult, accum_out=self.rank[b][:, g:g + 1])
        ins.then_inc(s["prepared"][b], 1)

    def reduce(self, v, b, n):
        s, nc = self.s, self.nc
        v.wait_ge(s["looked"][b], n + 1)
        need(v, s["reduced"][1 - b], n + b)
        for g in range(GROUP):
            ins = nc.vector.tensor_tensor_reduce(out=self.hit[:, g, :], in0=self.lo1[b][:, g, :],
                                                 in1=self.look[b][:, g, :], scale=1.0, scalar=0.0, op0=ALU.mult,
                                                 op1=ALU.add, accum_out=self.base[b][:, g:g + 1])
        ins.then_inc(s["reduced"][b], 1)
        v.wait_ge(s["reduced"][b], n + 1)
        need(v, s["scattered"][b], n * GROUP * 16)
        nc.vector.tensor_tensor(self.pos[b][:, :], self.base[b][:, :], self.rank[b][:, :], ALU.add)\
            .then_inc(s["pos_ready"][b], 1)

    def gpsimd(self, g, b, n):
        s = self.s
        g.wait_ge(s["pos_ready"][b], n + 1)
        g.wait_ge(s["pay_in"][b], n * 16 + 16)
        g.sem_inc(self.t.passed("pool"), 1)
        for q in range(GROUP):
            g.indirect_dma_start(out=self.out,
                                 out_offset=bass.IndirectOffsetOnAxis(ap=self.pos[b][:, q:q + 1], axis=0),
                                 in_=self.pay[b][:, q, :], in_offset=None).then_inc(s["scattered"][b], 16)

    def end(self, g):
        for b in range(2):
            g.wait_ge(self.s["scattered"][b], self.N * GROUP * 16)


def place_phase(nc, k, d, key, payload, width, dt, out):
    t = Pool2(nc, key+"_place")
    p = Placing(nc, k, t, d, key, payload, width, dt, out)
    with nc.Block() as block:
        @block.sync
        def _(sp):
            repeat(sp, p.N, lambda i: p.sync(sp, i))

        @block.scalar
        def _(act):
            def body(i):
                for b in range(2):
                    p.scalar(act, b, i)
            repeat(act, p.N, body)

        @block.tensor
        def _(pe):
            p.begin(pe)

            def body(i):
                for b in range(2):
                    p.tensor(pe, b, i)
            repeat(pe, p.N, body)

        @block.vector
        def _(v):
            p.zero()

            def body(i):
                p.prepare(v, 0, i)
                if not isinstance(i, int) or i > 0:
                    p.reduce(v, 1, i - 1)
                p.prepare(v, 1, i)
                p.reduce(v, 0, i)
            repeat(v, p.N, body)
            p.reduce(v, 1, p.N - 1)

        @block.gpsimd
        def _(g):
            def body(i):
                for b in range(2):
                    p.gpsimd(g, b, i)
            repeat(g, p.N, body)
            p.end(g)
    t.close()


def sort_payload(nc, k, d, io):
    m = Pool2(nc, "dst")
    entered = m.sem("entered")
    with nc.Block() as block:
        @block.sync
        def _(sp):
            sp.sem_inc(entered, 1)

        @block.gpsimd
        def _(g):
            g.sem_inc(entered, 1)

        @block.tensor
        def _(pe):
            pe.sem_inc(entered, 1)

        @block.scalar
        def _(act):
            act.sem_inc(entered, 1)

        @block.vector
        def _(v):
            v.sem_inc(entered, 1)
            v.wait_ge(entered, 5)
    digits(nc, k, m, d, io, "dst")
    c = Pool2(nc, "dst_count")
    counting = Counting(nc, k, c, d, "dst")
    zeroed, copied = c.sem("zeroed"), c.sem("copied")
    steps = d["T"] // Counting.H
    with nc.Block() as block:
        @block.sync
        def _(sp):
            sp.dma_start(k.d_pay_given, k.d_pay_sorted).then_inc(copied, 16)
            sp.wait_ge(copied, 16)

        @block.vector
        def _(v):
            nc.vector.memset(counting.table[:, :], 0.0).then_inc(zeroed, 1)
            repeat(v, steps, lambda i: counting.vector(v, i))

        @block.tensor
        def _(pe):
            pe.wait_ge(zeroed, 1)
            repeat(pe, steps, lambda i: counting.tensor(pe, i, 0, Counting.H))
    first_places(nc, k, c, d, "dst", counting.table, False)
    c.close()
    place_phase(nc, k, d, "dst", k.d_pay_given.rearrange("(p t) c -> p t c", t=d["T"]), PAY, F32, k.d_pay_sorted)
    m.close()


def final_nodes(nc, k, d, io):
    R, J = d["R"], d["J"]
    N = R // J // 2
    t = Pool2(nc, "final")
    two = range(2)
    xin = [t.sb(f"x{b}", [P, J, XW]) for b in two]
    acc = [t.sb(f"acc{b}", [P, J, C]) for b in two]
    cen = [t.sb(f"cen{b}", [P, J, C]) for b in two]
    sq = [t.sb(f"sq{b}", [P, J, C]) for b in two]
    stat = [t.sb(f"stat{b}", [P, 4, J]) for b in two]
    eps = t.sb("eps", [P, 1])
    s = {n: t.sems(n) for n in ("in", "step", "sum", "centred", "squared", "dev", "scale", "res", "stored")}
    init = t.sem("init")
    xt_nodes = k.d_xt.rearrange("(a b) o -> a (b o)", b=XW)[0:d["N_PAD"], :].rearrange("(p r) c -> p r c", r=R)
    acc_nodes = k.d_acc[0:d["N_PAD"], :].rearrange("(p r) c -> p r c", r=R)
    out_nodes = io["out"].rearrange("(p r) c -> p r c", r=R)
    with nc.Block() as block:
        @block.sync
        def _(sp):
            def body(n):
                for b in two:
                    at = n * 2 * J + b * J
                    need(sp, s["centred"][b], n)
                    sp.sem_inc(t.passed("sp"), 1)
                    sp.dma_start(xin[b][:, :, :], xt_nodes[:, bass.ds(at, J), :]).then_inc(s["in"][b], 16)
                    sp.dma_start(acc[b][:, :, :], acc_nodes[:, bass.ds(at, J), :]).then_inc(s["in"][b], 16)
            repeat(sp, N, body)

        @block.gpsimd
        def _(g):
            def body(n):
                for b in two:
                    at = n * 2 * J + b * J
                    g.wait_ge(s["res"][b], n + 1)
                    g.sem_inc(t.passed("pool"), 1)
                    g.dma_start(out_nodes[:, bass.ds(at, J), :], cen[b][:, :, :]).then_inc(s["stored"][b], 16)
            repeat(g, N, body)
            for b in two:
                g.wait_ge(s["stored"][b], 16 * N)

        @block.scalar
        def _(act):
            act.wait_ge(init, 1)

            def body(n):
                for b in two:
                    act.wait_ge(s["centred"][b], n + 1)
                    for j in range(J):
                        ins = nc.scalar.activation(sq[b][:, j, :], cen[b][:, j, :], ACT.Square,
                                                   accum_out=stat[b][:, 1, j:j + 1])
                    ins.then_inc(s["squared"][b], 1)
                    act.wait_ge(s["squared"][b], n + 1)
                    nc.scalar.activation(stat[b][:, 2, :], stat[b][:, 1, :], ACT.Sqrt, bias=eps[:, 0:1],
                                         scale=1.25 ** 2 / C).then_inc(s["dev"][b], 1)
            repeat(act, N, body)

        @block.vector
        def _(v):
            nc.vector.memset(eps[:, :], EPS).then_inc(init, 1)

            def centre(b, n):
                st = Steps(v, s["step"][b], n * 2)
                v.wait_ge(s["in"][b], n * 32 + 32)
                nc.vector.scalar_tensor_tensor(acc[b][:, :, :], acc[b][:, :, :], 0.2, xin[b][:, :, 0:C], ALU.mult,
                                               ALU.add).then_inc(s["sum"][b], 1)
                v.wait_ge(s["sum"][b], n + 1)
                st.link(nc.vector.tensor_reduce(stat[b][:, 0, :], acc[b][:, :, :], AX, ALU.add))
                st.link(nc.vector.tensor_scalar(stat[b][:, 0, :], stat[b][:, 0, :], 1.0 / C, None, ALU.mult))
                need(v, s["stored"][b], n * 16)
                nc.vector.tensor_tensor(cen[b][:, :, :], acc[b][:, :, :],
                                        stat[b][:, 0, :].unsqueeze(2).to_broadcast([P, J, C]), ALU.subtract)\
                    .then_inc(s["centred"][b], 1)

            def finish(b, n):
                v.wait_ge(s["dev"][b], n + 1)
                nc.vector.reciprocal(stat[b][:, 3, :], stat[b][:, 2, :]).then_inc(s["scale"][b], 1)
                v.wait_ge(s["scale"][b], n + 1)
                nc.vector.scalar_tensor_tensor(cen[b][:, :, :], cen[b][:, :, :], 1.25,
                                               stat[b][:, 3, :].unsqueeze(2).to_broadcast([P, J, C]), ALU.mult,
                                               ALU.mult)\
                    .then_inc(s["res"][b], 1)

            def body(n):
                centre(0, n)
                if not isinstance(n, int) or n > 0:
                    finish(1, n - 1)
                centre(1, n)
                finish(0, n)
            repeat(v, N, body)
            finish(1, N - 1)
    t.close()


def segments(nc, k, d, g, tag):
    T = d["T"]
    t = Pool2(nc, f"seg_{tag}")
    before, after = t.sb("before", [P, 1]), t.sb("after", [P, 1])
    n_lead = t.sb("n_lead", [P, 1])
    rowf = t.sb("rowf", [P, 1])
    away = t.sb("away", [P, T])
    v_step, shifted, ready = t.sem("v_step"), t.sem("shifted"), t.sem("ready")
    with nc.Block() as block:
        @block.sync
        def _(sp):
            sp.wait_ge(ready, 1)
            with nc.allow_non_contiguous_dma(reason="one key per partition"):
                sp.dma_start(before[1:P, :], g.key[0:P - 1, T - 1:T]).then_inc(shifted, 16)
                sp.dma_start(after[0:P - 1, :], g.key[1:P, 0:1]).then_inc(shifted, 16)

        @block.vector
        def _(v):
            st = Steps(v, v_step)
            nc.vector.memset(before[:, :], -1.0)
            nc.vector.memset(g.cont[:, 0:1], 0.0)
            nc.vector.memset(after[:, :], -1.0).then_inc(ready, 1)
            st.did(nc.vector.tensor_tensor(g.cont[:, 1:T], g.key[:, 1:T], g.key[:, 0:T - 1], ALU.is_equal))
            st.did(nc.vector.tensor_tensor(g.last[:, 0:T - 1], g.key[:, 0:T - 1], g.key[:, 1:T], ALU.not_equal))
            st.link(nc.vector.tensor_scalar(g.lead[:, :], g.key[:, :], g.key[:, 0:1], None, ALU.is_equal))
            st.link(nc.vector.tensor_reduce(n_lead[:, :], g.lead[:, :], AX, ALU.add))
            st.did(nc.vector.tensor_scalar(g.whole[:, :], n_lead[:, :], float(T), None, ALU.is_equal))
            nc.vector.memset(g.end_lead[:, T - 1:T], 1.0)
            st.did(nc.vector.tensor_copy(g.end_lead[:, 0:T - 1], g.last[:, 0:T - 1]))
            st.link(nc.vector.scalar_tensor_tensor(rowf[:, :], n_lead[:, :], -1.0, k.place[:, 0:1], ALU.add, ALU.add))
            nc.vector.tensor_copy(g.row[:, :], rowf[:, :])
            st.did(nc.vector.tensor_tensor(g.end_lead[:, :], g.end_lead[:, :], g.lead[:, :], ALU.mult))
            v.wait_ge(shifted, 32)
            st.did(nc.vector.tensor_tensor(g.joins[:, :], g.key[:, 0:1], before[:, :], ALU.is_equal))
            st.link(nc.vector.tensor_tensor(g.last[:, T - 1:T], g.key[:, T - 1:T], after[:, :], ALU.not_equal))
            st.link(nc.vector.tensor_scalar(away[:, :], k.place[:, :], float(d["N_PAD"]), None, ALU.add))
            st.link(nc.vector.tensor_tensor(g.at[:, :], g.key[:, :], away[:, :], ALU.subtract))
            st.link(nc.vector.tensor_tensor(g.at[:, :], g.at[:, :], g.last[:, :], ALU.mult))
            st.link(nc.vector.tensor_tensor(g.at[:, :], g.at[:, :], away[:, :], ALU.add))
    t.close()


class Segments:
    def __init__(self, m, T):
        self.key, self.cont, self.last, self.lead, self.end_lead, self.at = (
            m.sb(n, [P, T]) for n in ("key", "cont", "last", "lead", "end_lead", "at"))
        self.joins, self.whole, self.row = m.sb("joins", [P, 1]), m.sb("whole", [P, 1]), m.sb("row", [P, 1], I32)


def hand_over(nc, k, tag, width, state, carry, op, weight):
    t = Pool2(nc, f"hand_{tag}")
    ps_s, ps_w, ps_b = t.ps("state", [P, P]), t.ps("weight", [P, P]), t.ps("back", [P, P])
    wt = t.sb("wt", [P, P])
    out = t.sb("out", [P, P + 1])
    turned, wt_in, scanned, back = t.sem("turned"), t.sem("wt_in"), t.sem("scanned"), t.sem("back")
    with nc.Block() as block:
        @block.tensor
        def _(pe):
            nc.tensor.transpose(ps_s[0:width, :], state, k.ident[:, :])
            nc.tensor.transpose(ps_w[0:width, :], weight, k.ident[:, :]).then_inc(turned, 1)
            pe.wait_ge(scanned, 1)
            nc.tensor.transpose(ps_b[:, 0:width], out[0:width, 0:P], k.ident[0:width, 0:width]).then_inc(back, 1)

        @block.vector
        def _(v):
            nc.vector.memset(out[0:width, 0:1], 0.0)
            v.wait_ge(turned, 1)
            nc.vector.tensor_copy(wt[0:width, :], ps_w[0:width, :]).then_inc(wt_in, 1)
            v.wait_ge(wt_in, 1)
            nc.vector.tensor_tensor_scan(out[0:width, 1:P + 1], wt[0:width, :], ps_s[0:width, :], 0.0,
                                         ALU.mult if op == ALU.add else ALU.add, op).then_inc(scanned, 1)
            v.wait_ge(back, 1)
            nc.vector.tensor_copy(carry, ps_b[:, 0:width])
    t.close()


def attention(nc, k, d, io):
    T, S = d["T"], d["S"]
    m = Pool2(nc, "att")
    g = Segments(m, T)
    V = m.sb("values", [P, T, V_W])
    top = m.sb("top", [P, HEADS, T])
    wgt = m.sb("wgt", [P, HEADS, T])
    pen = m.sb("pen", [P, T])
    tail, carry = m.sb("tail", [P, 80]), m.sb("carry", [P, 80])
    w4, top_lead, decay = m.sb("w4", [P, HEADS]), m.sb("top_lead", [P, HEADS]), m.sb("decay", [P, HEADS])
    factor = m.sb("factor", [P, C + HEADS])
    factor_w = m.sb("factor_w", [P, C + HEADS])
    rden = m.sb("rden", [P, T, HEADS])
    at65 = m.sb("at65", [P, T])
    pay_rows = k.d_pay_sorted.rearrange("(p t) c -> p t c", t=T)

    a = Pool2(nc, "att_load")
    loaded, keyed = a.sem("loaded"), a.sem("keyed")
    with nc.Block() as block:
        @block.sync
        def _(sp):
            q = T // 4
            for c in range(4):
                sp.dma_start(V[:, c * q:(c + 1) * q, :], pay_rows[:, c * q:(c + 1) * q, 0:V_W]).then_inc(loaded, 16)

        @block.vector
        def _(v):
            v.wait_ge(loaded, 64)
            nc.vector.tensor_copy(g.key[:, :], V[:, :, 68]).then_inc(keyed, 1)
    a.close()
    segments(nc, k, d, g, "dst")

    a = Pool2(nc, "att_max")
    step = a.sem("step")
    with nc.Block() as block:
        @block.vector
        def _(v):
            st = Steps(v, step)
            st.link(nc.vector.tensor_scalar(pen[:, :], g.cont[:, :], -1.0, BIG, ALU.add, ALU.mult))
            for h in range(HEADS):
                st.did(nc.vector.tensor_tensor_scan(top[:, h, :], pen[:, :], V[:, :, C + h], -BIG, ALU.add, ALU.max))
            st.settle()
            st.did(nc.vector.tensor_copy(tail[:, 0:HEADS], top[:, :, T - 1]))
            st.link(nc.vector.tensor_tensor(w4[:, 0:1], g.joins[:, :], g.whole[:, :], ALU.mult))
            for h in range(HEADS):
                st.did(nc.vector.tensor_scalar(tail[:, 8 + h:9 + h], w4[:, 0:1], -1.0, BIG, ALU.add, ALU.mult))
            st.settle()
    a.close()
    hand_over(nc, k, "max", HEADS, tail[:, 0:HEADS], carry[:, 0:HEADS], ALU.max, tail[:, 8:8 + HEADS])

    a = Pool2(nc, "att_sum")
    step, for_exp, exped = a.sem("step"), a.sem("for_exp"), a.sem("exped")
    diff = a.sb("diff", [P, HEADS, T])
    with nc.Block() as block:
        @block.scalar
        def _(act):
            act.wait_ge(for_exp, 1)
            nc.scalar.activation(wgt[:, :, :], wgt[:, :, :], ACT.Exp)
            nc.scalar.activation(diff[:, :, :], diff[:, :, :], ACT.Exp)
            nc.scalar.activation(decay[:, :], decay[:, :], ACT.Exp).then_inc(exped, 1)

        @block.vector
        def _(v):
            st = Steps(v, step)
            st.link(nc.vector.tensor_scalar(pen[:, :], g.lead[:, :], g.joins[:, 0:1], -1.0, ALU.mult, ALU.add))
            st.link(nc.vector.tensor_scalar(pen[:, :], pen[:, :], BIG, None, ALU.mult))
            for h in range(HEADS):
                st.did(nc.vector.scalar_tensor_tensor(top[:, h, :], pen[:, :], carry[:, h:h + 1], top[:, h, :],
                                                      ALU.add, ALU.max))
            st.settle()
            st.did(nc.vector.tensor_scalar(pen[:, :], g.lead[:, :], -1.0, BIG, ALU.add, ALU.mult))
            st.settle()
            for h in range(HEADS):
                st.did(nc.vector.tensor_tensor(diff[:, h, :], top[:, h, :], pen[:, :], ALU.add))
                st.did(nc.vector.tensor_tensor(wgt[:, h, :], V[:, :, C + h], top[:, h, :], ALU.subtract))
            st.settle()
            st.link(nc.vector.tensor_reduce(top_lead[:, :], diff[:, :, :], AX, ALU.max))
            st.link(nc.vector.tensor_tensor(decay[:, :], carry[:, 0:HEADS], top_lead[:, :], ALU.subtract))
            nc.vector.tensor_scalar(decay[:, :], decay[:, :], 0.0, None, ALU.min)
            st.did(nc.vector.memset(diff[:, :, 0:1], 0.0))
            st.link(nc.vector.tensor_tensor(diff[:, :, 1:T], top[:, :, 0:T - 1], top[:, :, 1:T], ALU.subtract))
            nc.vector.tensor_scalar(diff[:, :, :], diff[:, :, :], 0.0, None, ALU.min).then_inc(for_exp, 1)
            v.wait_ge(exped, 1)
            for h in range(HEADS):
                cols = slice(h * HD, (h + 1) * HD)
                st.did(nc.vector.tensor_tensor(top[:, h, :], diff[:, h, :], g.cont[:, :], ALU.mult))
                st.did(nc.vector.tensor_copy(V[:, :, C + h], wgt[:, h, :]))
                st.did(nc.vector.tensor_tensor(V[:, :, cols], V[:, :, cols],
                                               wgt[:, h, :].unsqueeze(2).to_broadcast([P, T, HD]), ALU.mult))
            st.settle()
            with v.Fori(0, HD) as f:
                for h in range(HEADS):
                    col = V[:, :, bass.ds(f + h * HD, 1)].rearrange("p t o -> p (t o)")
                    nc.vector.tensor_tensor_scan(col, top[:, h, :], col, 0.0, ALU.mult, ALU.add)
            for h in range(HEADS):
                st.did(nc.vector.tensor_tensor_scan(V[:, :, C + h], top[:, h, :], V[:, :, C + h], 0.0,
                                                    ALU.mult, ALU.add))
            st.settle()
            st.did(nc.vector.tensor_copy(tail[:, 0:C + HEADS], V[:, T - 1, 0:C + HEADS]))
            st.link(nc.vector.tensor_scalar(decay[:, :], decay[:, :], g.joins[:, 0:1], None, ALU.mult))
            st.did(nc.vector.tensor_copy(factor[:, 0:C].rearrange("p (h c) -> p h c", h=HEADS),
                                         decay[:, :].unsqueeze(2).to_broadcast([P, HEADS, HD])))
            st.did(nc.vector.tensor_copy(factor[:, C:C + HEADS], decay[:, :]))
            st.settle()
            st.link(nc.vector.tensor_scalar(factor_w[:, :], factor[:, :], g.whole[:, 0:1], None, ALU.mult))
    a.close()
    hand_over(nc, k, "sum", C + HEADS, tail[:, 0:C + HEADS], carry[:, 0:C + HEADS], ALU.add, factor_w[:, :])

    a = Pool2(nc, "att_rows")
    two = range(2)
    N = S // 2
    step, fixed = a.sem("step"), a.sem("fixed")
    xd = [a.sb(f"xd{b}", [P, GROUP, C]) for b in two]
    att = [a.sb(f"att{b}", [P, GROUP, C]) for b in two]
    att_t = [a.sb(f"att_t{b}", [C, GE]) for b in two]
    y = [a.sb(f"y{b}", [P, GROUP, C]) for b in two]
    sq = [a.sb(f"sq{b}", [P, GROUP, C]) for b in two]
    stat = [a.sb(f"stat{b}", [P, 4, GROUP]) for b in two]
    res = [a.sb(f"res{b}", [P, GROUP, C]) for b in two]
    idx = [a.sb(f"idx{b}", [P, GROUP], I32) for b in two]
    eps = a.sb("eps", [P, 1])
    ps_t = [a.ps(f"ps_t{b}", [C, GE]) for b in two]
    ps_y = [a.ps(f"ps_y{b}", [P, GROUP, C]) for b in two]
    s = {n: a.sems(n) for n in ("xd_in", "att", "turned", "turned_sb", "proj", "y_made", "cen", "sq", "var", "dev",
                                "res", "scattered", "v_step")}
    with nc.Block() as block:
        @block.sync
        def _(sp):
            with sp.Fori(0, N) as i:
                for b in two:
                    sp.wait_ge(s["y_made"][b], i)
                    sp.sem_inc(a.passed("sp"), 1)
                    sp.dma_start(xd[b][:, :, :], pay_rows[:, bass.ds(i * 2 * GROUP + b * GROUP, GROUP), XD:])\
                        .then_inc(s["xd_in"][b], 16)

        @block.tensor
        def _(pe):
            with pe.Fori(0, N) as i:
                for b in two:
                    pe.wait_ge(s["att"][b], i + 1)
                    pe.wait_ge(s["turned_sb"][b], i)
                    pe.sem_inc(a.passed("pe"), 1)
                    for q in range(GROUP):
                        ins = nc.tensor.transpose(ps_t[b][:, q * P:(q + 1) * P], att[b][:, q, :], k.ident[:, :])
                    ins.then_inc(s["turned"][b], 1)
                for b in two:
                    pe.wait_ge(s["turned_sb"][b], i + 1)
                    pe.wait_ge(s["y_made"][b], i)
                    for q in range(GROUP):
                        ins = nc.tensor.matmul(ps_y[b][:, q, :], att_t[b][:, q * P:(q + 1) * P], k.w_proj[:, :],
                                               start=True, stop=True)
                    ins.then_inc(s["proj"][b], 1)

        @block.scalar
        def _(act):
            with act.Fori(0, N) as i:
                for b in two:
                    act.wait_ge(s["turned"][b], i + 1)
                    act.wait_ge(s["proj"][b], i)
                    nc.scalar.activation(att_t[b][:, :], ps_t[b][:, :], ACT.Copy).then_inc(s["turned_sb"][b], 1)
                for b in two:
                    act.wait_ge(s["cen"][b], i + 1)
                    nc.scalar.activation(sq[b][:, :, :], y[b][:, :, :], ACT.Square).then_inc(s["sq"][b], 1)
                for b in two:
                    act.wait_ge(s["var"][b], i + 1)
                    nc.scalar.activation(stat[b][:, 2, :], stat[b][:, 1, :], ACT.Sqrt, bias=eps[:, 0:1],
                                         scale=1.0 / C).then_inc(s["dev"][b], 1)

        @block.vector
        def _(v):
            st = Steps(v, step)
            nc.vector.memset(eps[:, :], EPS)
            st.link(nc.vector.tensor_tensor(carry[:, 0:C + HEADS], carry[:, 0:C + HEADS], factor[:, :], ALU.mult))
            with v.Fori(0, (C + HEADS) // 4) as f:
                for q in range(4):
                    col = V[:, :, bass.ds(f * 4 + q, 1)].rearrange("p t o -> p (t o)")
                    nc.vector.scalar_tensor_tensor(col, g.end_lead[:, :], carry[:, bass.ds(f * 4 + q, 1)], col,
                                                   ALU.mult, ALU.add)
            st.link(nc.vector.memset(tail[:, 0:1], 0.0))
            st.did(nc.vector.tensor_scalar(at65[:, :], g.at[:, :], float(XW), None, ALU.mult))
            st.link(nc.vector.tensor_scalar(rden[:, :, :], V[:, :, C:C + HEADS], 1e-16, None, ALU.add))
            st.link(nc.vector.reciprocal(rden[:, :, :], rden[:, :, :]))

            def weigh(b, n):
                at = n * 2 * GROUP + b * GROUP
                v.wait_ge(s["turned"][b], n)
                for h in range(HEADS):
                    cols = slice(h * HD, (h + 1) * HD)
                    ins = nc.vector.tensor_tensor(att[b][:, :, cols], V[:, bass.ds(at, GROUP), cols],
                                                  rden[:, bass.ds(at, GROUP), h:h + 1].to_broadcast([P, GROUP, HD]),
                                                  ALU.mult)
                ins.then_inc(s["att"][b], 1)

            for b in two:
                weigh(b, 0)

            def rows(i, more):
                base = [Steps(v, s["v_step"][b], i * 3) for b in two]
                for b in two:
                    v.wait_ge(s["proj"][b], i + 1)
                    v.wait_ge(s["xd_in"][b], i * 16 + 16)
                    v.wait_ge(s["res"][b], i)
                    nc.vector.tensor_tensor(y[b][:, :, :], ps_y[b][:, :, :], xd[b][:, :, :], ALU.add)\
                        .then_inc(s["y_made"][b], 1)
                for b in two:
                    v.wait_ge(s["y_made"][b], i + 1)
                    base[b].did(nc.vector.tensor_reduce(stat[b][:, 0, :], y[b][:, :, :], AX, ALU.add))
                for b in two:
                    base[b].settle()
                    base[b].did(nc.vector.tensor_scalar(stat[b][:, 0, :], stat[b][:, 0, :], 1.0 / C, None, ALU.mult))
                for b in two:
                    base[b].settle()
                    nc.vector.tensor_tensor(y[b][:, :, :], y[b][:, :, :],
                                            stat[b][:, 0, :].unsqueeze(2).to_broadcast([P, GROUP, C]),
                                            ALU.subtract).then_inc(s["cen"][b], 1)
                if more:
                    for b in two:
                        weigh(b, i + 1)
                for b in two:
                    v.wait_ge(s["sq"][b], i + 1)
                    nc.vector.tensor_reduce(stat[b][:, 1, :], sq[b][:, :, :], AX, ALU.add).then_inc(s["var"][b], 1)
                for b in two:
                    at = i * 2 * GROUP + b * GROUP
                    v.wait_ge(s["dev"][b], i + 1)
                    base[b].did(nc.vector.reciprocal(stat[b][:, 3, :], stat[b][:, 2, :]))
                    v.wait_ge(s["scattered"][b], i * GROUP * 16)
                    nc.vector.tensor_scalar(idx[b][:, :], at65[:, bass.ds(at, GROUP)], 1.0, None, ALU.mult)
                    base[b].settle()
                    nc.vector.tensor_tensor(res[b][:, :, :], y[b][:, :, :],
                                            stat[b][:, 3, :].unsqueeze(2).to_broadcast([P, GROUP, C]),
                                            ALU.mult).then_inc(s["res"][b], 1)

            with v.Fori(0, N - 1) as i:
                rows(i, True)
            rows(N - 1, False)

        @block.gpsimd
        def _(gp):
            with gp.Fori(0, N) as i:
                for b in two:
                    gp.wait_ge(s["res"][b], i + 1)
                    gp.sem_inc(a.passed("pool"), 1)
                    for q in range(GROUP):
                        gp.indirect_dma_start(out=k.d_xt,
                                              out_offset=bass.IndirectOffsetOnAxis(ap=idx[b][:, q:q + 1], axis=0),
                                              in_=res[b][:, q, :], in_offset=None).then_inc(s["scattered"][b], 16)
            for b in two:
                gp.wait_ge(s["scattered"][b], N * GROUP * 16)
    a.close()
    m.close()


def layers(nc, k, d, io):
    T, S = d["T"], d["S"]
    m = Pool2(nc, "lay")
    two = range(2)
    N = S // 2
    CH = 7
    TC = T // CH
    g = Segments(m, T)
    rec = m.sb("rec", [P, T, 2], I32)
    nbr = m.sb("nbr", [P, T])
    G = m.sb("gathered", [P, T, XW])
    inv_deg = m.sb("inv_deg", [P, T])
    inv_row = m.sb("inv_row", [P, 1])
    joins_w = m.sb("joins_w", [P, C])
    joins_c = m.sb("joins_c", [P, C])
    carry = m.sb("carry", [P, C])
    tail = m.sb("tail", [P, C])
    tmp = m.sb("tmp", [P, T])

    a = Pool2(nc, "lay_load")
    loaded, keyed = a.sem("loaded"), a.sem("keyed")
    with nc.Block() as block:
        @block.sync
        def _(sp):
            sp.dma_start(rec[:, :, :], k.d_rec_sorted.rearrange("(p t) c -> p t c", t=T)).then_inc(loaded, 16)

        @block.vector
        def _(v):
            v.wait_ge(loaded, 16)
            nc.vector.tensor_copy(g.key[:, :], rec[:, :, 0])
            nc.vector.tensor_copy(nbr[:, :], rec[:, :, 1]).then_inc(keyed, 1)
    a.close()
    segments(nc, k, d, g, "src")

    a = Pool2(nc, "lay_deg")
    step = a.sem("step")
    with nc.Block() as block:
        @block.vector
        def _(v):
            st = Steps(v, step)
            st.did(nc.vector.tensor_tensor_scan(inv_deg[:, :], g.cont[:, :], k.ones[:, 0:T], 0.0, ALU.mult, ALU.add))
            st.did(nc.vector.tensor_tensor(joins_w[:, 0:1], g.joins[:, :], g.whole[:, :], ALU.mult))
            st.settle()
            st.did(nc.vector.tensor_scalar(joins_w[:, 1:C], k.ones[:, 1:C], joins_w[:, 0:1], None, ALU.mult))
            st.did(nc.vector.tensor_scalar(joins_c[:, :], k.ones[:, 0:C], g.joins[:, 0:1], None, ALU.mult))
            st.did(nc.vector.tensor_scalar(tail[:, :], k.ones[:, 0:C], inv_deg[:, T - 1:T], None, ALU.mult))
            st.settle()
    a.close()
    hand_over(nc, k, "deg", C, tail[:, :], carry[:, :], ALU.add, joins_w[:, :])
    a = Pool2(nc, "lay_inv")
    step = a.sem("step")
    with nc.Block() as block:
        @block.vector
        def _(v):
            st = Steps(v, step)
            st.link(nc.vector.tensor_tensor(carry[:, :], carry[:, :], joins_c[:, :], ALU.mult))
            st.link(nc.vector.scalar_tensor_tensor(inv_deg[:, :], g.lead[:, :], carry[:, 0:1], inv_deg[:, :],
                                                   ALU.mult, ALU.add))
            st.link(nc.vector.reciprocal(inv_deg[:, :], inv_deg[:, :]))
            st.link(nc.vector.tensor_tensor(tmp[:, :], inv_deg[:, :], g.end_lead[:, :], ALU.mult))
            st.link(nc.vector.tensor_reduce(inv_row[:, :], tmp[:, :], AX, ALU.add))
    a.close()

    xt_rows = k.d_xt.rearrange("(a b) o -> a (b o)", b=XW)[0:d["N_PAD"], :]
    for layer in range(3):
        first = layer == 0
        width = XW if first else C
        table = xt_rows if first else k.d_z[layer - 1]
        z = k.d_z[layer]
        z_rows = z[0:d["E_PAD"], :].rearrange("(p t) c -> p t c", t=T)
        a = Pool2(nc, f"lay{layer}")
        idx = [a.sb(f"idx{b}", [P, GROUP], I32) for b in two]
        got = [a.sb(f"got{b}", [P, GROUP, width]) for b in two]
        ends = a.sb("ends", [P, CH + 1, C])
        s = {n: a.sems(n) for n in ("idx", "gathered", "copied")}
        step, scaled, stored = a.sem("step"), a.sem("scaled"), a.sem("stored")
        with nc.Block() as block:
            @block.gpsimd
            def _(gp):
                with gp.Fori(0, N) as i:
                    for b in two:
                        gp.wait_ge(s["idx"][b], i + 1)
                        gp.wait_ge(s["copied"][b], i)
                        gp.sem_inc(a.passed("pool"), 1)
                        for q in range(GROUP):
                            gp.indirect_dma_start(out=got[b][:, q, :], out_offset=None, in_=table,
                                                  in_offset=bass.IndirectOffsetOnAxis(ap=idx[b][:, q:q + 1], axis=0),
                                                  ).then_inc(s["gathered"][b], 16)

            @block.scalar
            def _(act):

                def indices(b, n):
                    at = n * 2 * GROUP + b * GROUP
                    act.wait_ge(s["gathered"][b], n * GROUP * 16)
                    act.sem_inc(a.passed("act"), 1)
                    nc.scalar.activation(idx[b][:, :], nbr[:, bass.ds(at, GROUP)], ACT.Copy).then_inc(s["idx"][b], 1)

                def copy(b, n):
                    at = n * 2 * GROUP + b * GROUP
                    act.wait_ge(s["gathered"][b], n * GROUP * 16 + GROUP * 16)
                    act.sem_inc(a.passed("act"), 1)
                    nc.scalar.activation(G[:, bass.ds(at, GROUP), 0:width], got[b][:, :, :], ACT.Copy)\
                        .then_inc(s["copied"][b], 1)

                for b in two:
                    indices(b, 0)
                with act.Fori(0, N - 1) as i:
                    for b in two:
                        indices(b, i + 1)
                        copy(b, i)
                for b in two:
                    copy(b, N - 1)

            @block.vector
            def _(v):
                st = Steps(v, step)
                st.did(nc.vector.memset(ends[:, 0, :], 0.0))
                for c in range(CH):
                    lo = c * TC
                    groups = (c + 1) * TC // GROUP
                    for b in two:
                        v.wait_ge(s["copied"][b], (groups + 1 - b) // 2)
                    st.settle()
                    with v.Fori(0, C // 4) as f:
                        for q in range(4):
                            col = G[:, lo:lo + TC, bass.ds(f * 4 + q, 1)].rearrange("p t o -> p (t o)")
                            nc.vector.tensor_tensor_scan(col, g.cont[:, lo:lo + TC], col, ends[:, c, bass.ds(f * 4 + q, 1)],
                                                         ALU.mult, ALU.add)
                    st.link(nc.vector.memset(tmp[:, 0:1], 0.0))
                    st.link(nc.vector.tensor_copy(ends[:, c + 1, :], G[:, lo + TC - 1, 0:C]))
                    nc.vector.tensor_tensor(G[:, lo:lo + TC, 0:C], G[:, lo:lo + TC, 0:C],
                                            inv_deg[:, lo:lo + TC].unsqueeze(2).to_broadcast([P, TC, C]), ALU.mult)\
                        .then_inc(scaled, 1)
                nc.vector.tensor_copy(tail[:, :], ends[:, CH, :])
                if first:
                    nc.vector.tensor_copy(nbr[:, :], G[:, :, C])

            @block.sync
            def _(sp):
                for c in range(CH):
                    sp.wait_ge(scaled, c + 1)
                    sp.dma_start(z_rows[:, c * TC:(c + 1) * TC, :], G[:, c * TC:(c + 1) * TC, 0:C])\
                        .then_inc(stored, 16)
                sp.wait_ge(stored, 16 * CH)
        a.close()
        hand_over(nc, k, f"lay{layer}", C, tail[:, :], carry[:, :], ALU.add, joins_w[:, :])
        a = Pool2(nc, f"fix{layer}")
        row = a.sb("row", [P, C])
        got, step, done = a.sem("got"), a.sem("step"), a.sem("done")
        with nc.Block() as block:
            @block.gpsimd
            def _(gp):
                gp.indirect_dma_start(out=row[:, :], out_offset=None, in_=z[0:d["E_PAD"], :],
                                      in_offset=bass.IndirectOffsetOnAxis(ap=g.row[:, 0:1], axis=0)).then_inc(got, 16)
                gp.wait_ge(step, 3)
                gp.sem_inc(a.passed("pool"), 1)
                gp.indirect_dma_start(out=z, out_offset=bass.IndirectOffsetOnAxis(ap=g.row[:, 0:1], axis=0),
                                      in_=row[:, :], in_offset=None).then_inc(done, 16)
                gp.wait_ge(done, 16)

            @block.vector
            def _(v):
                st = Steps(v, step)
                st.link(nc.vector.tensor_tensor(carry[:, :], carry[:, :], joins_c[:, :], ALU.mult))
                st.link(nc.vector.tensor_scalar(carry[:, :], carry[:, :], inv_row[:, 0:1], None, ALU.mult))
                v.wait_ge(got, 16)
                st.did(nc.vector.tensor_tensor(row[:, :], row[:, :], carry[:, :], ALU.add))
        a.close()

    a = Pool2(nc, "sums")
    zin = [[a.sb(f"z{b}{n}", [P, GROUP, C]) for n in range(3)] for b in two]
    idx = [a.sb(f"idx{b}", [P, GROUP], I32) for b in two]
    s = {n: a.sems(n) for n in ("in", "part", "sum", "scattered")}
    with nc.Block() as block:
        @block.sync
        def _(sp):
            with sp.Fori(0, N) as i:
                for b in two:
                    at = i * 2 * GROUP + b * GROUP
                    sp.wait_ge(s["scattered"][b], i * GROUP * 16)
                    sp.sem_inc(a.passed("sp"), 1)
                    for n in range(3):
                        rows = k.d_z[n][0:d["E_PAD"], :].rearrange("(p t) c -> p t c", t=T)
                        sp.dma_start(zin[b][n][:, :, :], rows[:, bass.ds(at, GROUP), :]).then_inc(s["in"][b], 16)

        @block.vector
        def _(v):
            with v.Fori(0, N) as i:
                for b in two:
                    at = i * 2 * GROUP + b * GROUP
                    z0, z1, z2 = (zin[b][n][:, :, :] for n in range(3))
                    v.wait_ge(s["in"][b], i * 48 + 48)
                    nc.vector.tensor_tensor(z0, z0, z1, ALU.add).then_inc(s["part"][b], 1)
                    v.wait_ge(s["part"][b], i + 1)
                    nc.vector.tensor_scalar(idx[b][:, :], g.at[:, bass.ds(at, GROUP)], 1.0, None, ALU.mult)
                    nc.vector.tensor_tensor(z0, z0, z2, ALU.add).then_inc(s["sum"][b], 1)

        @block.gpsimd
        def _(gp):
            with gp.Fori(0, N) as i:
                for b in two:
                    gp.wait_ge(s["sum"][b], i + 1)
                    gp.sem_inc(a.passed("pool"), 1)
                    for q in range(GROUP):
                        gp.indirect_dma_start(out=k.d_acc,
                                              out_offset=bass.IndirectOffsetOnAxis(ap=idx[b][:, q:q + 1], axis=0),
                                              in_=zin[b][0][:, q, :], in_offset=None).then_inc(s["scattered"][b], 16)
            for b in two:
                gp.wait_ge(s["scattered"][b], N * GROUP * 16)
    a.close()
    m.close()


def build(nc, d, io):
    k = Pool2(nc, "k")
    N_PAD, E_PAD, T = d["N_PAD"], d["E_PAD"], d["T"]
    k.d_xt = nc.dram_tensor("node_table", ((N_PAD + E_PAD) * XW, 1), F32).ap()
    k.d_acc = nc.dram_tensor("layer_sums", (N_PAD + E_PAD, C), F32).ap()
    k.d_z = [nc.dram_tensor(f"layer_{n}", (E_PAD + P, C), F32).ap() for n in range(3)]
    k.d_last = nc.dram_tensor("last_place", (d["HP"], KEYS_PER_PART), F32).ap()
    k.d_pay_given = nc.dram_tensor("payload_given", (E_PAD, PAY), F32).ap()
    k.d_pay_sorted = nc.dram_tensor("payload_sorted", (E_PAD, PAY), F32).ap()
    k.d_pay_rows = k.d_pay_sorted.rearrange("(p t) c -> p t c", t=T)
    k.d_rec_sorted = nc.dram_tensor("edges_sorted", (E_PAD, 2), I32).ap()
    setup(nc, k, d, io)
    edges_and_nodes(nc, k, d, io)
    unsorted = nc.values_load(k.unsorted[0:1, 0:1], min_val=0, max_val=1)
    with nc.If(unsorted > 0):
        sort_payload(nc, k, d, io)
    place_phase(nc, k, d, "src", io['rec'], 2, I32, k.d_rec_sorted)
    attention(nc, k, d, io)
    layers(nc, k, d, io)
    final_nodes(nc, k, d, io)
    k.close()


_WEIGHTS = ("Wq", "bq", "W_src", "b_src", "W_dst", "W_fc1", "b_fc1", "W_fc2", "b_fc2", "W_fc3", "b_fc3",
            "W_kv", "b_kv", "W_proj", "b_proj")


def dims(n_nodes, n_edges):
    unit = KEYS_PER_PART * P // 128
    hp = -(-(n_nodes + 1) // unit)
    while (hp * KEYS_PER_PART) % (P * 28) or (hp * KEYS_PER_PART // P) % 56:
        hp += 1
    t = -(-n_edges // P)
    t = -(-t // 56) * 56
    n_pad = hp * KEYS_PER_PART
    return {"N": n_nodes, "E": n_edges, "HP": hp, "N_PAD": n_pad, "T": t, "E_PAD": t * P, "S": t // GROUP,
            "R": n_pad // P, "J": 28}


def layout(inputs, d):
    import numpy as np
    x = np.asarray(inputs["x"])
    xp = np.zeros((d["N_PAD"], C), x.dtype)
    xp[:d["N"]] = x
    arrays = {"x": xp}
    pads = {}
    for key in ("src", "dst"):
        e = np.full((d["E_PAD"],), d["N"], np.int32)
        e[:d["E"]] = np.asarray(inputs[key])
        pads[key] = e.reshape(P, d["T"])
        arrays[f"{key}_pt"] = pads[key]
        arrays[f"{key}_tp"] = np.ascontiguousarray(pads[key].T).reshape(d["S"], GE)
    arrays["rec"] = np.ascontiguousarray(np.stack([pads["src"], pads["dst"]], axis=-1))
    ea = np.zeros((d["E_PAD"], C), x.dtype)
    ea[:d["E"]] = np.asarray(inputs["edge_attr_64"])
    arrays["ea"] = np.ascontiguousarray(
        ea.reshape(P, d["S"] // 2, 2, GROUP, C).transpose(1, 2, 4, 3, 0)).reshape(d["S"] // 2, P, GE)
    ew = np.zeros((d["E_PAD"],), x.dtype)
    ew[:d["E"]] = np.asarray(inputs["edge_weight1"])[:, 0]
    arrays["ew"] = ew.reshape(P, d["T"])
    for w in _WEIGHTS:
        arrays[w] = np.ascontiguousarray(np.asarray(inputs[f"L0_gnn_{w}"]))
    return arrays


def kernel(**inputs):
    import concourse.bacc as _bacc
    from concourse import mybir as _mybir
    from concourse.bass_utils import run_bass_kernel_spmd as _run

    d = dims(inputs["x"].shape[0], inputs["src"].shape[0])
    arrays = layout(inputs, d)
    nc = _bacc.Bacc("TRN2", target_bir_lowering=False, num_devices=1)
    io = {n: nc.dram_tensor(f"in_{n}", a.shape, _mybir.dt.from_np(a.dtype), kind="ExternalInput").ap()
          for n, a in arrays.items()}
    io["out"] = nc.dram_tensor("out_rows", (d["N_PAD"], C), F32, kind="ExternalOutput").ap()
    build(nc, d, io)
    r = _run(nc, [{f"in_{n}": a for n, a in arrays.items()}], core_ids=[0])
    return r.results[0]["out_rows"][:d["N"]]
```

```python
import concourse.bass as bass
from concourse import mybir
from contextlib import ExitStack

F32, F16, I32 = mybir.dt.float32, mybir.dt.float16, mybir.dt.int32
ALU = mybir.AluOpType
ACT = mybir.ActivationFunctionType
AX = mybir.AxisListType.X

P = 128
C = 64
HEADS, HD = 4, 16
GROUP = 4
GE = GROUP * P
LO = 256
BLK = 4
KEYS_PER_PART = BLK * LO
PAY = 136
V_W = 69
XD = 72
XW = 65
EPS = 1e-5
BIG = 1e37


class Pool2:

    def __init__(self, nc, tag):
        self.nc, self.tag, self.stack, self.marks = nc, tag, ExitStack(), {}
        self.counters = []

    def sb(self, name, shape, dt=F32):
        return self.stack.enter_context(self.nc.sbuf_tensor(f"{self.tag}_{name}", shape, dt))

    def ps(self, name, shape, dt=F32):
        return self.stack.enter_context(self.nc.psum_tensor(f"{self.tag}_{name}", shape, dt))

    def sem(self, name):
        self.counters.append(self.nc.alloc_semaphore(f"{self.tag}_{name}"))
        return self.counters[-1]

    def sems(self, name, n=2):
        return [self.sem(f"{name}{k}") for k in range(n)]

    def passed(self, engine):
        if engine not in self.marks:
            self.marks[engine] = self.sem(f"passed_{engine}")
        return self.marks[engine]

    def close(self):
        self.stack.close()
        if self.counters:
            self.nc.clear_and_free_semaphores(self.counters)
            self.nc.all_engine_barrier()


class Steps:

    def __init__(self, eng, sem, base=0):
        self.eng, self.sem, self.base, self.n = eng, sem, base, 0

    def did(self, ins):
        ins.then_inc(self.sem, 1)
        self.n += 1

    def settle(self):
        self.eng.wait_ge(self.sem, self.base + self.n)

    def link(self, ins):
        self.did(ins)
        self.settle()


def need(eng, sem, value):
    if not (isinstance(value, int) and value == 0):
        eng.wait_ge(sem, value)


def repeat(eng, n, body):
    body(0)
    if n > 1:
        with eng.Fori(1, n) as i:
            body(i)


def setup(nc, k, d, io):
    T, HP, S = d["T"], d["HP"], d["S"]
    k.ident = k.sb("ident", [P, P])
    k.iota_lo = k.sb("iota_lo", [P, LO], F16)
    k.iota_hi = k.sb("iota_hi", [P, BLK, HP], F16)
    k.hi_of_part = k.sb("hi_of_part", [P, BLK])
    k.below = k.sb("below", [P, P])
    k.earlier = k.sb("earlier", [P, GE], F16)
    k.ones = k.sb("ones", [P, KEYS_PER_PART])
    k.place = k.sb("place", [P, T])
    k.w_kvx = k.sb("w_kvx", [P, 2, P])
    k.w_out = k.sb("w_out", [P, 2, 3 * C])
    k.w_fc = k.sb("w_fc", [P, 3, P])
    k.w_proj = k.sb("w_proj", [C + 1, C])
    k.b_col = k.sb("b_col", [P, 4])
    k.b_kv = k.sb("b_kv", [P, 2 * C])
    k.b_q = k.sb("b_q", [P, GROUP, C])
    k.b_proj = k.sb("b_proj", [P, 1, C])
    k.key = {key: k.sb(f"key_{key}", [P, T]) for key in ("dst", "src")}
    k.ew = k.sb("ew", [P, T])
    k.unsorted = k.sb("unsorted", [1, 1], I32)
    k.digits = {}

    t = Pool2(nc, "setup")
    ki = t.sb("ki", [P, 2, T], I32)
    drop = t.sb("drop", [P, T])
    after = t.sb("after", [P, 1])
    drops = t.sb("drops", [P, 4])
    tri = t.sb("tri", [P, P])
    ps = t.ps("ps", [P, 8])
    loaded, wl, made, v_step, shifted, keyed, counted, summed = (
        t.sem(n) for n in ("loaded", "weights", "made", "v_step", "shifted", "keyed", "counted", "summed"))
    n_weights = 1 + 4 + 4 + 6 + 2 + 8 + 1 + GROUP + 1
    with nc.Block() as block:
        @block.sync
        def _(sp):
            for n, key in enumerate(("dst", "src")):
                sp.dma_start(ki[:, n, :], io[f"{key}_pt"]).then_inc(loaded, 16)
            sp.dma_start(k.ew[:, :], io["ew"]).then_inc(wl, 16)
            sp.wait_ge(made, 1)
            up, low = slice(0, C), slice(C, P)
            for w, to in (("W_src", k.w_kvx[up, 0, 0:C]), ("W_dst", k.w_kvx[low, 0, 0:C]),
                          ("W_dst", k.w_kvx[up, 1, C:P]), ("W_src", k.w_kvx[low, 1, C:P]),
                          ("W_kv", k.w_out[up, 0, 0:2 * C]), ("Wq", k.w_out[low, 0, 2 * C:3 * C]),
                          ("W_kv", k.w_out[low, 1, 0:2 * C]), ("Wq", k.w_out[up, 1, 2 * C:3 * C])):
                sp.dma_start(to, io[w]).then_inc(wl, 16)
            for n in range(3):
                for half in (up, low):
                    sp.dma_start(k.w_fc[half, n, half], io[f"W_fc{n + 1}"]).then_inc(wl, 16)
            sp.dma_start(k.w_proj[0:C, :], io["W_proj"]).then_inc(wl, 16)
            sp.dma_start(k.w_proj[C:C + 1, :], io["b_proj"].rearrange("(o c) -> o c", o=1)).then_inc(wl, 16)
            with nc.allow_non_contiguous_dma(reason="one bias or key per partition"):
                for n, b in enumerate(("b_fc1", "b_fc2", "b_fc3", "b_src")):
                    for half in (up, low):
                        sp.dma_start(k.b_col[half, n:n + 1], io[b].rearrange("(c o) -> c o", o=1)).then_inc(wl, 16)
                sp.wait_ge(keyed, 1)
                sp.dma_start(after[0:P - 1, :], k.key["dst"][1:P, 0:1]).then_inc(shifted, 16)
            sp.dma_start(k.b_kv[:, :], io["b_kv"].partition_broadcast(P)).then_inc(wl, 16)
            for g in range(GROUP):
                sp.dma_start(k.b_q[:, g, :], io["bq"].partition_broadcast(P)).then_inc(wl, 16)
            sp.dma_start(k.b_proj[:, 0, :], io["b_proj"].partition_broadcast(P)).then_inc(wl, 16)

        @block.gpsimd
        def _(g):
            nc.gpsimd.memset(k.w_kvx[:, :, :], 0.0)
            nc.gpsimd.memset(k.w_fc[:, :, :], 0.0)
            nc.gpsimd.memset(k.w_out[:, :, :], 0.0).then_inc(made, 1)
            nc.gpsimd.memset(k.ident[:, :], 0.0)
            nc.gpsimd.memset(k.ones[:, :], 1.0)
            nc.gpsimd.memset(tri[:, :], 1.0).then_inc(made, 1)
            nc.gpsimd.iota(k.iota_lo[:, :], pattern=[[1, LO]], base=0, channel_multiplier=0,
                           allow_small_or_imprecise_dtypes=True)
            nc.gpsimd.iota(k.iota_hi[:, :, :], pattern=[[1, BLK], [BLK, HP]], base=0, channel_multiplier=0,
                           allow_small_or_imprecise_dtypes=True)
            nc.gpsimd.iota(k.hi_of_part[:, :], pattern=[[1, BLK]], base=0, channel_multiplier=BLK,
                           allow_small_or_imprecise_dtypes=True)
            nc.gpsimd.iota(k.place[:, :], pattern=[[1, T]], base=0, channel_multiplier=T,
                           allow_small_or_imprecise_dtypes=True)
            nc.gpsimd.memset(k.earlier[:, :], 1.0).then_inc(made, 1)
            g.wait_ge(made, 3)
            nc.gpsimd.affine_select(out=k.ident[:, :], in_=k.ident[:, :], compare_op=ALU.not_equal, fill=1.0,
                                    base=0, pattern=[[-1, P]], channel_multiplier=1)
            nc.gpsimd.affine_select(out=k.below[:, :], in_=tri[:, :], compare_op=ALU.is_gt, fill=0.0,
                                    base=0, pattern=[[1, P]], channel_multiplier=-1)
            last = k.earlier[:, GE - P:GE]
            nc.gpsimd.affine_select(out=last, in_=last, compare_op=ALU.is_gt, fill=0.0,
                                    base=0, pattern=[[-1, P]], channel_multiplier=1).then_inc(made, 1)

        @block.tensor
        def _(pe):
            pe.wait_ge(counted, 1)
            pe.wait_ge(made, 3)
            nc.tensor.matmul(ps[0:1, 0:4], k.ones[:, 0:1], drops[:, :], start=True, stop=True).then_inc(summed, 1)

        @block.vector
        def _(v):
            st = Steps(v, v_step)
            nc.vector.memset(after[:, :], float(d["N_PAD"]))
            nc.vector.memset(drops[:, :], 0.0)
            v.wait_ge(loaded, 32)
            nc.vector.tensor_copy(k.key["src"][:, :], ki[:, 1, :])
            nc.vector.tensor_copy(k.key["dst"][:, :], ki[:, 0, :]).then_inc(keyed, 1)
            v.wait_ge(keyed, 1)
            key = k.key["dst"]
            st.did(nc.vector.tensor_tensor(drop[:, 1:T], key[:, 0:T - 1], key[:, 1:T], ALU.is_gt))
            v.wait_ge(shifted, 16)
            st.link(nc.vector.tensor_tensor(drop[:, 0:1], key[:, T - 1:T], after[:, :], ALU.is_gt))
            nc.vector.tensor_reduce(drops[:, 0:1], drop[:, :], AX, ALU.add).then_inc(counted, 1)
            v.wait_ge(summed, 1)
            st.link(nc.vector.tensor_scalar(k.unsorted[:, :], ps[0:1, 0:1], 1.0, None, ALU.min))
            v.wait_ge(wl, 16 * n_weights)
            for half, n in ((slice(C, P), 0), (slice(0, C), 1)):
                wq = k.w_out[half, n, 2 * C:3 * C]
                nc.vector.tensor_scalar(wq, wq, HD ** -0.5, None, ALU.mult)
            st.link(nc.vector.tensor_scalar(k.b_q[:, :, :], k.b_q[:, :, :], HD ** -0.5, None, ALU.mult))
    t.close()
    digits(nc, k, k, d, io, "src")


class Digits:

    def __init__(self, nc, m, d, key):
        self.hi, self.lo = m.sb(f"hi_{key}", [P, d["T"]]), m.sb(f"lo_{key}", [P, d["T"]])
        self.start_hi = m.sb(f"start_hi_{key}", [d["HP"], KEYS_PER_PART], F16)
        self.start_lo = m.sb(f"start_lo_{key}", [d["HP"], KEYS_PER_PART], F16)
        self.hi_rows = nc.dram_tensor(f"hi_rows_{key}", (d["S"], GE), F16).ap()
        self.key_rows = nc.dram_tensor(f"key_rows_{key}", (d["S"], GE), F32).ap()


def digits(nc, k, m, d, io, key):
    T, S = d["T"], d["S"]
    k.digits[key] = g = Digits(nc, m, d, key)
    t = Pool2(nc, f"dig_{key}")
    ki = t.sb("ki", [P, T], I32)
    ti = t.sb("ti", [S, GE], I32)
    dig = t.sb("dig", [P, 2, T], I32)
    tdig = t.sb("tdig", [S, GE], I32)
    hi16 = t.sb("hi16", [S, GE], F16)
    kf = t.sb("kf", [S, GE])
    loaded, step, stored = t.sem("loaded"), t.sem("step"), t.sem("stored")
    with nc.Block() as block:
        @block.sync
        def _(sp):
            sp.dma_start(ki[:, :], io[f"{key}_pt"]).then_inc(loaded, 16)
            sp.dma_start(ti[:, :], io[f"{key}_tp"]).then_inc(loaded, 16)
            sp.wait_ge(step, 2)
            sp.dma_start(g.hi_rows, hi16[:, :]).then_inc(stored, 16)
            sp.dma_start(g.key_rows, kf[:, :]).then_inc(stored, 16)
            sp.wait_ge(stored, 32)

        @block.vector
        def _(v):
            st = Steps(v, step)
            v.wait_ge(loaded, 32)
            nc.vector.tensor_scalar(dig[:, 0, :], ki[:, :], 8, None, ALU.logical_shift_right)
            nc.vector.tensor_copy(kf[:, :], ti[:, :])
            nc.vector.tensor_scalar(dig[:, 1, :], ki[:, :], LO - 1, None, ALU.bitwise_and)
            st.link(nc.vector.tensor_scalar(tdig[:, :], ti[:, :], 8, None, ALU.logical_shift_right))
            st.link(nc.vector.tensor_copy(hi16[:, :], tdig[:, :]))
            nc.vector.tensor_copy(g.hi[:, :], dig[:, 0, :])
            nc.vector.tensor_copy(g.lo[:, :], dig[:, 1, :])
    t.close()


def one_hots(nc, k, g, at, lo_out, hi_out):
    nc.vector.tensor_scalar(lo_out, k.iota_lo[:, :], g.lo[:, bass.ds(at, 1)], None, ALU.is_equal)
    return nc.vector.tensor_scalar(hi_out, k.iota_hi[:, :, :], g.hi[:, bass.ds(at, 1)], None, ALU.is_equal)


class Counting:

    H = 14

    def __init__(self, nc, k, t, d, key):
        self.nc, self.k, self.g = nc, k, k.digits[key]
        self.lo1 = t.sb("count_lo", [P, self.H, LO], F16)
        self.hi1 = t.sb("count_hi", [P, self.H, BLK, d["HP"]], F16)
        self.table = t.ps("table", [d["HP"], KEYS_PER_PART])
        self.hot, self.used = t.sem("count_hot"), t.sem("count_used")

    def vector(self, v, i):
        for j in range(self.H):
            if not isinstance(i, int) or i > 0:
                v.wait_ge(self.used, i * self.H + (j + 1 - self.H))
            one_hots(self.nc, self.k, self.g, i * self.H + j, self.lo1[:, j, :], self.hi1[:, j, :, :])\
                .then_inc(self.hot, 1)

    def tensor(self, pe, i, lo, hi):
        for j in range(lo, hi):
            pe.wait_ge(self.hot, i * self.H + j + 1)
            for q in range(BLK):
                ins = self.nc.tensor.matmul(self.table[:, q * LO:(q + 1) * LO], self.hi1[:, j, q, :],
                                            self.lo1[:, j, :], start=False, stop=False, skip_group_check=True)
            ins.then_inc(self.used, 1)


def first_places(nc, k, t, d, key, counts, store_last):
    HP = d["HP"]
    g = k.digits[key]
    base = t.ps("base", [HP, 8])
    count = t.sb("count", [HP, KEYS_PER_PART])
    run = t.sb("run", [HP, KEYS_PER_PART])
    start = t.sb("start", [HP, KEYS_PER_PART])
    off = t.sb("off", [HP, 8])
    totals, based, step, last_ready, out_s = (t.sem(n) for n in ("totals", "based", "step", "last_ready", "out"))
    with nc.Block() as block:
        @block.vector
        def _(v):
            st = Steps(v, step)
            nc.vector.memset(off[:, :], 0.0)
            st.link(nc.vector.tensor_copy(count[:, :], counts[:, :]))
            st.link(nc.vector.tensor_tensor_scan(run[:, :], k.ones[0:HP, :], count[:, :], 0.0, ALU.mult, ALU.add))
            nc.vector.tensor_copy(off[:, 0:1], run[:, KEYS_PER_PART - 1:KEYS_PER_PART]).then_inc(totals, 1)
            st.did(nc.vector.tensor_tensor(start[:, :], run[:, :], count[:, :], ALU.subtract))
            v.wait_ge(based, 1)
            st.link(nc.vector.tensor_copy(off[:, 1:2], base[:, 0:1]))
            st.link(nc.vector.tensor_scalar(start[:, :], start[:, :], off[:, 1:2], None, ALU.add))
            st.link(nc.vector.tensor_copy(g.start_hi[:, :], start[:, :]))
            st.link(nc.vector.tensor_tensor(g.start_lo[:, :], start[:, :], g.start_hi[:, :], ALU.subtract))
            if store_last:
                st.link(nc.vector.tensor_tensor(run[:, :], start[:, :], count[:, :], ALU.add))
                st.link(nc.vector.tensor_scalar(count[:, :], count[:, :], 1.0, None, ALU.min))
                st.link(nc.vector.scalar_tensor_tensor(run[:, :], run[:, :], -1.0 - d["E_PAD"], count[:, :],
                                                       ALU.add, ALU.mult))
                nc.vector.tensor_scalar(run[:, :], run[:, :], float(d["E_PAD"]), None, ALU.add)\
                    .then_inc(last_ready, 1)

        @block.tensor
        def _(pe):
            pe.wait_ge(totals, 1)
            nc.tensor.matmul(base[:, 0:1], k.below[0:HP, 0:HP], off[:, 0:1], start=True, stop=True)\
                .then_inc(based, 1)

        @block.sync
        def _(sp):
            if store_last:
                sp.wait_ge(last_ready, 1)
                sp.dma_start(k.d_last, run[:, :]).then_inc(out_s, 16)
                sp.wait_ge(out_s, 16)


class Messages:

    def __init__(self, nc, k, t, d, io):
        two = range(2)
        self.nc, self.k, self.t, self.io, self.N = nc, k, t, io, d["S"] // 2
        self.idx = [t.sb(f"idx{b}", [P, 2, GROUP], I32) for b in two]
        self.xg = [t.sb(f"xg{b}", [P, GROUP, 2 * C]) for b in two]
        self.xt = [t.sb(f"xt{b}", [P, GE]) for b in two]
        self.ea = t.sb("ea", [P, GE])
        self.h1, self.h2, self.w3 = (t.sb(n, [P, GE]) for n in ("h1", "h2", "w3"))
        self.pay = [t.sb(f"pay{b}", [P, GROUP, C + XD]) for b in two]
        self.qb = [t.sb(f"qb{b}", [P, GROUP, C]) for b in two]
        self.ps_x = [t.ps(f"ps_x{b}", [P, GE]) for b in two]
        self.ps_e = t.ps("ps_e", [P, GE])
        self.ps_o = t.ps("ps_o", [P, 2, GE])
        self.s = {n: t.sems(n) for n in ("idx_in", "gathered", "xT", "xT_sb", "tp", "out_ps", "out_used",
                                         "step", "pay_ready", "stored", "x_stored")}
        self.e = {n: t.sem(n) for n in ("ea_in", "h1_ps", "h1_sb", "h2_ps", "h2_sb", "w_ps", "w_sb", "kv_ps")}
        self.init = t.sem("init")

    def src_half(self, b):
        return slice(0, C) if b == 0 else slice(C, P)

    def dst_half(self, b):
        return slice(C, P) if b == 0 else slice(0, C)

    def attributes(self, sp, i):
        need(sp, self.e["h1_ps"], i)
        sp.sem_inc(self.t.passed("sp"), 1)
        sp.dma_start(self.ea[:, :], self.io["ea"][bass.ds(i, 1), :, :].rearrange("a p e -> p (a e)"))\
            .then_inc(self.e["ea_in"], 16)

    def sync(self, sp, i, next):
        for b in range(2):
            at = i * 2 * GROUP + b * GROUP
            if not isinstance(i, int) or i > 0:
                self.store_x(sp, b, i - 1)
            for side, key in enumerate(("src", "dst") if b == 0 else ("dst", "src")):
                sp.dma_start(self.idx[b][:, side, :], self.io[f"{key}_pt"][:, bass.ds(at, GROUP)])\
                    .then_inc(self.s["idx_in"][b], 16)
        if next:
            self.attributes(sp, i + 1)

    def gpsimd(self, g, i):
        for b in range(2):
            g.wait_ge(self.s["idx_in"][b], i * 32 + 32)
            need(g, self.s["x_stored"][b], i * 16)
            need(g, self.s["xT"][b], i)
            g.sem_inc(self.t.passed("pool"), 1)
            for side in range(2):
                for q in range(GROUP):
                    g.indirect_dma_start(
                        out=self.xg[b][:, q, side * C:(side + 1) * C], out_offset=None, in_=self.io["x"],
                        in_offset=bass.IndirectOffsetOnAxis(ap=self.idx[b][:, side, q:q + 1], axis=0),
                    ).then_inc(self.s["gathered"][b], 16)

    def fc1(self, pe, i):
        pe.wait_ge(self.e["ea_in"], i * 16 + 16)
        need(pe, self.e["w_sb"], i)
        self.nc.tensor.matmul(self.ps_e[:, :], self.k.w_fc[:, 0, :], self.ea[:, :], start=True, stop=True)\
            .then_inc(self.e["h1_ps"], 1)

    def fc2(self, pe, i):
        pe.wait_ge(self.e["h1_sb"], i + 1)
        self.nc.tensor.matmul(self.ps_e[:, :], self.k.w_fc[:, 1, :], self.h1[:, :], start=True, stop=True)\
            .then_inc(self.e["h2_ps"], 1)

    def fc3(self, pe, i):
        pe.wait_ge(self.e["h2_sb"], i + 1)
        self.nc.tensor.matmul(self.ps_e[:, :], self.k.w_fc[:, 2, :], self.h2[:, :], start=True, stop=True)\
            .then_inc(self.e["w_ps"], 1)

    def turn(self, pe, b, i):
        pe.wait_ge(self.s["gathered"][b], i * 128 + 128)
        if b == 0:
            need(pe, self.s["tp"][1], i)
        for q in range(GROUP):
            ins = self.nc.tensor.transpose(self.ps_x[b][:, q * P:(q + 1) * P], self.xg[b][:, q, :],
                                           self.k.ident[:, :])
        ins.then_inc(self.s["xT"][b], 1)

    def kv(self, pe, i):
        for b in range(2):
            pe.wait_ge(self.s["xT_sb"][b], i + 1)
            ins = self.nc.tensor.matmul(self.ps_x[0][:, :], self.k.w_kvx[:, b, :], self.xt[b][:, :], start=(b == 0),
                                        stop=(b == 1))
        ins.then_inc(self.e["kv_ps"], 1)

    def outputs(self, pe, b, i):
        pe.wait_ge(self.s["tp"][b], i + 1)
        if b == 0:
            need(pe, self.s["out_used"][1], i)
        else:
            pe.wait_ge(self.s["out_used"][0], i + 1)
        for q in range(GROUP):
            ins = self.nc.tensor.matmul(self.out_tile(q, 0, 3 * C), self.xt[b][:, q * P:(q + 1) * P],
                                        self.k.w_out[:, b, :], start=True, stop=True)
        ins.then_inc(self.s["out_ps"][b], 1)

    def tensor(self, pe, i, next, fill):
        self.turn(pe, 0, i)
        fill(0)
        self.turn(pe, 1, i)
        if next:
            self.fc1(pe, i + 1)
        self.kv(pe, i)
        fill(1)
        self.outputs(pe, 0, i)
        if next:
            self.fc2(pe, i + 1)
        fill(2)
        self.outputs(pe, 1, i)
        if next:
            self.fc3(pe, i + 1)

    def out_tile(self, q, lo, hi):
        return self.ps_o[:, q // 2, (q % 2) * 3 * C + lo:(q % 2) * 3 * C + hi]

    def store(self, act, i):
        for b in range(2):
            at = i * 2 * GROUP + b * GROUP
            act.wait_ge(self.s["pay_ready"][b], i + 1)
            act.sem_inc(self.t.passed("act"), 1)
            act.dma_start(self.k.d_pay_rows[:, bass.ds(at, GROUP), 0:XD], self.pay[b][:, :, C:])\
                .then_inc(self.s["stored"][b], 16)
            act.dma_start(self.k.values[:, bass.ds(at, GROUP), :], self.pay[b][:, :, C:C + V_W])\
                .then_inc(self.s["stored"][b], 16)

    def store_x(self, sp, b, i):
        sp.wait_ge(self.s["gathered"][b], i * 128 + 128)
        sp.sem_inc(self.t.passed("sp"), 1)
        sp.dma_start(self.k.d_pay_rows[:, bass.ds(i * 2 * GROUP + b * GROUP, GROUP), XD:],
                     self.xg[b][:, :, self.dst_half(b)]).then_inc(self.s["x_stored"][b], 16)

    def silu(self, act, n, out, i):
        act.wait_ge(self.e[f"h{n}_ps"], i + 1)
        self.nc.scalar.activation(out[:, :], self.ps_e[:, :], ACT.Silu, bias=self.k.b_col[:, n - 1:n])\
            .then_inc(self.e[f"h{n}_sb"], 1)

    def filters(self, act, i):
        act.wait_ge(self.e["w_ps"], i + 1)
        need(act, self.s["tp"][1], i)
        self.nc.scalar.activation(self.w3[:, :], self.ps_e[:, :], ACT.Identity, bias=self.k.b_col[:, 2:3])\
            .then_inc(self.e["w_sb"], 1)

    def scalar(self, act, i, next, fill=None):
        for b in range(2):
            act.wait_ge(self.s["xT"][b], i + 1)
            need(act, self.s["out_ps"][b], i)
            self.nc.scalar.activation(self.xt[b][:, :], self.ps_x[b][:, :], ACT.Copy).then_inc(self.s["xT_sb"][b], 1)
        if not isinstance(i, int) or i > 0:
            self.store(act, i - 1)
        if next:
            self.silu(act, 1, self.h1, i + 1)
        if fill:
            fill(0)
        if next:
            self.silu(act, 2, self.h2, i + 1)
        if fill:
            fill(1)
        if next:
            self.filters(act, i + 1)

    def begin(self, sp=None, pe=None, act=None):
        if sp:
            self.attributes(sp, 0)
        if pe:
            self.fc1(pe, 0)
            self.fc2(pe, 0)
            self.fc3(pe, 0)
        if act:
            self.silu(act, 1, self.h1, 0)
            self.silu(act, 2, self.h2, 0)
            self.filters(act, 0)

    def multiply(self, v, i):
        v.wait_ge(self.e["kv_ps"], i + 1)
        v.wait_ge(self.e["w_sb"], i + 1)
        for b in range(2):
            half = self.src_half(b)
            self.nc.vector.scalar_tensor_tensor(self.xt[b][half, :], self.ps_x[0][half, :], self.k.b_col[half, 3:4],
                                                self.w3[half, :], ALU.add, ALU.mult).then_inc(self.s["tp"][b], 1)

    def payload(self, v, b, i):
        nc, k, s = self.nc, self.k, self.s
        st = Steps(v, s["step"][b], i)
        pay, qb = self.pay[b], self.qb[b]
        need(v, s["stored"][b], i * 32)
        nc.vector.tensor_scalar(pay[:, :, C + 68], k.key["dst"][:, bass.ds(i * 2 * GROUP + b * GROUP, GROUP)], 1.0,
                                None, ALU.mult)
        v.wait_ge(s["out_ps"][b], i + 1)
        for q in range(GROUP):
            at = i * 2 * GROUP + (b * GROUP + q)
            nc.vector.scalar_tensor_tensor(pay[:, q, 0:2 * C], self.out_tile(q, 0, 2 * C),
                                           k.ew[:, bass.ds(at, 1)], k.b_kv[:, :], ALU.mult, ALU.add)
        q_ps = self.ps_o[:, :, 0:6 * C].rearrange("p a (t c) -> p a t c", t=2)[:, :, :, 2 * C:3 * C]
        nc.vector.tensor_tensor(qb[:, :, :].rearrange("p (a t) c -> p a t c", t=2), q_ps,
                                k.b_q[:, :, :].rearrange("p (a t) c -> p a t c", t=2), ALU.add)\
            .then_inc(s["out_used"][b], 1)
        v.wait_ge(s["out_used"][b], i + 1)
        st.link(nc.vector.tensor_tensor(qb[:, :, :], qb[:, :, :], pay[:, :, 0:C], ALU.mult))
        nc.vector.tensor_reduce(pay[:, :, 2 * C:2 * C + HEADS],
                                qb[:, :, :].rearrange("p g (h c) -> p g h c", h=HEADS), AX, ALU.add)\
            .then_inc(s["pay_ready"][b], 1)


class FirstNodes:

    def __init__(self, nc, k, t, d, io, J):
        self.nc, self.k, self.t, self.J, self.R = nc, k, t, J, d["R"]
        self.x = t.sb("nodes_x", [P, J, C])
        self.cen = t.sb("nodes_cen", [P, J, C])
        self.sq = t.sb("nodes_sq", [P, J, C])
        self.res = t.sb("nodes_res", [P, J, XW])
        self.stat = t.sb("nodes_stat", [P, 4, J])
        self.eps = t.sb("nodes_eps", [P, 1])
        self.last = t.sb("nodes_last", [P, d["R"]])
        self.rows_in = io["x"].rearrange("(p r) c -> p r c", r=d["R"])
        self.rows_out = k.d_xt.rearrange("(a b) o -> a (b o)", b=XW)[0:d["N_PAD"], :]\
            .rearrange("(p r) c -> p r c", r=d["R"])
        (self.last_in, self.x_in, self.step, self.scale, self.centred, self.squared, self.dev, self.made,
         self.stored) = (t.sem(f"nodes_{n}") for n in ("last_in", "x_in", "step", "scale", "centred", "squared", "dev",
                                                       "made", "stored"))

    def load(self, act, n, at, rows):
        need(act, self.centred, n)
        act.sem_inc(self.t.passed("act"), 1)
        act.dma_start(self.x[:, 0:rows, :], self.rows_in[:, bass.ds(at, rows), :]).then_inc(self.x_in, 16)

    def mean(self, v, n, rows):
        nc, st = self.nc, Steps(v, self.step, n * 3)
        x, mean = self.x[:, 0:rows, :], self.stat[:, 0, 0:rows]
        v.wait_ge(self.x_in, n * 16 + 16)
        st.link(nc.vector.tensor_tensor(x, x, self.k.b_proj[:, :, :].to_broadcast([P, rows, C]), ALU.add))
        st.link(nc.vector.tensor_reduce(mean, x, AX, ALU.add))
        st.did(nc.vector.tensor_scalar(mean, mean, 1.0 / C, None, ALU.mult))

    def centre(self, v, n, rows):
        nc, x, mean = self.nc, self.x[:, 0:rows, :], self.stat[:, 0, 0:rows]
        v.wait_ge(self.step, n * 3 + 3)
        need(v, self.made, n)
        nc.vector.tensor_tensor(self.cen[:, 0:rows, :], x, mean.unsqueeze(2).to_broadcast([P, rows, C]),
                                ALU.subtract).then_inc(self.centred, 1)

    def squares(self, act, n, lo, hi):
        if lo == 0:
            act.wait_ge(self.centred, n + 1)
        for j in range(lo, hi):
            ins = self.nc.scalar.activation(self.sq[:, j, :], self.cen[:, j, :], ACT.Square,
                                            accum_out=self.stat[:, 1, j:j + 1])
        ins.then_inc(self.squared, 1)

    def deviation(self, act, n, rows):
        nc = self.nc
        act.wait_ge(self.squared, n * 2 + 2)
        nc.scalar.activation(self.stat[:, 2, 0:rows], self.stat[:, 1, 0:rows], ACT.Sqrt, bias=self.eps[:, 0:1],
                             scale=1.0 / C).then_inc(self.dev, 1)

    def finish(self, v, n, at, rows):
        nc, st = self.nc, Steps(v, self.scale, n)
        v.wait_ge(self.dev, n + 1)
        need(v, self.stored, n * 16)
        st.did(nc.vector.reciprocal(self.stat[:, 3, 0:rows], self.stat[:, 2, 0:rows]))
        nc.vector.tensor_scalar(self.res[:, 0:rows, C], self.last[:, bass.ds(at, rows)], 1.0, None, ALU.mult)
        st.settle()
        nc.vector.tensor_tensor(self.res[:, 0:rows, 0:C], self.cen[:, 0:rows, :],
                                self.stat[:, 3, 0:rows].unsqueeze(2).to_broadcast([P, rows, C]), ALU.mult)\
            .then_inc(self.made, 1)

    def store(self, act, n, at, rows):
        act.wait_ge(self.made, n + 1)
        act.sem_inc(self.t.passed("act"), 1)
        act.dma_start(self.rows_out[:, bass.ds(at, rows), :], self.res[:, 0:rows, :]).then_inc(self.stored, 16)


def edges_and_nodes(nc, k, d, io):
    T, R = d["T"], d["R"]
    t = Pool2(nc, "msg")
    m = Messages(nc, k, t, d, io)
    A = T // Counting.H
    B = m.N - A
    J = -(-R // B)
    J_last = R - (B - 1) * J
    c = Pool2(nc, "count")
    counting = Counting(nc, k, c, d, "src")
    zeroed, zero_s = c.sem("zeroed"), c.sem("zero")
    ZR = R // A
    zeros = c.sb("zeros", [P, max(ZR, R - A * ZR), C])
    acc_rows = k.d_acc[0:d["N_PAD"], :].rearrange("(p r) c -> p r c", r=R)
    with nc.Block() as block:
        @block.sync
        def _(sp):
            m.begin(sp=sp)
            sp.wait_ge(zeroed, 2)

            def body(i):
                m.sync(sp, i, True)
                sp.dma_start(acc_rows[:, bass.ds(i * ZR, ZR), :], zeros[:, 0:ZR, :]).then_inc(zero_s, 16)
            repeat(sp, A, body)
            if R > A * ZR:
                sp.dma_start(acc_rows[:, A * ZR:R, :], zeros[:, 0:R - A * ZR, :]).then_inc(zero_s, 16)
            for rows in (k.d_acc[d["N_PAD"]:d["SPARE"], :], *(z[d["E_PAD"]:d["E_PAD"] + P, :] for z in k.d_z)):
                sp.dma_start(rows, zeros[:, 0, :]).then_inc(zero_s, 16)
            sp.wait_ge(zero_s, 16 * (A + (R > A * ZR) + 1 + len(k.d_z)))

        @block.gpsimd
        def _(g):
            repeat(g, A, lambda i: m.gpsimd(g, i))

        @block.tensor
        def _(pe):
            pe.wait_ge(zeroed, 1)
            m.begin(pe=pe)
            cuts = (0, 5, 10, Counting.H)
            repeat(pe, A, lambda i: m.tensor(pe, i, True, lambda n: counting.tensor(pe, i, cuts[n], cuts[n + 1])))

        @block.scalar
        def _(act):
            m.begin(act=act)
            repeat(act, A, lambda i: m.scalar(act, i, True))

        @block.vector
        def _(v):
            nc.vector.memset(counting.table[:, :], 0.0).then_inc(zeroed, 1)
            for b in range(2):
                nc.vector.memset(m.pay[b][:, :, :], 0.0).then_inc(m.init, 1)
            v.wait_ge(m.init, 2)
            nc.vector.memset(zeros[:, :, :], 0.0).then_inc(zeroed, 1)

            def body(i):
                counting.vector(v, i)
                m.multiply(v, i)
                for b in range(2):
                    m.payload(v, b, i)

            repeat(v, A, body)
    first_places(nc, k, c, d, "src", counting.table, True)
    c.close()

    f = Pool2(nc, "nodes")
    nodes = FirstNodes(nc, k, f, d, io, J)
    init = f.sem("init")
    with nc.Block() as block:
        @block.sync
        def _(sp):
            sp.dma_start(nodes.last[:, :], k.d_last.rearrange("a b -> (a b)").rearrange("(p r) -> p r", r=R))\
                .then_inc(nodes.last_in, 16)

            with sp.Fori(A, m.N - 1) as i:
                m.sync(sp, i, True)
            m.sync(sp, m.N - 1, False)
            for b in range(2):
                m.store_x(sp, b, m.N - 1)
            for b in range(2):
                sp.wait_ge(m.s["x_stored"][b], 16 * m.N)

        @block.gpsimd
        def _(g):
            with g.Fori(A, m.N) as i:
                m.gpsimd(g, i)

        @block.tensor
        def _(pe):
            with pe.Fori(A, m.N - 1) as i:
                m.tensor(pe, i, True, lambda n: None)
            m.tensor(pe, m.N - 1, False, lambda n: None)

        @block.scalar
        def _(act):
            act.wait_ge(init, 1)

            def nodes_before(n, part, rows):
                if not isinstance(n, int) or n > 0:
                    if part == 0:
                        if not isinstance(n, int) or n > 1:
                            nodes.store(act, n - 2, (n - 2) * J, J)
                        nodes.load(act, n, n * J, rows)
                        nodes.squares(act, n - 1, 0, J // 2)
                    else:
                        nodes.squares(act, n - 1, J // 2, J)
                        nodes.deviation(act, n - 1, J)

            def body(n, rows=J, next=True):
                m.scalar(act, n + A, next, lambda part: nodes_before(n, part, rows))
            nodes.load(act, 0, 0, J)
            body(0)
            body(1)
            if B > 3:
                with act.Fori(2, B - 1) as n:
                    body(n)
            body(B - 1, J_last, False)
            m.store(act, m.N - 1)
            nodes.store(act, B - 2, (B - 2) * J, J)
            nodes.squares(act, B - 1, 0, J_last // 2)
            nodes.squares(act, B - 1, J_last // 2, J_last)
            nodes.deviation(act, B - 1, J_last)
            nodes.store(act, B - 1, (B - 1) * J, J_last)
            act.wait_ge(nodes.stored, 16 * B)
            for b in range(2):
                act.wait_ge(m.s["stored"][b], 32 * m.N)

        @block.vector
        def _(v):
            nc.vector.memset(nodes.eps[:, :], EPS).then_inc(init, 1)
            v.wait_ge(nodes.last_in, 16)

            def body(n, rows=J):
                m.multiply(v, n + A)
                for b in range(2):
                    m.payload(v, b, n + A)
                nodes.mean(v, n, rows)
                if not isinstance(n, int) or n > 0:
                    nodes.finish(v, n - 1, (n - 1) * J, J)
                nodes.centre(v, n, rows)
            repeat(v, B - 1, body)
            body(B - 1, J_last)
            nodes.finish(v, B - 1, (B - 1) * J, J_last)
    f.close()
    t.close()


class Placing:

    def __init__(self, nc, k, t, d, key, payload, width, dt, out):
        two = range(2)
        HP = d["HP"]
        self.nc, self.k, self.t, self.g, self.key = nc, k, t, k.digits[key], k.key[key]
        self.N, self.HP, self.payload, self.out = d["S"] // 2, HP, payload, out
        self.hi_b = [t.sb(f"hi_b{b}", [HP, GE], F16) for b in two]
        self.key_b = [t.sb(f"key_b{b}", [P, GE]) for b in two]
        self.pay = [t.sb(f"pay{b}", [P, GROUP, width], dt) for b in two]
        self.hi_t = [t.sb(f"hi_t{b}", [HP, BLK, GE], F16) for b in two]
        self.lo1 = [t.sb(f"lo1{b}", [P, GROUP, LO], F16) for b in two]
        self.hi1 = [t.sb(f"hi1{b}", [P, GROUP, BLK, HP], F16) for b in two]
        self.next = t.sb("next", [HP, KEYS_PER_PART], I32)
        self.low = [t.sb(f"low{b}", [HP, KEYS_PER_PART], F16) for b in two]
        self.high = [t.sb(f"high{b}", [HP, KEYS_PER_PART], F16) for b in two]
        self.same = t.sb("same", [P, GROUP, GE], F16)
        self.hit = t.sb("hit", [P, GROUP, LO], F16)
        self.rank = [t.sb(f"rank{b}", [P, GROUP]) for b in two]
        self.base = [t.sb(f"base{b}", [P, GROUP]) for b in two]
        self.pos = [t.sb(f"pos{b}", [P, GROUP], I32) for b in two]
        self.ident16 = t.sb("ident16", [P, P], F16)
        self.table = t.ps("place_table", [HP, KEYS_PER_PART])
        self.look = [t.ps(f"look{b}", [P, GROUP, LO]) for b in two]
        self.s = {n: t.sems(n) for n in ("rows_in", "pay_in", "prepared", "split", "updated", "looked", "reduced",
                                         "pos_ready", "scattered")}
        self.zeroed, self.started, self.whole = t.sem("zeroed"), t.sem("started"), t.sem("next_made")

    def load_digits(self, sp, b, i):
        s, g, at = self.s, self.g, i * 2 + b
        need(sp, s["prepared"][b], i)
        sp.sem_inc(self.t.passed("sp"), 1)
        sp.dma_start(self.hi_b[b][:, :], g.hi_rows[bass.ds(at, 1), :].to_broadcast([self.HP, GE]))\
            .then_inc(s["rows_in"][b], 16)
        sp.dma_start(self.key_b[b][:, :], g.key_rows[bass.ds(at, 1), :].to_broadcast([P, GE]))\
            .then_inc(s["rows_in"][b], 16)

    def load_payload(self, sp, b, i):
        need(sp, self.s["scattered"][b], i * GROUP * 16)
        sp.sem_inc(self.t.passed("sp"), 1)
        sp.dma_start(self.pay[b][:, :, :], self.payload[:, bass.ds(i * 2 * GROUP + b * GROUP, GROUP), :])\
            .then_inc(self.s["pay_in"][b], 16)

    def sync(self, sp, i, also=None):
        self.load_digits(sp, 0, i)
        if not isinstance(i, int) or i > 0:
            self.load_payload(sp, 1, i - 1)
        self.load_digits(sp, 1, i)
        if also:
            also(i)
        self.load_payload(sp, 0, i)

    def sync_last(self, sp):
        self.load_payload(sp, 1, self.N - 1)

    def scalar(self, act, b, n):
        s, nc = self.s, self.nc
        if b == 0:
            need(act, s["updated"][1], n)
            act.wait_ge(self.started, 1)
        else:
            act.wait_ge(s["updated"][0], n + 1)
        need(act, s["looked"][b], n)
        need(act, s["split"][1 - b], n + b)
        nc.scalar.activation(self.next[:, :], self.table[:, :], ACT.Copy).then_inc(self.whole, 1)
        act.wait_ge(self.whole, n * 2 + (b + 1))
        by = self.next[:, :].bitcast(mybir.dt.uint8).rearrange("p (c b) -> p c b", b=4)
        nc.scalar.activation(self.low[b][:, :], by[:, :, 0], ACT.Copy)
        nc.scalar.activation(self.high[b][:, :], by[:, :, 1], ACT.Copy, scale=256.0).then_inc(s["split"][b], 1)

    def begin(self, pe):
        pe.wait_ge(self.zeroed, 1)
        for half in (self.g.start_hi, self.g.start_lo):
            for q in range(0, KEYS_PER_PART, 512):
                ins = self.nc.tensor.matmul(self.table[:, q:q + 512], self.ident16[0:self.HP, 0:self.HP],
                                            half[:, q:q + 512], start=False, stop=False, skip_group_check=True)
        ins.then_inc(self.started, 1)

    def update(self, pe, b, n):
        s, nc = self.s, self.nc
        pe.wait_ge(s["prepared"][b], n + 1)
        pe.wait_ge(s["split"][b], n + 1)
        for g in range(GROUP):
            for q in range(BLK):
                ins = nc.tensor.matmul(self.table[:, q * LO:(q + 1) * LO], self.hi1[b][:, g, q, :],
                                       self.lo1[b][:, g, :], start=False, stop=False, skip_group_check=True)
        ins.then_inc(s["updated"][b], 1)

    def lookup(self, pe, b, n):
        s, nc = self.s, self.nc
        need(pe, s["reduced"][b], n)
        for g in range(GROUP):
            m = 0
            for part in (self.low[b], self.high[b]):
                for q in range(BLK):
                    ins = nc.tensor.matmul(self.look[b][:, g, :], self.hi_t[b][:, q, g * P:(g + 1) * P],
                                           part[:, q * LO:(q + 1) * LO], start=(m == 0), stop=(m == 2 * BLK - 1))
                    m += 1
        ins.then_inc(s["looked"][b], 1)

    def zero(self):
        self.nc.vector.memset(self.table[:, :], 0.0)
        self.nc.vector.tensor_copy(self.ident16[:, :], self.k.ident[:, :]).then_inc(self.zeroed, 1)

    def prepare(self, v, b, n):
        s, nc = self.s, self.nc
        v.wait_ge(s["rows_in"][b], n * 32 + 32)
        need(v, s["looked"][b], n)
        need(v, s["pos_ready"][b], n)
        for q in range(BLK):
            nc.vector.tensor_scalar(self.hi_t[b][:, q, :], self.hi_b[b][:, :], self.k.hi_of_part[0:self.HP, q:q + 1],
                                    None, ALU.is_equal)
        for g in range(GROUP):
            at = n * 2 * GROUP + (b * GROUP + g)
            one_hots(nc, self.k, self.g, at, self.lo1[b][:, g, :], self.hi1[b][:, g, :, :])
        need(v, s["prepared"][1 - b], n + b)
        for g in range(GROUP):
            at = n * 2 * GROUP + (b * GROUP + g)
            w = (g + 1) * P
            ins = nc.vector.scalar_tensor_tensor(self.same[:, g, 0:w], self.key_b[b][:, 0:w],
                                                 self.key[:, bass.ds(at, 1)], self.k.earlier[:, GE - w:],
                                                 ALU.is_equal, ALU.mult, accum_out=self.rank[b][:, g:g + 1])
        ins.then_inc(s["prepared"][b], 1)

    def reduce(self, v, b, n):
        s, nc = self.s, self.nc
        v.wait_ge(s["looked"][b], n + 1)
        need(v, s["reduced"][1 - b], n + b)
        for g in range(GROUP):
            ins = nc.vector.tensor_tensor_reduce(out=self.hit[:, g, :], in0=self.lo1[b][:, g, :],
                                                 in1=self.look[b][:, g, :], scale=1.0, scalar=0.0, op0=ALU.mult,
                                                 op1=ALU.add, accum_out=self.base[b][:, g:g + 1])
        ins.then_inc(s["reduced"][b], 1)
        v.wait_ge(s["reduced"][b], n + 1)
        need(v, s["scattered"][b], n * GROUP * 16)
        nc.vector.tensor_tensor(self.pos[b][:, :], self.base[b][:, :], self.rank[b][:, :], ALU.add)\
            .then_inc(s["pos_ready"][b], 1)

    def gpsimd(self, g, b, n):
        s = self.s
        g.wait_ge(s["pos_ready"][b], n + 1)
        g.wait_ge(s["pay_in"][b], n * 16 + 16)
        g.sem_inc(self.t.passed("pool"), 1)
        for q in range(GROUP):
            g.indirect_dma_start(out=self.out,
                                 out_offset=bass.IndirectOffsetOnAxis(ap=self.pos[b][:, q:q + 1], axis=0),
                                 in_=self.pay[b][:, q, :], in_offset=None).then_inc(s["scattered"][b], 16)

    def end(self, g):
        for b in range(2):
            g.wait_ge(self.s["scattered"][b], self.N * GROUP * 16)


def sort_payload(nc, k, d, io):
    m = Pool2(nc, "dst")
    entered = m.sem("entered")
    with nc.Block() as block:
        @block.sync
        def _(sp):
            sp.sem_inc(entered, 1)

        @block.gpsimd
        def _(g):
            g.sem_inc(entered, 1)

        @block.tensor
        def _(pe):
            pe.sem_inc(entered, 1)

        @block.scalar
        def _(act):
            act.sem_inc(entered, 1)

        @block.vector
        def _(v):
            v.sem_inc(entered, 1)
            v.wait_ge(entered, 5)
    digits(nc, k, m, d, io, "dst")
    c = Pool2(nc, "dst_count")
    counting = Counting(nc, k, c, d, "dst")
    zeroed, copied = c.sem("zeroed"), c.sem("copied")
    steps = d["T"] // Counting.H
    with nc.Block() as block:
        @block.sync
        def _(sp):
            sp.dma_start(k.d_pay_given, k.d_pay_sorted).then_inc(copied, 16)
            sp.wait_ge(copied, 16)

        @block.vector
        def _(v):
            nc.vector.memset(counting.table[:, :], 0.0).then_inc(zeroed, 1)
            repeat(v, steps, lambda i: counting.vector(v, i))

        @block.tensor
        def _(pe):
            pe.wait_ge(zeroed, 1)
            repeat(pe, steps, lambda i: counting.tensor(pe, i, 0, Counting.H))
    first_places(nc, k, c, d, "dst", counting.table, False)
    c.close()
    t = Pool2(nc, "dst_place")
    p = Placing(nc, k, t, d, "dst", k.d_pay_given.rearrange("(p t) c -> p t c", t=d["T"]), PAY, F32, k.d_pay_sorted)
    with nc.Block() as block:
        @block.sync
        def _(sp):
            repeat(sp, p.N, lambda i: p.sync(sp, i))
            p.sync_last(sp)

        @block.scalar
        def _(act):
            def body(i):
                for b in range(2):
                    p.scalar(act, b, i)
            repeat(act, p.N, body)

        @block.tensor
        def _(pe):
            p.begin(pe)

            def body(i):
                for b in range(2):
                    p.update(pe, b, i)
                    p.lookup(pe, b, i)
            repeat(pe, p.N, body)

        @block.vector
        def _(v):
            p.zero()

            def body(i):
                p.prepare(v, 0, i)
                if not isinstance(i, int) or i > 0:
                    p.reduce(v, 1, i - 1)
                p.prepare(v, 1, i)
                p.reduce(v, 0, i)
            repeat(v, p.N, body)
            p.reduce(v, 1, p.N - 1)

        @block.gpsimd
        def _(g):
            def body(i):
                for b in range(2):
                    p.gpsimd(g, b, i)
            repeat(g, p.N, body)
            p.end(g)
    t.close()
    t = Pool2(nc, "dst_values")
    loaded = t.sem("loaded")
    with nc.Block() as block:
        @block.sync
        def _(sp):
            sp.dma_start(k.values[:, :, :], k.d_pay_rows[:, :, 0:V_W]).then_inc(loaded, 16)
            sp.wait_ge(loaded, 16)
    t.close()
    m.close()


def final_nodes(nc, k, d, io):
    R, J = d["R"], d["J"]
    SLOTS = 4
    N = R // J // SLOTS
    t = Pool2(nc, "final")
    slots = range(SLOTS)
    xin = [t.sb(f"x{b}", [P, J, XW]) for b in slots]
    acc = [t.sb(f"acc{b}", [P, J, C]) for b in slots]
    cen = [t.sb(f"cen{b}", [P, J, C]) for b in slots]
    sq = [t.sb(f"sq{b}", [P, J, C]) for b in slots]
    stat = [t.sb(f"stat{b}", [P, 4, J]) for b in slots]
    eps = t.sb("eps", [P, 1])
    s = {n: t.sems(n, SLOTS) for n in ("in", "step", "sum", "centred", "squared", "dev", "scale", "res", "stored")}
    init = t.sem("init")
    xt_nodes = k.d_xt.rearrange("(a b) o -> a (b o)", b=XW)[0:d["N_PAD"], :].rearrange("(p r) c -> p r c", r=R)
    acc_nodes = k.d_acc[0:d["N_PAD"], :].rearrange("(p r) c -> p r c", r=R)
    out_nodes = io["out"].rearrange("(p r) c -> p r c", r=R)
    with nc.Block() as block:
        @block.sync
        def _(sp):
            def body(n):
                for b in slots:
                    at = n * SLOTS * J + b * J
                    need(sp, s["centred"][b], n)
                    sp.sem_inc(t.passed("sp"), 1)
                    sp.dma_start(xin[b][:, :, :], xt_nodes[:, bass.ds(at, J), :]).then_inc(s["in"][b], 16)
                    sp.dma_start(acc[b][:, :, :], acc_nodes[:, bass.ds(at, J), :]).then_inc(s["in"][b], 16)
            repeat(sp, N, body)

        @block.gpsimd
        def _(g):
            def body(n):
                for b in slots:
                    at = n * SLOTS * J + b * J
                    g.wait_ge(s["res"][b], n + 1)
                    g.sem_inc(t.passed("pool"), 1)
                    g.dma_start(out_nodes[:, bass.ds(at, J), :], cen[b][:, :, :]).then_inc(s["stored"][b], 16)
            repeat(g, N, body)
            for b in slots:
                g.wait_ge(s["stored"][b], 16 * N)

        @block.scalar
        def _(act):
            act.wait_ge(init, 1)

            def body(n):
                for b in slots:
                    act.wait_ge(s["centred"][b], n + 1)
                    for j in range(J):
                        ins = nc.scalar.activation(sq[b][:, j, :], cen[b][:, j, :], ACT.Square,
                                                   accum_out=stat[b][:, 1, j:j + 1])
                    ins.then_inc(s["squared"][b], 1)
                    act.wait_ge(s["squared"][b], n + 1)
                    nc.scalar.activation(stat[b][:, 2, :], stat[b][:, 1, :], ACT.Sqrt, bias=eps[:, 0:1],
                                         scale=1.25 ** 2 / C).then_inc(s["dev"][b], 1)
            repeat(act, N, body)

        @block.vector
        def _(v):
            nc.vector.memset(eps[:, :], EPS).then_inc(init, 1)

            def centre(b, n):
                st = Steps(v, s["step"][b], n * 2)
                v.wait_ge(s["in"][b], n * 32 + 32)
                nc.vector.scalar_tensor_tensor(acc[b][:, :, :], acc[b][:, :, :], 0.2, xin[b][:, :, 0:C], ALU.mult,
                                               ALU.add).then_inc(s["sum"][b], 1)
                v.wait_ge(s["sum"][b], n + 1)
                st.link(nc.vector.tensor_reduce(stat[b][:, 0, :], acc[b][:, :, :], AX, ALU.add))
                st.link(nc.vector.tensor_scalar(stat[b][:, 0, :], stat[b][:, 0, :], 1.0 / C, None, ALU.mult))
                need(v, s["stored"][b], n * 16)
                nc.vector.tensor_tensor(cen[b][:, :, :], acc[b][:, :, :],
                                        stat[b][:, 0, :].unsqueeze(2).to_broadcast([P, J, C]), ALU.subtract)\
                    .then_inc(s["centred"][b], 1)

            def finish(b, n):
                v.wait_ge(s["dev"][b], n + 1)
                nc.vector.reciprocal(stat[b][:, 3, :], stat[b][:, 2, :]).then_inc(s["scale"][b], 1)
                v.wait_ge(s["scale"][b], n + 1)
                nc.vector.scalar_tensor_tensor(cen[b][:, :, :], cen[b][:, :, :], 1.25,
                                               stat[b][:, 3, :].unsqueeze(2).to_broadcast([P, J, C]), ALU.mult,
                                               ALU.mult)\
                    .then_inc(s["res"][b], 1)

            def body(n):
                for b in slots:
                    centre(b, n)
                    if b > 1:
                        finish(b - 2, n)
                    elif not isinstance(n, int) or n > 0:
                        finish(SLOTS - 2 + b, n - 1)
            repeat(v, N, body)
            for b in (SLOTS - 2, SLOTS - 1):
                finish(b, N - 1)
    t.close()


def segments(nc, k, d, g, tag):
    T = d["T"]
    t = Pool2(nc, f"seg_{tag}")
    before, after = t.sb("before", [P, 1]), t.sb("after", [P, 1])
    n_lead = t.sb("n_lead", [P, 1])
    rowf = t.sb("rowf", [P, 1])
    away = t.sb("away", [P, T])
    v_step, shifted, ready = t.sem("v_step"), t.sem("shifted"), t.sem("ready")
    with nc.Block() as block:
        @block.sync
        def _(sp):
            sp.wait_ge(ready, 1)
            with nc.allow_non_contiguous_dma(reason="one key per partition"):
                sp.dma_start(before[1:P, :], g.key[0:P - 1, T - 1:T]).then_inc(shifted, 16)
                sp.dma_start(after[0:P - 1, :], g.key[1:P, 0:1]).then_inc(shifted, 16)

        @block.vector
        def _(v):
            st = Steps(v, v_step)
            nc.vector.memset(before[:, :], -1.0)
            nc.vector.memset(g.cont[:, 0:1], 0.0)
            nc.vector.memset(after[:, :], -1.0).then_inc(ready, 1)
            st.did(nc.vector.tensor_tensor(g.cont[:, 1:T], g.key[:, 1:T], g.key[:, 0:T - 1], ALU.is_equal))
            st.did(nc.vector.tensor_tensor(g.last[:, 0:T - 1], g.key[:, 0:T - 1], g.key[:, 1:T], ALU.not_equal))
            st.link(nc.vector.tensor_scalar(g.lead[:, :], g.key[:, :], g.key[:, 0:1], None, ALU.is_equal))
            st.link(nc.vector.tensor_reduce(n_lead[:, :], g.lead[:, :], AX, ALU.add))
            st.did(nc.vector.tensor_scalar(g.whole[:, :], n_lead[:, :], float(T), None, ALU.is_equal))
            nc.vector.memset(g.end_lead[:, T - 1:T], 1.0)
            st.did(nc.vector.tensor_copy(g.end_lead[:, 0:T - 1], g.last[:, 0:T - 1]))
            st.link(nc.vector.scalar_tensor_tensor(rowf[:, :], n_lead[:, :], -1.0, k.place[:, 0:1], ALU.add, ALU.add))
            nc.vector.tensor_copy(g.row[:, :], rowf[:, :])
            st.did(nc.vector.tensor_tensor(g.end_lead[:, :], g.end_lead[:, :], g.lead[:, :], ALU.mult))
            v.wait_ge(shifted, 32)
            st.did(nc.vector.tensor_tensor(g.joins[:, :], g.key[:, 0:1], before[:, :], ALU.is_equal))
            st.link(nc.vector.tensor_tensor(g.last[:, T - 1:T], g.key[:, T - 1:T], after[:, :], ALU.not_equal))
            st.link(nc.vector.tensor_scalar(away[:, :], k.place[:, :], float(d["SPARE"]), None, ALU.add))
            st.link(nc.vector.tensor_tensor(g.at[:, :], g.key[:, :], away[:, :], ALU.subtract))
            st.link(nc.vector.tensor_tensor(g.at[:, :], g.at[:, :], g.last[:, :], ALU.mult))
            st.link(nc.vector.tensor_tensor(g.at[:, :], g.at[:, :], away[:, :], ALU.add))
    t.close()


class Segments:
    def __init__(self, m, T):
        self.key, self.cont, self.last, self.lead, self.end_lead, self.at = (
            m.sb(n, [P, T]) for n in ("key", "cont", "last", "lead", "end_lead", "at"))
        self.joins, self.whole, self.row = m.sb("joins", [P, 1]), m.sb("whole", [P, 1]), m.sb("row", [P, 1], I32)


def hand_over(nc, k, tag, width, state, carry, op, weight):
    t = Pool2(nc, f"hand_{tag}")
    ps_s, ps_w, ps_b = t.ps("state", [P, P]), t.ps("weight", [P, P]), t.ps("back", [P, P])
    wt = t.sb("wt", [P, P])
    out = t.sb("out", [P, P + 1])
    turned, wt_in, scanned, back = t.sem("turned"), t.sem("wt_in"), t.sem("scanned"), t.sem("back")
    with nc.Block() as block:
        @block.tensor
        def _(pe):
            nc.tensor.transpose(ps_s[0:width, :], state, k.ident[:, :])
            nc.tensor.transpose(ps_w[0:width, :], weight, k.ident[:, :]).then_inc(turned, 1)
            pe.wait_ge(scanned, 1)
            nc.tensor.transpose(ps_b[:, 0:width], out[0:width, 0:P], k.ident[0:width, 0:width]).then_inc(back, 1)

        @block.vector
        def _(v):
            nc.vector.memset(out[0:width, 0:1], 0.0)
            v.wait_ge(turned, 1)
            nc.vector.tensor_copy(wt[0:width, :], ps_w[0:width, :]).then_inc(wt_in, 1)
            v.wait_ge(wt_in, 1)
            nc.vector.tensor_tensor_scan(out[0:width, 1:P + 1], wt[0:width, :], ps_s[0:width, :], 0.0,
                                         ALU.mult if op == ALU.add else ALU.add, op).then_inc(scanned, 1)
            v.wait_ge(back, 1)
            nc.vector.tensor_copy(carry, ps_b[:, 0:width])
    t.close()


def attention(nc, k, d, io):
    T, S = d["T"], d["S"]
    m = Pool2(nc, "att")
    g = Segments(m, T)
    V = k.values
    tail, carry = m.sb("tail", [P, 80]), m.sb("carry", [P, 80])
    w4, top_lead, decay = m.sb("w4", [P, HEADS]), m.sb("top_lead", [P, HEADS]), m.sb("decay", [P, HEADS])
    factor = m.sb("factor", [P, C + HEADS])
    factor_w = m.sb("factor_w", [P, C + HEADS])

    a = Pool2(nc, "att_key")
    keyed = a.sem("keyed")
    with nc.Block() as block:
        @block.vector
        def _(v):
            nc.vector.tensor_copy(g.key[:, :], V[:, :, 68]).then_inc(keyed, 1)
    a.close()
    segments(nc, k, d, g, "dst")

    w = Pool2(nc, "att_work")
    top = w.sb("top", [P, HEADS, T])
    wgt = w.sb("wgt", [P, HEADS, T])
    pen = w.sb("pen", [P, T])
    a = Pool2(nc, "att_max")
    step = a.sem("step")
    with nc.Block() as block:
        @block.vector
        def _(v):
            st = Steps(v, step)
            st.link(nc.vector.tensor_scalar(pen[:, :], g.cont[:, :], -1.0, BIG, ALU.add, ALU.mult))
            for h in range(HEADS):
                st.did(nc.vector.tensor_tensor_scan(top[:, h, :], pen[:, :], V[:, :, C + h], -BIG, ALU.add, ALU.max))
            st.settle()
            st.did(nc.vector.tensor_copy(tail[:, 0:HEADS], top[:, :, T - 1]))
            st.link(nc.vector.tensor_tensor(w4[:, 0:1], g.joins[:, :], g.whole[:, :], ALU.mult))
            for h in range(HEADS):
                st.did(nc.vector.tensor_scalar(tail[:, 8 + h:9 + h], w4[:, 0:1], -1.0, BIG, ALU.add, ALU.mult))
            st.settle()
    a.close()
    hand_over(nc, k, "max", HEADS, tail[:, 0:HEADS], carry[:, 0:HEADS], ALU.max, tail[:, 8:8 + HEADS])

    a = Pool2(nc, "att_sum")
    step, for_exp, exped = a.sem("step"), a.sem("for_exp"), a.sem("exped")
    diff = a.sb("diff", [P, HEADS, T])
    with nc.Block() as block:
        @block.scalar
        def _(act):
            act.wait_ge(for_exp, 1)
            nc.scalar.activation(wgt[:, :, :], wgt[:, :, :], ACT.Exp)
            nc.scalar.activation(diff[:, :, :], diff[:, :, :], ACT.Exp)
            nc.scalar.activation(decay[:, :], decay[:, :], ACT.Exp).then_inc(exped, 1)

        @block.vector
        def _(v):
            st = Steps(v, step)
            st.link(nc.vector.tensor_scalar(pen[:, :], g.lead[:, :], g.joins[:, 0:1], -1.0, ALU.mult, ALU.add))
            st.link(nc.vector.tensor_scalar(pen[:, :], pen[:, :], BIG, None, ALU.mult))
            for h in range(HEADS):
                st.did(nc.vector.scalar_tensor_tensor(top[:, h, :], pen[:, :], carry[:, h:h + 1], top[:, h, :],
                                                      ALU.add, ALU.max))
            st.settle()
            st.did(nc.vector.tensor_scalar(pen[:, :], g.lead[:, :], -1.0, BIG, ALU.add, ALU.mult))
            st.settle()
            for h in range(HEADS):
                st.did(nc.vector.tensor_tensor(diff[:, h, :], top[:, h, :], pen[:, :], ALU.add))
                st.did(nc.vector.tensor_tensor(wgt[:, h, :], V[:, :, C + h], top[:, h, :], ALU.subtract))
            st.settle()
            st.link(nc.vector.tensor_reduce(top_lead[:, :], diff[:, :, :], AX, ALU.max))
            st.link(nc.vector.tensor_tensor(decay[:, :], carry[:, 0:HEADS], top_lead[:, :], ALU.subtract))
            nc.vector.tensor_scalar(decay[:, :], decay[:, :], 0.0, None, ALU.min)
            st.did(nc.vector.memset(diff[:, :, 0:1], 0.0))
            st.link(nc.vector.tensor_tensor(diff[:, :, 1:T], top[:, :, 0:T - 1], top[:, :, 1:T], ALU.subtract))
            nc.vector.tensor_scalar(diff[:, :, :], diff[:, :, :], 0.0, None, ALU.min).then_inc(for_exp, 1)
            v.wait_ge(exped, 1)
            for h in range(HEADS):
                cols = slice(h * HD, (h + 1) * HD)
                st.did(nc.vector.tensor_tensor(top[:, h, :], diff[:, h, :], g.cont[:, :], ALU.mult))
                st.did(nc.vector.tensor_copy(V[:, :, C + h], wgt[:, h, :]))
                st.did(nc.vector.tensor_tensor(V[:, :, cols], V[:, :, cols],
                                               wgt[:, h, :].unsqueeze(2).to_broadcast([P, T, HD]), ALU.mult))
            st.settle()
            with v.Fori(0, HEADS) as h:
                decays = top[:, bass.ds(h, 1), :].rearrange("p o t -> p (o t)")
                for c in range(HD):
                    col = V[:, :, bass.ds(h * HD + c, 1)].rearrange("p t o -> p (t o)")
                    nc.vector.tensor_tensor_scan(col, decays, col, 0.0, ALU.mult, ALU.add)
            for h in range(HEADS):
                st.did(nc.vector.tensor_tensor_scan(V[:, :, C + h], top[:, h, :], V[:, :, C + h], 0.0,
                                                    ALU.mult, ALU.add))
            st.settle()
            st.did(nc.vector.tensor_copy(tail[:, 0:C + HEADS], V[:, T - 1, 0:C + HEADS]))
            st.link(nc.vector.tensor_scalar(decay[:, :], decay[:, :], g.joins[:, 0:1], None, ALU.mult))
            st.did(nc.vector.tensor_copy(factor[:, 0:C].rearrange("p (h c) -> p h c", h=HEADS),
                                         decay[:, :].unsqueeze(2).to_broadcast([P, HEADS, HD])))
            st.did(nc.vector.tensor_copy(factor[:, C:C + HEADS], decay[:, :]))
            st.settle()
            st.link(nc.vector.tensor_scalar(factor_w[:, :], factor[:, :], g.whole[:, 0:1], None, ALU.mult))
    a.close()
    hand_over(nc, k, "sum", C + HEADS, tail[:, 0:C + HEADS], carry[:, 0:C + HEADS], ALU.add, factor_w[:, :])

    w.close()
    rows_and_places(nc, k, d, io, V, g, carry, factor)
    m.close()


class NodeRows:

    def __init__(self, nc, k, t, d, V, at65):
        two = range(2)
        W = 2 * GROUP
        self.nc, self.k, self.t, self.V, self.at65, self.N, self.W = nc, k, t, V, at65, d["S"] // 2, W
        self.xd = t.sb("xd", [P, W, C])
        self.att = [t.sb(f"att{b}", [P, GROUP, C]) for b in two]
        self.att_t = [t.sb(f"att_t{b}", [C + 1, GE]) for b in two]
        self.y = t.sb("y", [P, W, C])
        self.cen = t.sb("cen", [P, W, C])
        self.sq = t.sb("sq", [P, W, C])
        self.stat = t.sb("stat", [P, 4, W])
        self.res = t.sb("res", [P, W, C])
        self.idx = t.sb("idx", [P, W], I32)
        self.eps = t.sb("eps", [P, 1])
        self.ps_t = t.ps("ps_t", [C, GE])
        self.ps_y = t.ps("ps_y", [P, W, C])
        self.s = {n: t.sems(n) for n in ("att_made", "turned", "turned_sb", "proj")}
        (self.xd_in, self.y_made, self.summed, self.mean, self.centred, self.squared, self.dev, self.scale,
         self.made, self.scattered) = (t.sem(f"rows_{n}") for n in ("xd_in", "y_made", "summed", "mean", "centred",
                                                                    "squared", "dev", "scale", "made", "scattered"))

    def sync(self, sp, n):
        need(sp, self.y_made, n)
        sp.sem_inc(self.t.passed("sp"), 1)
        sp.dma_start(self.xd[:, :, :], self.k.d_pay_rows[:, bass.ds(n * self.W, self.W), XD:])\
            .then_inc(self.xd_in, 16)

    def weigh(self, v, b, n):
        at = n * self.W + b * GROUP
        need(v, self.s["turned"][b], n)
        heads = lambda rows: rows.rearrange("p g (h c) -> p g h c", h=HEADS)
        self.nc.vector.tensor_tensor(
            heads(self.att[b][:, :, :]), heads(self.V[:, bass.ds(at, GROUP), 0:C]),
            self.V[:, bass.ds(at, GROUP), C:C + HEADS].unsqueeze(3).to_broadcast([P, GROUP, HEADS, HD]), ALU.mult)\
            .then_inc(self.s["att_made"][b], 1)

    def turn(self, pe, b, n):
        pe.wait_ge(self.s["att_made"][b], n + 1)
        if b == 0:
            need(pe, self.s["turned_sb"][1], n)
        else:
            pe.wait_ge(self.s["turned_sb"][0], n + 1)
        pe.sem_inc(self.t.passed("pe"), 1)
        for q in range(GROUP):
            ins = self.nc.tensor.transpose(self.ps_t[:, q * P:(q + 1) * P], self.att[b][:, q, :], self.k.ident[:, :])
        ins.then_inc(self.s["turned"][b], 1)

    def copy(self, act, b, n):
        act.wait_ge(self.s["turned"][b], n + 1)
        need(act, self.s["proj"][b], n)
        self.nc.scalar.activation(self.att_t[b][0:C, :], self.ps_t[:, :], ACT.Copy)\
            .then_inc(self.s["turned_sb"][b], 1)

    def project(self, pe, b, n):
        pe.wait_ge(self.s["turned_sb"][b], n + 1)
        if b == 0:
            need(pe, self.y_made, n)
        for q in range(GROUP):
            ins = self.nc.tensor.matmul(self.ps_y[:, b * GROUP + q, :], self.att_t[b][:, q * P:(q + 1) * P],
                                        self.k.w_proj[:, :], start=True, stop=True)
        ins.then_inc(self.s["proj"][b], 1)

    def centre(self, v, n):
        nc, mean = self.nc, self.stat[:, 0, :]
        for b in range(2):
            v.wait_ge(self.s["proj"][b], n + 1)
        v.wait_ge(self.xd_in, n * 16 + 16)
        nc.vector.tensor_tensor(self.y[:, :, :], self.ps_y[:, :, :], self.xd[:, :, :], ALU.add)\
            .then_inc(self.y_made, 1)
        v.wait_ge(self.y_made, n + 1)
        nc.vector.tensor_reduce(mean, self.y[:, :, :], AX, ALU.add).then_inc(self.summed, 1)
        v.wait_ge(self.summed, n + 1)
        nc.vector.tensor_scalar(mean, mean, 1.0 / C, None, ALU.mult).then_inc(self.mean, 1)
        v.wait_ge(self.mean, n + 1)
        need(v, self.made, n)
        nc.vector.tensor_tensor(self.cen[:, :, :], self.y[:, :, :],
                                mean.unsqueeze(2).to_broadcast([P, self.W, C]), ALU.subtract)\
            .then_inc(self.centred, 1)

    def square(self, act, n):
        nc = self.nc
        act.wait_ge(self.centred, n + 1)
        need(act, self.made, n)
        for j in range(self.W):
            ins = nc.scalar.activation(self.sq[:, j, :], self.cen[:, j, :], ACT.Square,
                                       accum_out=self.stat[:, 1, j:j + 1])
        ins.then_inc(self.squared, 1)
        act.wait_ge(self.squared, n + 1)
        nc.scalar.activation(self.stat[:, 2, :], self.stat[:, 1, :], ACT.Sqrt, bias=self.eps[:, 0:1], scale=1.0 / C)\
            .then_inc(self.dev, 1)

    def finish(self, v, n):
        nc = self.nc
        v.wait_ge(self.dev, n + 1)
        nc.vector.reciprocal(self.stat[:, 3, :], self.stat[:, 2, :]).then_inc(self.scale, 1)
        need(v, self.scattered, n * self.W * 16)
        nc.vector.tensor_scalar(self.idx[:, :], self.at65[:, bass.ds(n * self.W, self.W)], 1.0, None, ALU.mult)
        v.wait_ge(self.scale, n + 1)
        nc.vector.tensor_tensor(self.res[:, :, :], self.cen[:, :, :],
                                self.stat[:, 3, :].unsqueeze(2).to_broadcast([P, self.W, C]), ALU.mult)\
            .then_inc(self.made, 1)

    def gpsimd(self, g, n):
        g.wait_ge(self.made, n + 1)
        g.sem_inc(self.t.passed("pool"), 1)
        for q in range(self.W):
            g.indirect_dma_start(out=self.k.d_xt,
                                 out_offset=bass.IndirectOffsetOnAxis(ap=self.idx[:, q:q + 1], axis=0),
                                 in_=self.res[:, q, :], in_offset=None).then_inc(self.scattered, 16)


def rows_and_places(nc, k, d, io, V, g, carry, factor):
    a = Pool2(nc, "rows")
    rows = NodeRows(nc, k, a, d, V, g.at)
    places = Placing(nc, k, a, d, "src", io["rec"], 2, I32, k.d_rec_sorted)
    N = rows.N
    lead, scale = a.sb("lead", [P, d["T"]]), a.sb("scale", [P, HEADS])
    part_t, row, row_at = a.sb("part_t", [C, P]), a.sb("row", [P, C]), a.sb("row_at", [P, 1], I32)
    step, divided, turned, part_in, projected, located, got, fixed, done = (
        a.sem(n) for n in ("step", "divided", "turned", "part_in", "projected", "located", "got", "fixed", "done"))
    x_rows = k.d_pay_sorted.rearrange("r (c o) -> (r c) o", o=1)
    with nc.Block() as block:
        @block.sync
        def _(sp):
            def load_rows(n):
                if isinstance(n, int):
                    sp.wait_ge(done, 16)
                rows.sync(sp, n)
            repeat(sp, N, lambda i: places.sync(sp, i, load_rows))
            places.sync_last(sp)

        @block.tensor
        def _(pe):
            places.begin(pe)
            pe.wait_ge(divided, 1)
            nc.tensor.transpose(rows.ps_t[:, 0:P], carry[:, 0:C], k.ident[:, :]).then_inc(turned, 1)
            pe.wait_ge(part_in, 1)
            nc.tensor.matmul(rows.ps_y[:, 0, :], part_t[:, :], k.w_proj[0:C, :], start=True, stop=True)\
                .then_inc(projected, 1)
            pe.wait_ge(fixed, 1)

            def body(i):
                for b in range(2):
                    places.update(pe, b, i)
                    rows.turn(pe, b, i)
                    places.lookup(pe, b, i)
                    rows.project(pe, b, i)
            repeat(pe, N, body)

        @block.scalar
        def _(act):
            def body(i):
                places.scalar(act, 0, i)
                rows.copy(act, 0, i)
                places.scalar(act, 1, i)
                if not isinstance(i, int) or i > 0:
                    rows.square(act, i - 1)
                rows.copy(act, 1, i)
            repeat(act, N, body)
            rows.square(act, N - 1)

        @block.vector
        def _(v):
            st = Steps(v, step)
            places.zero()
            nc.vector.tensor_scalar(row_at[:, :], g.row[:, :], PAY, XD, ALU.mult, ALU.add).then_inc(located, 1)
            for b in range(2):
                st.did(nc.vector.memset(rows.att_t[b][C:C + 1, :], 1.0))
            st.did(nc.vector.memset(rows.eps[:, :], EPS))
            st.link(nc.vector.tensor_tensor(carry[:, 0:C + HEADS], carry[:, 0:C + HEADS], factor[:, :], ALU.mult))
            for h in range(C, C + HEADS):
                st.did(nc.vector.scalar_tensor_tensor(V[:, :, h], g.end_lead[:, :], carry[:, h:h + 1], V[:, :, h],
                                                      ALU.mult, ALU.add))
            st.settle()
            st.did(nc.vector.tensor_scalar(g.at[:, :], g.at[:, :], float(XW), None, ALU.mult))
            den = V[:, :, C:C + HEADS]
            st.link(nc.vector.tensor_scalar(den, den, 1e-16, None, ALU.add))
            st.link(nc.vector.reciprocal(den, den))
            for h in range(HEADS):
                st.link(nc.vector.scalar_tensor_tensor(lead[:, :], V[:, :, C + h], 1.0, g.end_lead[:, :], ALU.mult,
                                                       ALU.mult, accum_out=scale[:, h:h + 1]))
            part = carry[:, 0:C].rearrange("p (h c) -> p h c", h=HEADS)
            nc.vector.tensor_tensor(part, part, scale[:, :].unsqueeze(2).to_broadcast([P, HEADS, HD]), ALU.mult)\
                .then_inc(divided, 1)
            v.wait_ge(turned, 1)
            nc.vector.tensor_copy(part_t[:, :], rows.ps_t[:, 0:P]).then_inc(part_in, 1)
            v.wait_ge(projected, 1)
            v.wait_ge(got, 16)
            nc.vector.tensor_tensor(row[:, :], row[:, :], rows.ps_y[:, 0, :], ALU.add).then_inc(fixed, 1)
            for b in range(2):
                rows.weigh(v, b, 0)

            def body(i):
                later, more = not isinstance(i, int) or i > 0, not isinstance(i, int) or i < N - 1
                places.prepare(v, 0, i)
                if later:
                    places.reduce(v, 1, i - 1)
                    rows.centre(v, i - 1)
                places.prepare(v, 1, i)
                if more:
                    rows.weigh(v, 0, i + 1)
                places.reduce(v, 0, i)
                if later:
                    rows.finish(v, i - 1)
                if more:
                    rows.weigh(v, 1, i + 1)
            repeat(v, N - 1, body)
            body(N - 1)
            places.reduce(v, 1, N - 1)
            rows.centre(v, N - 1)
            rows.finish(v, N - 1)

        @block.gpsimd
        def _(gp):
            gp.wait_ge(located, 1)
            gp.indirect_dma_start(out=row[:, :], out_offset=None, in_=x_rows,
                                  in_offset=bass.IndirectOffsetOnAxis(ap=row_at[:, 0:1], axis=0)).then_inc(got, 16)
            gp.wait_ge(fixed, 1)
            gp.indirect_dma_start(out=x_rows, out_offset=bass.IndirectOffsetOnAxis(ap=row_at[:, 0:1], axis=0),
                                  in_=row[:, :], in_offset=None).then_inc(done, 16)

            def body(i):
                places.gpsimd(gp, 0, i)
                if not isinstance(i, int) or i > 0:
                    rows.gpsimd(gp, i - 1)
                places.gpsimd(gp, 1, i)
            repeat(gp, N, body)
            rows.gpsimd(gp, N - 1)
            places.end(gp)
            gp.wait_ge(rows.scattered, N * rows.W * 16)
    a.close()


class Gathering:

    W = 7

    def __init__(self, nc, t, d, G, at, width):
        self.nc, self.t, self.G, self.at, self.width, self.N = nc, t, G, at, width, d["T"] // (2 * self.W)
        self.idx = [t.sb(f"idx{b}", [P, self.W], I32) for b in range(2)]
        self.rows = [t.sb(f"rows{b}", [P, self.W, width]) for b in range(2)]
        self.s = {n: t.sems(n) for n in ("idx_made", "gathered", "copied", "staged", "scattered")}

    def tile(self, b, n):
        return n * 2 * self.W + b * self.W

    def gpsimd(self, g, table):
        def body(n):
            for b in range(2):
                g.wait_ge(self.s["idx_made"][b], n + 1)
                need(g, self.s["copied"][b], n)
                g.sem_inc(self.t.passed("pool"), 1)
                for q in range(self.W):
                    g.indirect_dma_start(out=self.rows[b][:, q, :], out_offset=None, in_=table,
                                         in_offset=bass.IndirectOffsetOnAxis(ap=self.idx[b][:, q:q + 1], axis=0))\
                        .then_inc(self.s["gathered"][b], 16)
        repeat(g, self.N, body)

    def scalar(self, act):
        def indices(b, n):
            self.nc.scalar.activation(self.idx[b][:, :], self.at[:, bass.ds(self.tile(b, n), self.W)], ACT.Copy)\
                .then_inc(self.s["idx_made"][b], 1)

        def copy(b, n, more):
            act.wait_ge(self.s["gathered"][b], n * self.W * 16 + self.W * 16)
            act.sem_inc(self.t.passed("act"), 1)
            if more:
                indices(b, n + 1)
            self.nc.scalar.activation(self.G[:, bass.ds(self.tile(b, n), self.W), 0:self.width],
                                      self.rows[b][:, :, :], ACT.Copy).then_inc(self.s["copied"][b], 1)

        for b in range(2):
            indices(b, 0)
        with act.Fori(0, self.N - 1) as n:
            for b in range(2):
                copy(b, n, True)
        for b in range(2):
            copy(b, self.N - 1, False)

    def stage(self, act, at, ready):
        s = self.s

        def body(n):
            ready(n)
            for b in range(2):
                act.wait_ge(s["copied"][b], self.N)
                need(act, s["scattered"][b], n * self.W * 16)
                act.sem_inc(self.t.passed("act"), 1)
                self.nc.scalar.activation(self.idx[b][:, :], at[:, bass.ds(self.tile(b, n), self.W)], ACT.Copy)
                self.nc.scalar.activation(self.rows[b][:, :, :], self.G[:, bass.ds(self.tile(b, n), self.W), 0:C],
                                          ACT.Copy).then_inc(s["staged"][b], 1)
        repeat(act, self.N, body)

    def scatter(self, g, table):
        def body(n):
            for b in range(2):
                g.wait_ge(self.s["staged"][b], n + 1)
                g.sem_inc(self.t.passed("pool"), 1)
                for q in range(self.W):
                    g.indirect_dma_start(out=table, in_=self.rows[b][:, q, :], in_offset=None,
                                         out_offset=bass.IndirectOffsetOnAxis(ap=self.idx[b][:, q:q + 1], axis=0))\
                        .then_inc(self.s["scattered"][b], 16)
        repeat(g, self.N, body)
        for b in range(2):
            g.wait_ge(self.s["scattered"][b], self.N * self.W * 16)


def layers(nc, k, d, io):
    T = d["T"]
    m = Pool2(nc, "lay")
    TC = 4 * Gathering.W
    CH = T // TC
    FW = 32
    g = Segments(m, T)
    nbr = m.sb("nbr", [P, T])
    G = m.sb("gathered", [P, T, XW])
    inv_deg = m.sb("inv_deg", [P, T])
    inv_row = m.sb("inv_row", [P, 1])
    row_at = m.sb("row_at", [P, 1], I32)
    joins_w = m.sb("joins_w", [P, C])
    joins_t = m.sb("joins_t", [C, P])
    joins_c = m.sb("joins_c", [P, C])
    carry = m.sb("carry", [P, C])
    tail = m.sb("tail", [P, C])

    a = Pool2(nc, "lay_load")
    rec = a.sb("rec", [P, T, 2], I32)
    loaded, keyed = a.sem("loaded"), a.sem("keyed")
    with nc.Block() as block:
        @block.sync
        def _(sp):
            sp.dma_start(rec[:, :, :], k.d_rec_sorted.rearrange("(p t) c -> p t c", t=T)).then_inc(loaded, 16)

        @block.vector
        def _(v):
            v.wait_ge(loaded, 16)
            nc.vector.tensor_copy(g.key[:, :], rec[:, :, 0])
            nc.vector.tensor_copy(nbr[:, :], rec[:, :, 1]).then_inc(keyed, 1)
    a.close()
    segments(nc, k, d, g, "src")

    a = Pool2(nc, "lay_deg")
    step = a.sem("step")
    with nc.Block() as block:
        @block.vector
        def _(v):
            st = Steps(v, step)
            st.did(nc.vector.tensor_tensor_scan(inv_deg[:, :], g.cont[:, :], k.ones[:, 0:T], 0.0, ALU.mult, ALU.add))
            st.did(nc.vector.tensor_tensor(joins_w[:, 0:1], g.joins[:, :], g.whole[:, :], ALU.mult))
            st.settle()
            st.did(nc.vector.tensor_scalar(joins_w[:, 1:C], k.ones[:, 1:C], joins_w[:, 0:1], None, ALU.mult))
            st.did(nc.vector.tensor_scalar(joins_c[:, :], k.ones[:, 0:C], g.joins[:, 0:1], None, ALU.mult))
            st.did(nc.vector.tensor_scalar(tail[:, :], k.ones[:, 0:C], inv_deg[:, T - 1:T], None, ALU.mult))
            st.settle()
    a.close()
    hand_over(nc, k, "deg", C, tail[:, :], carry[:, :], ALU.add, joins_w[:, :])
    a = Pool2(nc, "lay_inv")
    tmp, row_f = a.sb("tmp", [P, T]), a.sb("row_f", [P, 4])
    ps_w = a.ps("ps_w", [P, P])
    step, turned = a.sem("step"), a.sem("turned")
    with nc.Block() as block:
        @block.tensor
        def _(pe):
            nc.tensor.transpose(ps_w[0:C, :], joins_w[:, :], k.ident[:, :]).then_inc(turned, 1)

        @block.vector
        def _(v):
            st = Steps(v, step)
            st.link(nc.vector.tensor_tensor(carry[:, :], carry[:, :], joins_c[:, :], ALU.mult))
            st.link(nc.vector.scalar_tensor_tensor(inv_deg[:, :], g.lead[:, :], carry[:, 0:1], inv_deg[:, :],
                                                   ALU.mult, ALU.add))
            st.link(nc.vector.reciprocal(inv_deg[:, :], inv_deg[:, :]))
            st.link(nc.vector.tensor_tensor(tmp[:, :], inv_deg[:, :], g.end_lead[:, :], ALU.mult))
            st.link(nc.vector.tensor_reduce(inv_row[:, :], tmp[:, :], AX, ALU.add))
            st.link(nc.vector.tensor_tensor(tmp[:, :], g.last[:, :], g.end_lead[:, :], ALU.mult))
            st.link(nc.vector.tensor_reduce(row_f[:, 0:1], tmp[:, :], AX, ALU.add))
            st.link(nc.vector.tensor_scalar(row_f[:, 1:2], k.hi_of_part[:, 0:1], 1.0 / BLK, float(d["N_PAD"]),
                                            ALU.mult, ALU.add))
            st.link(nc.vector.tensor_tensor(row_f[:, 2:3], g.key[:, 0:1], row_f[:, 1:2], ALU.subtract))
            st.link(nc.vector.scalar_tensor_tensor(row_f[:, 3:4], row_f[:, 2:3], row_f[:, 0:1], row_f[:, 1:2],
                                                   ALU.mult, ALU.add))
            st.did(nc.vector.tensor_copy(row_at[:, :], row_f[:, 3:4]))
            st.did(nc.vector.tensor_scalar(joins_c[:, :], joins_c[:, :], inv_row[:, 0:1], None, ALU.mult))
            v.wait_ge(turned, 1)
            st.link(nc.vector.tensor_copy(joins_t[:, :], ps_w[0:C, :]))
    a.close()

    xt_rows = k.d_xt.rearrange("(a b) o -> a (b o)", b=XW)[0:d["N_PAD"], :]
    for layer in range(3):
        first, summing = layer == 0, layer == 2
        table = xt_rows if first else k.d_z[layer - 1]
        out = k.d_acc if summing else k.d_z[layer]
        at = row_at if summing else g.row
        z_rows = [z[0:d["E_PAD"], :].rearrange("(p t) c -> p t c", t=T) for z in k.d_z]
        a = Pool2(nc, f"lay{layer}")
        gathering = Gathering(nc, a, d, G, nbr, XW if first else C)
        ends = a.sb("ends", [P, C])
        row = a.sb("row", [P, C])
        zin = [[a.sb(f"zin{u}{n}", [P, TC, C]) for n in range(2)] for u in range(2)] if summing else None
        ps_s, ps_b = a.ps("ps_s", [P, P]), a.ps("ps_b", [P, P])
        over = a.sb("over", [C, P + 1])
        begun, scanned, held, scaled, paired, added, stored = (
            a.sem(n) for n in ("begun", "scanned", "held", "scaled", "paired", "added", "stored"))
        zin_in = a.sems("zin_in")
        ended, turned, passed_on, back, weighed, got, fixed, done = (
            a.sem(n) for n in ("ended", "turned", "passed_on", "back", "weighed", "got", "fixed", "done"))
        with nc.Block() as block:
            @block.gpsimd
            def _(gp):
                gathering.gpsimd(gp, table)
                if summing:
                    gathering.scatter(gp, out)
                else:
                    gp.wait_ge(stored, 16 * CH)
                filled = out[0:d["SPARE"] if summing else d["E_PAD"], :]
                gp.indirect_dma_start(out=row[:, :], out_offset=None, in_=filled,
                                      in_offset=bass.IndirectOffsetOnAxis(ap=at[:, 0:1], axis=0)).then_inc(got, 16)
                gp.wait_ge(fixed, 1)
                gp.sem_inc(a.passed("pool"), 1)
                gp.indirect_dma_start(out=out, out_offset=bass.IndirectOffsetOnAxis(ap=at[:, 0:1], axis=0),
                                      in_=row[:, :], in_offset=None).then_inc(done, 16)
                gp.wait_ge(done, 16)

            @block.scalar
            def _(act):
                gathering.scalar(act)
                if summing:
                    gathering.stage(act, g.at, lambda n: act.wait_ge(added, n + 1))

            @block.vector
            def _(v):
                nc.vector.memset(over[:, 0:1], 0.0)
                nc.vector.memset(ends[:, :], 0.0).then_inc(begun, 1)
                v.wait_ge(begun, 1)

                def chunk(c, u, i):
                    lo = c * TC
                    for b in range(2):
                        v.wait_ge(gathering.s["copied"][b], c * 2 + 2)
                    need(v, held, c)
                    v.sem_inc(a.passed("dve"), 1)
                    with v.Fori(0, C // FW) as f:
                        for q in range(FW):
                            col = G[:, bass.ds(lo, TC), bass.ds(f * FW + q, 1)].rearrange("p t o -> p (t o)")
                            ins = nc.vector.tensor_tensor_scan(col, g.cont[:, bass.ds(lo, TC)], col,
                                                               ends[:, bass.ds(f * FW + q, 1)], ALU.mult, ALU.add)
                        ins.then_inc(scanned, 1)
                    v.wait_ge(scanned, c * (C // FW) + C // FW)
                    rows = G[:, bass.ds(lo, TC), 0:C]
                    nc.vector.tensor_copy(ends[:, :].unsqueeze(1), G[:, bass.ds(lo + TC - 1, 1), 0:C])\
                        .then_inc(held, 1)
                    v.wait_ge(held, c + 1)
                    nc.vector.tensor_tensor(rows, rows, inv_deg[:, bass.ds(lo, TC)].unsqueeze(2)
                                            .to_broadcast([P, TC, C]), ALU.mult).then_inc(scaled, 1)
                    if summing:
                        v.wait_ge(zin_in[u], i * 32 + 32)
                        v.wait_ge(scaled, c + 1)
                        nc.vector.tensor_tensor(zin[u][0][:, :, :], zin[u][0][:, :, :], zin[u][1][:, :, :], ALU.add)\
                            .then_inc(paired, 1)
                        v.wait_ge(paired, c + 1)
                        nc.vector.tensor_tensor(rows, rows, zin[u][0][:, :, :], ALU.add).then_inc(added, 2)

                def body(i):
                    for u in range(2):
                        chunk(i * 2 + u, u, i)
                repeat(v, CH // 2, body)
                nc.vector.tensor_copy(tail[:, :], ends[:, :]).then_inc(ended, 1)
                v.wait_ge(turned, 1)
                nc.vector.tensor_tensor_scan(over[:, 1:P + 1], joins_t[:, :], ps_s[0:C, :], 0.0, ALU.mult, ALU.add)\
                    .then_inc(passed_on, 1)
                v.wait_ge(back, 1)
                nc.vector.tensor_tensor(carry[:, :], ps_b[:, 0:C], joins_c[:, :], ALU.mult).then_inc(weighed, 1)
                v.wait_ge(weighed, 1)
                v.wait_ge(got, 16)
                nc.vector.tensor_tensor(row[:, :], row[:, :], carry[:, :], ALU.add).then_inc(fixed, 1)
                if first:
                    nc.vector.tensor_copy(nbr[:, :], G[:, :, C])

            @block.tensor
            def _(pe):
                pe.wait_ge(ended, 1)
                nc.tensor.transpose(ps_s[0:C, :], tail[:, :], k.ident[:, :]).then_inc(turned, 1)
                pe.wait_ge(passed_on, 1)
                nc.tensor.transpose(ps_b[:, 0:C], over[:, 0:P], k.ident[0:C, 0:C]).then_inc(back, 1)

            @block.sync
            def _(sp):
                if summing:
                    def body(i):
                        for u in range(2):
                            c = i * 2 + u
                            if not isinstance(i, int):
                                sp.wait_ge(added, c * 2 - 2)
                            sp.sem_inc(a.passed("sp"), 1)
                            for n in range(2):
                                sp.dma_start(zin[u][n][:, :, :], z_rows[n][:, bass.ds(c * TC, TC), :])\
                                    .then_inc(zin_in[u], 16)
                    repeat(sp, CH // 2, body)
                else:
                    with sp.Fori(0, CH) as c:
                        sp.wait_ge(scaled, c + 1)
                        sp.sem_inc(a.passed("sp"), 1)
                        sp.dma_start(z_rows[layer][:, bass.ds(c * TC, TC), :], G[:, bass.ds(c * TC, TC), 0:C])\
                            .then_inc(stored, 16)
        a.close()
    m.close()


def build(nc, d, io):
    k = Pool2(nc, "k")
    N_PAD, E_PAD, T = d["N_PAD"], d["E_PAD"], d["T"]
    k.d_xt = nc.dram_tensor("node_table", ((d["SPARE"] + E_PAD) * XW, 1), F32).ap()
    k.d_acc = nc.dram_tensor("layer_sums", (d["SPARE"] + E_PAD, C), F32).ap()
    k.d_z = [nc.dram_tensor(f"layer_{n}", (E_PAD + P, C), F32).ap() for n in range(2)]
    k.d_last = nc.dram_tensor("last_place", (d["HP"], KEYS_PER_PART), F32).ap()
    k.d_pay_given = nc.dram_tensor("payload_given", (E_PAD, PAY), F32).ap()
    k.d_pay_sorted = nc.dram_tensor("payload_sorted", (E_PAD, PAY), F32).ap()
    k.d_pay_rows = k.d_pay_sorted.rearrange("(p t) c -> p t c", t=T)
    k.d_rec_sorted = nc.dram_tensor("edges_sorted", (E_PAD, 2), I32).ap()
    setup(nc, k, d, io)
    kept = Pool2(nc, "kept")
    k.values = kept.sb("values", [P, T, V_W])
    edges_and_nodes(nc, k, d, io)
    unsorted = nc.values_load(k.unsorted[0:1, 0:1], min_val=0, max_val=1)
    with nc.If(unsorted > 0):
        sort_payload(nc, k, d, io)
    attention(nc, k, d, io)
    kept.close()
    layers(nc, k, d, io)
    final_nodes(nc, k, d, io)
    k.close()


_WEIGHTS = ("Wq", "bq", "W_src", "b_src", "W_dst", "W_fc1", "b_fc1", "W_fc2", "b_fc2", "W_fc3", "b_fc3",
            "W_kv", "b_kv", "W_proj", "b_proj")


def dims(n_nodes, n_edges):
    unit = KEYS_PER_PART * P // 128
    hp = -(-(n_nodes + 1) // unit)
    while (hp * KEYS_PER_PART) % (P * 28) or (hp * KEYS_PER_PART // P) % 112:
        hp += 1
    t = -(-n_edges // P)
    t = -(-t // 56) * 56
    n_pad = hp * KEYS_PER_PART
    return {"N": n_nodes, "E": n_edges, "HP": hp, "N_PAD": n_pad, "SPARE": n_pad + P, "T": t, "E_PAD": t * P,
            "S": t // GROUP,
            "R": n_pad // P, "J": 28}


def layout(inputs, d):
    import numpy as np
    x = np.asarray(inputs["x"])
    xp = np.zeros((d["N_PAD"], C), x.dtype)
    xp[:d["N"]] = x
    arrays = {"x": xp}
    pads = {}
    for key in ("src", "dst"):
        e = np.full((d["E_PAD"],), d["N"], np.int32)
        e[:d["E"]] = np.asarray(inputs[key])
        pads[key] = e.reshape(P, d["T"])
        arrays[f"{key}_pt"] = pads[key]
        arrays[f"{key}_tp"] = np.ascontiguousarray(pads[key].T).reshape(d["S"], GE)
    arrays["rec"] = np.ascontiguousarray(np.stack([pads["src"], pads["dst"]], axis=-1))
    ea = np.zeros((d["E_PAD"], C), x.dtype)
    ea[:d["E"]] = np.asarray(inputs["edge_attr_64"])
    arrays["ea"] = np.ascontiguousarray(
        ea.reshape(P, d["S"] // 2, 2, GROUP, C).transpose(1, 2, 4, 3, 0)).reshape(d["S"] // 2, P, GE)
    ew = np.zeros((d["E_PAD"],), x.dtype)
    ew[:d["E"]] = np.asarray(inputs["edge_weight1"])[:, 0]
    arrays["ew"] = ew.reshape(P, d["T"])
    for w in _WEIGHTS:
        arrays[w] = np.ascontiguousarray(np.asarray(inputs[f"L0_gnn_{w}"]))
    return arrays


def kernel(**inputs):
    import concourse.bacc as _bacc
    from concourse import mybir as _mybir
    from concourse.bass_utils import run_bass_kernel_spmd as _run

    d = dims(inputs["x"].shape[0], inputs["src"].shape[0])
    arrays = layout(inputs, d)
    nc = _bacc.Bacc("TRN2", target_bir_lowering=False, num_devices=1)
    io = {n: nc.dram_tensor(f"in_{n}", a.shape, _mybir.dt.from_np(a.dtype), kind="ExternalInput").ap()
          for n, a in arrays.items()}
    io["out"] = nc.dram_tensor("out_rows", (d["N_PAD"], C), F32, kind="ExternalOutput").ap()
    build(nc, d, io)
    r = _run(nc, [{f"in_{n}": a for n, a in arrays.items()}], core_ids=[0])
    return r.results[0]["out_rows"][:d["N"]]
```
